# Optimizing a Trainium2 kernel written in Bass

```python
import numpy as np
import jax
import jax.numpy as jnp

def _softmax(x, axis=-1):
    return jax.nn.softmax(x, axis=axis)

def _gelu(x):
    return jax.nn.gelu(x, approximate=True)

def _silu(x):
    return jax.nn.silu(x)

def _sigmoid(x):
    return jax.nn.sigmoid(x)

def _layernorm(x, axis=-1, eps=1e-05):
    m = jnp.mean(x, axis=axis, keepdims=True)
    v = jnp.var(x, axis=axis, keepdims=True)
    return (x - m) / jnp.sqrt(v + eps)

def _scatter_add(tgt, idx, src, axis=0):
    return tgt.at[idx].add(src)

def _segment_sum(src, seg, n):
    return jax.ops.segment_sum(src, seg, n)
kernel_name = 'mk_macaron_d1_jaxref_r4_f4f024'

def setup_inputs(seed: int=0):
    np.random.seed(seed)
    _w = jnp.asarray

    def _L0_attn_setup():
        import jax, jax.numpy as jnp
        import numpy as np
        B, T, D, H = (4, 512, 256, 8)
        HD = D // H
        RES_SCALE = 1.0 / np.sqrt(2.0 * 2)

        def rmsnorm(x, w, eps=1e-06):
            return w * (x * jax.lax.rsqrt(jnp.mean(x * x, axis=-1, keepdims=True) + eps))

        def l2norm(x, eps=1e-06):
            return x * jax.lax.rsqrt(jnp.sum(x * x, axis=-1, keepdims=True) + eps)

        def _reference_tuple_inner(x, ln1_w, qw, kw, vw, bw, aw, A_log, dt_bias, gw, onorm_w, ow, ln2_w, fcw, pw):
            b, t, d = x.shape
            h = rmsnorm(x, ln1_w)
            q = l2norm(jax.nn.silu(h @ qw).reshape(b, t, H, HD))
            k = l2norm(jax.nn.silu(h @ kw).reshape(b, t, H, HD))
            v = jax.nn.silu(h @ vw).reshape(b, t, H, HD)
            beta = jax.nn.sigmoid(h @ bw)
            g = -jnp.exp(A_log) * jax.nn.softplus(h @ aw + dt_bias)
            qs, ks_, vs = (a.transpose(1, 0, 2, 3) for a in (q, k, v))
            bs, gs = (beta.transpose(1, 0, 2), g.transpose(1, 0, 2))

            def step(S, inp):
                q_t, k_t, v_t, b_t, g_t = inp
                Sg = jnp.exp(g_t)[..., None, None] * S
                kS = jnp.einsum('bhk,bhkv->bhv', k_t, Sg)
                S = Sg + jnp.einsum('bhk,bhv->bhkv', b_t[..., None] * k_t, v_t - kS)
                o_t = jnp.einsum('bhk,bhkv->bhv', q_t, S)
                return (S, o_t)
            S0 = jnp.zeros((b, H, HD, HD), x.dtype)
            S_f, os = jax.lax.scan(step, S0, (qs, ks_, vs, bs, gs))
            o = os.transpose(1, 0, 2, 3)
            gate = jax.nn.silu((h @ gw).reshape(b, t, H, HD))
            o = rmsnorm(o, onorm_w) * gate
            o = o.reshape(b, t, d) @ ow
            x1 = x + o * RES_SCALE
            h2 = rmsnorm(x1, ln2_w)
            y = x1 + jax.nn.silu(h2 @ fcw) @ pw * RES_SCALE
            return (y, S_f)
        key = jax.random.key(seed)
        ks = jax.random.split(key, 16)
        s = 0.02
        return {'x': jax.random.normal(ks[0], (B, T, D), dtype=jnp.float32), 'ln1_w': jnp.ones((D,), jnp.float32), 'qw': jax.random.normal(ks[1], (D, D), jnp.float32) * s, 'kw': jax.random.normal(ks[2], (D, D), jnp.float32) * s, 'vw': jax.random.normal(ks[3], (D, D), jnp.float32) * s, 'bw': jax.random.normal(ks[4], (D, H), jnp.float32) * s, 'aw': jax.random.normal(ks[5], (D, H), jnp.float32) * s, 'A_log': jnp.log(jax.random.uniform(ks[6], (H,), jnp.float32, 1.0, 16.0)), 'dt_bias': jnp.zeros((H,), jnp.float32), 'gw': jax.random.normal(ks[7], (D, D), jnp.float32) * s, 'onorm_w': jnp.ones((HD,), jnp.float32), 'ow': jax.random.normal(ks[8], (D, D), jnp.float32) * s, 'ln2_w': jnp.ones((D,), jnp.float32), 'fcw': jax.random.normal(ks[9], (D, 4 * D), jnp.float32) * s, 'pw': jax.random.normal(ks[10], (4 * D, D), jnp.float32) * s}
    _L0_attn_in = _L0_attn_setup()

    def _L0_ffn_setup():
        import jax, jax.numpy as jnp
        import numpy as np
        E = 8
        K = 2
        CF = 1.25
        key = jax.random.key(seed)
        kx, kr, kg, ku, kd = jax.random.split(key, 5)
        D, F = (256, 1024)
        x = jax.random.normal(kx, (4, 512, D), dtype=jnp.float32)
        router_w = 0.02 * jax.random.normal(kr, (E, D), dtype=jnp.float32)
        wg = jax.random.normal(kg, (E, D, F), dtype=jnp.float32) / np.sqrt(D)
        wu = jax.random.normal(ku, (E, D, F), dtype=jnp.float32) / np.sqrt(D)
        wd = jax.random.normal(kd, (E, F, D), dtype=jnp.float32) / np.sqrt(F)
        return {'x': x, 'router_w': router_w, 'wg': wg, 'wu': wu, 'wd': wd}
    _L0_ffn_in = _L0_ffn_setup()
    _d = {'L0_attn_x': _L0_attn_in['x'], 'L0_attn_ln1_w': _L0_attn_in['ln1_w'], 'L0_attn_qw': _L0_attn_in['qw'], 'L0_attn_kw': _L0_attn_in['kw'], 'L0_attn_vw': _L0_attn_in['vw'], 'L0_attn_bw': _L0_attn_in['bw'], 'L0_attn_aw': _L0_attn_in['aw'], 'L0_attn_A_log': _L0_attn_in['A_log'], 'L0_attn_dt_bias': _L0_attn_in['dt_bias'], 'L0_attn_gw': _L0_attn_in['gw'], 'L0_attn_onorm_w': _L0_attn_in['onorm_w'], 'L0_attn_ow': _L0_attn_in['ow'], 'L0_attn_ln2_w': _L0_attn_in['ln2_w'], 'L0_attn_fcw': _L0_attn_in['fcw'], 'L0_attn_pw': _L0_attn_in['pw'], 'L0_ffn_router_w': _L0_ffn_in['router_w'], 'L0_ffn_wg': _L0_ffn_in['wg'], 'L0_ffn_wu': _L0_ffn_in['wu'], 'L0_ffn_wd': _L0_ffn_in['wd']}
    _x0 = _d['L0_attn_x']
    _d['L0_attn_x'] = jax.random.normal(jax.random.fold_in(jax.random.key(seed), 1), (4, 2048, 256), dtype=_x0.dtype)
    del _x0
    return _d

def reference(L0_attn_x, L0_attn_ln1_w, L0_attn_qw, L0_attn_kw, L0_attn_vw, L0_attn_bw, L0_attn_aw, L0_attn_A_log, L0_attn_dt_bias, L0_attn_gw, L0_attn_onorm_w, L0_attn_ow, L0_attn_ln2_w, L0_attn_fcw, L0_attn_pw, L0_ffn_router_w, L0_ffn_wg, L0_ffn_wu, L0_ffn_wd):

    def _L0_attn_ref(x, ln1_w, qw, kw, vw, bw, aw, A_log, dt_bias, gw, onorm_w, ow, ln2_w, fcw, pw):
        import jax, jax.numpy as jnp
        import numpy as np
        B, T, D, H = (4, 512, 256, 8)
        HD = D // H
        RES_SCALE = 1.0 / np.sqrt(2.0 * 2)

        def rmsnorm(x, w, eps=1e-06):
            return w * (x * jax.lax.rsqrt(jnp.mean(x * x, axis=-1, keepdims=True) + eps))

        def l2norm(x, eps=1e-06):
            return x * jax.lax.rsqrt(jnp.sum(x * x, axis=-1, keepdims=True) + eps)

        def _reference_tuple_inner(x, ln1_w, qw, kw, vw, bw, aw, A_log, dt_bias, gw, onorm_w, ow, ln2_w, fcw, pw):
            b, t, d = x.shape
            h = rmsnorm(x, ln1_w)
            q = l2norm(jax.nn.silu(h @ qw).reshape(b, t, H, HD))
            k = l2norm(jax.nn.silu(h @ kw).reshape(b, t, H, HD))
            v = jax.nn.silu(h @ vw).reshape(b, t, H, HD)
            beta = jax.nn.sigmoid(h @ bw)
            g = -jnp.exp(A_log) * jax.nn.softplus(h @ aw + dt_bias)
            qs, ks_, vs = (a.transpose(1, 0, 2, 3) for a in (q, k, v))
            bs, gs = (beta.transpose(1, 0, 2), g.transpose(1, 0, 2))

            def step(S, inp):
                q_t, k_t, v_t, b_t, g_t = inp
                Sg = jnp.exp(g_t)[..., None, None] * S
                kS = jnp.einsum('bhk,bhkv->bhv', k_t, Sg)
                S = Sg + jnp.einsum('bhk,bhv->bhkv', b_t[..., None] * k_t, v_t - kS)
                o_t = jnp.einsum('bhk,bhkv->bhv', q_t, S)
                return (S, o_t)
            S0 = jnp.zeros((b, H, HD, HD), x.dtype)
            S_f, os = jax.lax.scan(step, S0, (qs, ks_, vs, bs, gs))
            o = os.transpose(1, 0, 2, 3)
            gate = jax.nn.silu((h @ gw).reshape(b, t, H, HD))
            o = rmsnorm(o, onorm_w) * gate
            o = o.reshape(b, t, d) @ ow
            x1 = x + o * RES_SCALE
            h2 = rmsnorm(x1, ln2_w)
            y = x1 + jax.nn.silu(h2 @ fcw) @ pw * RES_SCALE
            return (y, S_f)
        return _reference_tuple_inner(x, ln1_w, qw, kw, vw, bw, aw, A_log, dt_bias, gw, onorm_w, ow, ln2_w, fcw, pw)[0]

    def _L0_ffn_ref(x, router_w, wg, wu, wd):
        import jax, jax.numpy as jnp
        import numpy as np
        E = 8
        K = 2
        CF = 1.25
        B, L, D = x.shape
        xf = x.reshape(-1, D)
        N = xf.shape[0]
        capacity = max(1, int(CF * N / E))
        logits = xf @ router_w.T
        probs = jax.nn.softmax(logits, axis=-1)
        topw, topi = jax.lax.top_k(probs, K)
        topw = topw / (topw.sum(-1, keepdims=True) + 1e-06)
        fe = topi.reshape(-1)
        fw = topw.reshape(-1)
        ft = jnp.repeat(jnp.arange(N), K)
        order = jnp.lexsort((-fw, fe))
        se, sw, st = (fe[order], fw[order], ft[order])
        counts = jax.ops.segment_sum(jnp.ones_like(se), se, num_segments=E)
        starts = jnp.cumsum(counts) - counts
        rank = jnp.arange(N * K) - starts[se]
        keep = rank < capacity
        pos = jnp.where(keep, rank, capacity)
        disp = jnp.zeros((E, capacity + 1, D), x.dtype).at[se, pos].set(xf[st])
        disp = disp[:, :capacity]
        g = jnp.einsum('ecd,edf->ecf', disp, wg)
        u = jnp.einsum('ecd,edf->ecf', disp, wu)
        eo = jnp.einsum('ecf,efd->ecd', jax.nn.silu(g) * u, wd)
        gathered = eo[se, jnp.minimum(pos, capacity - 1)]
        contrib = gathered * (sw * keep.astype(x.dtype))[:, None]
        out = jnp.zeros_like(xf).at[st].add(contrib)
        return out.reshape(B, L, D)
    x = L0_attn_x
    x = x + 0.5 * _L0_ffn_ref(_layernorm(x, axis=-1), L0_ffn_router_w, L0_ffn_wg, L0_ffn_wu, L0_ffn_wd)
    x = x + _L0_attn_ref(_layernorm(x, axis=-1), L0_attn_ln1_w, L0_attn_qw, L0_attn_kw, L0_attn_vw, L0_attn_bw, L0_attn_aw, L0_attn_A_log, L0_attn_dt_bias, L0_attn_gw, L0_attn_onorm_w, L0_attn_ow, L0_attn_ln2_w, L0_attn_fcw, L0_attn_pw)
    x = x + 0.5 * _L0_ffn_ref(_layernorm(x, axis=-1), L0_ffn_router_w, L0_ffn_wg, L0_ffn_wu, L0_ffn_wd)
    return x

_drawn_inputs = setup_inputs


def setup_inputs(seed=0):
    import zlib

    import numpy as np

    out = dict(_drawn_inputs(seed))
    spreads = {'L0_attn_ln1_w': (1.0, 0.6),
     'L0_attn_dt_bias': (0.0, 0.8),
     'L0_attn_onorm_w': (1.0, 0.6),
     'L0_attn_ln2_w': (1.0, 0.6)}
    factors = {'L0_attn_qw': 3.483,
     'L0_attn_kw': 3.477,
     'L0_attn_vw': 3.417,
     'L0_attn_bw': 8.0,
     'L0_attn_aw': 8.0,
     'L0_attn_A_log': 8.0,
     'L0_attn_gw': 3.493,
     'L0_attn_ow': 3.398}
    for name, (base, spread) in spreads.items():
        noise = np.random.default_rng([zlib.crc32(name.encode()), seed]).standard_normal(out[name].shape)
        drawn = base * np.exp(spread * noise) if base else spread * noise
        out[name] = jnp.asarray(drawn.astype(out[name].dtype))
    for name, factor in factors.items():
        out[name] = (out[name] * factor).astype(out[name].dtype)
    return out
```

```python
from contextlib import ExitStack

import concourse.bass as bass
import numpy as np
from concourse import mybir
from concourse.alu_op_type import AluOpType as ALU

ACT = mybir.ActivationFunctionType
AX = mybir.AxisListType
F32 = mybir.dt.float32
I32 = mybir.dt.int32

P = 128
B, T, D = 4, 2048, 256
N = B * T
TILES = N // P
KD = D // P
E, TOPK, CAP = 8, 2, max(1, int(1.25 * N / 8))
F = 1024
FB = F // P
H, HD = 8, 32
C = 32
NC = P // C
HG = 4
LEVELS = 5
SLOTS = E * CAP
SKIP = SLOTS
G_LEAST = -200.0
RES = 0.5


def constants():
    p = np.arange(P)
    same = (p[:, None] // C) == (p[None, :] // C)
    cols = {
        "ident": np.eye(P),
        "ones": np.ones((P, P)),
        "before": p[:, None] < p[None, :],
        "upto": same & (p[:, None] <= p[None, :]),
        "after": same & (p[:, None] > p[None, :]),
        "within": (p[:, None] % C) <= np.arange(C)[None, :],
        "causal": (same & (p[:, None] <= p[None, :])),
        "diag": same,
        "chunk": (p[:, None] // C) == np.arange(NC)[None, :],
        "minus_half": np.full((P, 16), -0.5),
        "expert_less_8": np.broadcast_to(np.arange(E)[None, :, None] - 8.0, (P, E, TILES)).reshape(P, -1),
        "first_slot": np.broadcast_to((np.arange(E) * CAP)[None, :, None] - float(SKIP), (P, E, TILES)).reshape(P, -1),
        "not_first_tile": np.broadcast_to((np.arange(TILES) != 0)[None, None, :], (P, E, TILES)).reshape(P, -1),
    }
    at, where, parts = 0, {}, []
    for name, a in cols.items():
        where[name] = (at, a.shape[1])
        parts.append(a.astype(np.float32))
        at += a.shape[1]
    levels = [((p[:, None] >> (s + 1)) == (p[None, :] >> (s + 1))) & ((p[:, None] >> s) % 2 == 0) & ((p[None, :] >> s) % 2 == 1)
              for s in range(LEVELS)]
    return np.concatenate(parts, 1), where, np.concatenate(levels, 1).astype(np.int32)


class Step:

    def __init__(self, meter, k, turn=0):
        self.meter, self.k, self.turn = meter, k, turn


class Meter:

    def __init__(self, sem, name, unit, each_turn):
        self.sem, self.name, self.unit, self.each_turn, self.k = sem, name, unit, each_turn, 0
        self.ahead = 0 if name.startswith("swdma") else 1


class Phase:

    def __init__(self, prog, name, turns=0):
        self.nc, self.book, self.name, self.turns = prog.nc, prog.book, name, turns
        self.semaphore = lambda n: prog.ctx.enter_context(prog.nc.semaphore(f"{name}_{n}"))
        self.loop = ExitStack()
        self.engines = {"pe": self.nc.tensor, "act": self.nc.scalar, "dve": self.nc.vector, "pool": self.nc.gpsimd, "sp": self.nc.sync}
        self.meters, self.waited, self.owners = {}, {}, {}

    def __enter__(self):
        for name, (unit, each_turn) in sorted(self.book.get((self.name, "meters"), {}).items()):
            m = self.meters[name] = Meter(self.semaphore(name), name, unit, each_turn)
            if self.turns and m.ahead:
                self.nc.sync.sem_inc(m.sem, unit * each_turn)
        self.passed = self.semaphore("passed")
        self.i = self.loop.enter_context(self.nc.Fori(0, self.turns)) if self.turns else 0
        return self

    def meter(self, name, unit):
        if name not in self.meters:
            self.meters[name] = Meter(self.semaphore(name), name, unit, 1)
        return self.meters[name]

    def wait(self, engine, *steps, plain=False):
        need = {}
        for s in steps:
            m = s.meter
            assert s.turn == 0 or m.ahead
            at = s.k + (m.each_turn if self.turns else 0) * (m.ahead + s.turn)
            if at > max(need.get(m.name, 0), self.waited.get((engine, m.name), 0)):
                need[m.name] = at
        for name, at in need.items():
            m = self.meters[name]
            self.waited[engine, name] = at
            self.engines[engine].wait_ge(m.sem, self.i * (m.unit * m.each_turn) + m.unit * at if self.turns else m.unit * at)
        if need and plain and self.turns:
            self.engines[engine].sem_inc(self.passed, 1)

    def run(self, engine, make, *steps, plain=False):
        self.wait(engine, *steps, plain=plain or engine == "pool")
        m = self.meter(engine, 1)
        m.k += 1
        make().then_inc(m.sem, 1)
        return Step(m, m.k)

    def dma(self, queue, buffer, make, *steps):
        self.wait(queue, *steps, plain=queue in ("pool", "sp"))
        m = self.meter(("swdma_" if queue == "pool" else "dma_") + buffer, 16)
        m.k += 1
        make().then_inc(m.sem, 16)
        return Step(m, m.k)

    def relay(self, engine, *steps):
        self.wait(engine, *steps)
        m = self.meter(engine, 1)
        m.k += 1
        self.engines[engine].sem_inc(m.sem, 1)
        return Step(m, m.k)

    def pe(self, make, *steps):
        return self.run("pe", make, *steps)

    def act(self, make, *steps):
        return self.run("act", make, *steps)

    def dve(self, make, *steps, plain=False):
        return self.run("dve", make, *steps, plain=plain)

    def pool(self, make, *steps):
        return self.run("pool", make, *steps)

    def release(self, buffer, *steps):
        self.owners[buffer] = steps

    def free(self, buffer):
        if buffer in self.owners:
            return self.owners[buffer]
        last = self.book.get((self.name, "owners"), {}).get(buffer, ())
        return tuple(Step(self.meters[name], k, -1) for name, k in last)

    def __exit__(self, *error):
        self.loop.close()
        if error[0] is not None:
            return
        self.book[self.name, "owners"] = {b: [(s.meter.name, s.k) for s in steps] for b, steps in self.owners.items()}
        self.book[self.name, "meters"] = {n: (m.unit, m.k) for n, m in self.meters.items()}
        for m in self.meters.values():
            if m.unit == 16:
                self.nc.sync.wait_ge(m.sem, 16 * m.k * (self.turns + m.ahead if self.turns else 1))
        self.nc.all_engine_barrier()


class Program:
    def __init__(self, nc, book, ctx, dram):
        self.nc, self.book, self.ctx, self.dram = nc, book, ctx, dram
        self.sync, self.tensor, self.vector, self.scalar, self.gpsimd = nc.sync, nc.tensor, nc.vector, nc.scalar, nc.gpsimd
        self.temps = 0
        sb = self.sb
        self.bank = ctx.enter_context(nc.psum_tensor("bank", [P, 8, 512], F32))
        _, self.where, _ = constants()
        width = sum(w for _, w in self.where.values())
        self.const = sb("const", [P, width])
        self.level = sb("level", [P, LEVELS, P], I32)
        self.router = sb("router", [P, KD, E])
        self.w_qk, self.w_vg, self.w_ba = sb("w_qk", [P, KD, 2 * D]), sb("w_vg", [P, KD, 2 * D]), sb("w_ba", [P, KD, 2 * H])
        self.w_o, self.w_fc, self.w_p = sb("w_o", [P, KD, D]), sb("w_fc", [P, KD, F]), sb("w_p", [P, FB, D])
        self.ln1, self.ln2 = sb("ln1", [P, KD]), sb("ln2", [P, KD])
        self.onorm = sb("onorm", [P, HD])
        self.decay, self.dt_bias = sb("decay", [P, H]), sb("dt_bias", [P, H])
        self.logits = sb("logits", [P, E, TILES])
        self.slot = sb("slot", [P, TOPK, TILES], I32)
        self.fetch = sb("fetch", [P, TOPK, TILES], I32)
        self.weight = sb("weight", [P, TOPK, TILES])

    def sb(self, name, shape, dtype=F32):
        return self.ctx.enter_context(self.nc.sbuf_tensor(name, shape, dtype))

    def temp(self, stack, name, shape, dtype=F32):
        self.temps += 1
        return stack.enter_context(self.nc.sbuf_tensor(f"{name}_{self.temps}", shape, dtype))

    def c(self, name):
        at, width = self.where[name]
        return self.const[:, at:at + width]

    def rows(self, name, first, count):
        return self.dram[name][bass.ds(first, count), :].rearrange("(j p) d -> p j d", p=P)

    def start(self):
        nc, dram = self.nc, self.dram
        with Phase(self, "start") as ph, ExitStack() as tmp:
            zero = self.temp(tmp, "zero", [P, 8, D], F32)
            z = ph.dve(lambda: nc.vector.memset(zero[:, :, :], 0.0))
            for name in ("disp1", "disp2"):
                for n in range(SLOTS // (8 * P)):
                    ph.dma("act", "zero", lambda: nc.scalar.dma_start(self.rows(name, n * 8 * P, 8 * P), zero[:, :, :]), z)

            def load(dst, src, **how):
                return ph.dma("sp", "const", lambda: nc.sync.dma_start(dst, src, **how))

            blocks = lambda name: dram[name].rearrange("(k p) f -> p k f", p=P)
            load(self.const[:, :], dram["const"])
            load(self.level[:, :, :], dram["level"].rearrange("p (s i) -> p s i", s=LEVELS))
            load(self.router[:, :, :], blocks("router_t"))
            for w, a, b in ((self.w_qk, "qw", "kw"), (self.w_vg, "vw", "gw"), (self.w_ba, "bw", "aw")):
                half = w.shape[2] // 2
                load(w[:, :, 0:half], blocks(a))
                load(w[:, :, half:], blocks(b))
            load(self.w_o[:, :, :], blocks("ow"))
            load(self.w_fc[:, :, :], blocks("fcw"))
            load(self.w_p[:, :, :], blocks("pw"))
            load(self.ln1[:, :], dram["ln1_w"].rearrange("(k p) -> p k", p=P), allow_slow_non_contiguous=True)
            load(self.ln2[:, :], dram["ln2_w"].rearrange("(k p) -> p k", p=P), allow_slow_non_contiguous=True)
            load(self.onorm[:, :], dram["onorm_w"].partition_broadcast(P))
            load(self.decay[:, :], dram["A_log"].partition_broadcast(P))
            last = load(self.dt_bias[:, :], dram["dt_bias"].partition_broadcast(P))
            e = ph.act(lambda: nc.scalar.activation(self.decay[:, :], self.decay[:, :], ACT.Exp), last)
            ph.dve(lambda: nc.vector.tensor_scalar(self.decay[:, :], self.decay[:, :], -1.0, None, ALU.mult), e)

    def route_first(self):
        nc = self.nc
        J, U = 4, 2
        with ExitStack() as tmp:
            sb = lambda n, s: self.temp(tmp, n, s, F32)
            x4 = [sb(f"x4_{u}", [P, J, D]) for u in range(U)]
            xn = [sb(f"xn_{u}", [P, J, D]) for u in range(U)]
            xt = [sb(f"xt_{u}", [P, J, KD, P]) for u in range(U)]
            st = [sb(f"st_{u}", [P, J, 6]) for u in range(U)]
            mv = [sb(f"mv_{u}", [P, J, 2]) for u in range(U)]
            rs = [sb(f"rs_{u}", [P, J]) for u in range(U)]
            with Phase(self, "route1", TILES // (J * U)) as ph:
                for u in range(U):
                    row = ph.i * (J * U * P) + u * J * P
                    x = ph.dma("sp", f"x{u}", lambda: nc.sync.dma_start(x4[u][:, :, :], self.rows("x", row, J * P)), *ph.free(f"x4_{u}"))
                    for j in range(J):
                        s = ph.dve(lambda: nc.vector.bn_stats(st[u][:, j, :], x4[u][:, j, :]), x, *ph.free(f"st{u}"))
                    for j in range(J):
                        s = ph.dve(lambda: nc.vector.bn_aggr(mv[u][:, j, :], st[u][:, j, :]), s, *ph.free(f"mv{u}"), plain=True)
                    r = self.rsqrt(ph, rs[u][:, :], mv[u][:, :, 1], 1.0, 1e-5, s, *ph.free(f"mv{u}"))
                    ph.release(f"st{u}", s)
                    for j in range(J):
                        n = ph.dve(lambda: nc.vector.tensor_scalar(xn[u][:, j, :], x4[u][:, j, :], mv[u][:, j, 0:1], rs[u][:, j:j + 1],
                                                                   ALU.subtract, ALU.mult), r, *ph.free(f"xn{u}"))
                    ph.release(f"x4_{u}", n)
                    ph.release(f"mv{u}", n)
                    kept = ph.dma("sp", f"xn{u}", lambda: nc.sync.dma_start(self.rows("xn", row, J * P), xn[u][:, :, :]), n)
                    for j in range(J):
                        for k in range(KD):
                            o = self.bank[:, 2 * u + j // 2, (j % 2 * KD + k) * P:(j % 2 * KD + k + 1) * P]
                            t = ph.pe(lambda: nc.tensor.transpose(o, xn[u][:, j, k * P:(k + 1) * P], self.c("ident")), n, *ph.free(f"xt bank{u}"))
                    ph.release(f"xn{u}", kept, t)
                    for j in range(0, J, 2):
                        e = ph.act(lambda: nc.scalar.activation(xt[u][:, j:j + 2, :, :].rearrange("p j k t -> p (j k t)"), self.bank[:, 2 * u + j // 2, :], ACT.Copy),
                                   t, *ph.free(f"xt{u}"))
                    ph.release(f"xt bank{u}", e)
                    for j in range(J):
                        for k in range(KD):
                            m = ph.pe(lambda: nc.tensor.matmul(self.bank[:, 4 + u, j * E:(j + 1) * E], xt[u][:, j, k, :], self.router[:, k, :],
                                                               start=k == 0, stop=k == KD - 1), e, *ph.free(f"logit bank{u}"))
                    ph.release(f"xt{u}", m)
                    l = ph.dve(lambda: nc.vector.tensor_copy(self.logits[:, :, bass.ds(ph.i * (J * U) + u * J, J)],
                                                             self.bank[:, 4 + u, 0:J * E].rearrange("p (j e) -> p e j", e=E)), m, )
                    ph.release(f"logit bank{u}", l)

    def rsqrt(self, ph, out, in_, scale, eps, *steps):
        nc = self.nc
        a = ph.pool(lambda: nc.gpsimd.tensor_scalar(out, in_, scale, eps, ALU.mult, ALU.add), *steps)
        half = self.c("minus_half")[:, 0:out.free_size()]
        return ph.pool(lambda: nc.gpsimd.tensor_tensor(out, out, half, ALU.pow), a)

    def choose(self, name):
        nc, v, c = self.nc, self.nc.vector, self.c
        with ExitStack() as tmp:
            sb = lambda n, s, d=F32: self.temp(tmp, n, s, d)
            full = lambda n: sb(n, [P, E, TILES])
            p, hot1, hot2, w, a, b, s = (full(n) for n in ("p", "hot1", "hot2", "w", "a", "b", "s"))
            m, r, m1, m2 = (sb(n, [P, TILES]) for n in ("m", "r", "m1", "m2"))
            per = lambda n, d=F32: sb(n, [P, E], d)
            cand, least, more, count, quota = per("cand", I32), per("least", I32), per("more", I32), per("count"), per("quota")
            flat = lambda t: t[:, :, :].rearrange("p e t -> p (e t)")
            te = lambda t: t[:, :, :].rearrange("p e t -> p t e")
            over_e = lambda t: t[:, :].unsqueeze(1).to_broadcast([P, E, TILES])
            over_t = lambda t: t.unsqueeze(2).to_broadcast([P, E, TILES])
            bank = [self.bank[:, n, :] for n in range(4)]
            psum = lambda n: bank[n].rearrange("p (e t) -> p e t", e=E)
            less8 = c("expert_less_8").rearrange("p (e t) -> p e t", e=E)
            tt, ts, stt = v.tensor_tensor, v.tensor_scalar, v.scalar_tensor_tensor
            with Phase(self, name) as ph:
                last = [()]

                def dve(make, *steps):
                    last[0] = (ph.dve(make, *last[0], *steps),)
                    return last[0][0]

                A = lambda t: t[:, :, :]
                dve(lambda: v.tensor_reduce(m[:, :], te(self.logits), AX.X, ALU.max))
                x = dve(lambda: tt(A(p), A(self.logits), over_e(m), ALU.subtract))
                x = ph.act(lambda: nc.scalar.activation(A(p), A(p), ACT.Exp), x)
                dve(lambda: v.tensor_reduce(m[:, :], te(p), AX.X, ALU.add), x)
                dve(lambda: v.reciprocal(r[:, :], m[:, :]))
                dve(lambda: tt(A(p), A(p), over_e(r), ALU.mult))
                for best, hot in ((m1, hot1), (m2, hot2)):
                    dve(lambda: v.tensor_reduce(best[:, :], te(p), AX.X, ALU.max))
                    dve(lambda: tt(A(a), A(p), over_e(best), ALU.is_equal))
                    dve(lambda: tt(A(a), A(a), less8, ALU.mult))
                    dve(lambda: v.tensor_reduce(m[:, :], te(a), AX.X, ALU.min))
                    dve(lambda: tt(A(hot), less8, over_e(m), ALU.is_equal))
                    if best is m1:
                        dve(lambda: stt(flat(p), flat(hot), -2.0, flat(p), ALU.mult, ALU.add))
                dve(lambda: stt(r[:, :], m1[:, :], 1e-6, m2[:, :], ALU.add, ALU.add))
                dve(lambda: v.reciprocal(r[:, :], r[:, :]))
                dve(lambda: tt(m1[:, :], m1[:, :], r[:, :], ALU.mult))
                dve(lambda: tt(m2[:, :], m2[:, :], r[:, :], ALU.mult))
                dve(lambda: tt(A(a), A(hot1), over_e(m1), ALU.mult))
                dve(lambda: tt(A(w), A(hot2), over_e(m2), ALU.mult))
                dve(lambda: tt(A(w), A(w), A(a), ALU.add))
                dve(lambda: tt(A(s), A(hot1), A(hot2), ALU.add))

                def total(src, out_bank, width, lhs="ones"):
                    x = last[0][0]
                    return ph.pe(lambda: nc.tensor.matmul(bank[out_bank][:, 0:width], c(lhs), src, start=True, stop=True), x)

                dve(lambda: v.memset(least[:, :], 0))
                for bit in range(29, -1, -1):
                    dve(lambda: v.tensor_scalar(cand[:, :], least[:, :], 1 << bit, None, ALU.bitwise_or))
                    dve(lambda: tt(A(a), A(w), over_t(cand[:, :].bitcast(F32)), ALU.is_ge))
                    dve(lambda: v.tensor_reduce(count[:, :], A(a), AX.X, ALU.add))
                    x = total(count[:, :], 0, E)
                    dve(lambda: ts(more[:, :], bank[0][:, 0:E], float(CAP), None, ALU.is_ge), x)
                    dve(lambda: v.copy_predicated(least[:, :], more[:, :], cand[:, :]))
                floor = over_t(least[:, :].bitcast(F32))
                dve(lambda: tt(A(a), A(w), floor, ALU.is_gt))
                dve(lambda: v.tensor_reduce(count[:, :], A(a), AX.X, ALU.add))
                x = total(count[:, :], 0, E)
                dve(lambda: ts(quota[:, :], bank[0][:, 0:E], -1.0, float(CAP), ALU.mult, ALU.add), x)
                dve(lambda: tt(A(b), A(w), floor, ALU.is_equal))
                dve(lambda: tt(A(b), A(b), A(s), ALU.mult))

                def before(mask, out, tmp_):
                    total(flat(mask), 1, E * TILES, "before")
                    x = total(flat(mask), 2, E * TILES)
                    dve(lambda: v.tensor_copy(flat(tmp_), bank[2]), x)
                    dve(lambda: v.tensor_tensor_scan(flat(out), c("not_first_tile"), flat(tmp_), 0.0, ALU.mult, ALU.add))
                    dve(lambda: tt(A(out), A(out), A(tmp_), ALU.subtract))
                    dve(lambda: tt(A(out), A(out), psum(1), ALU.add), x)

                before(b, p, w)
                dve(lambda: tt(A(p), A(p), over_t(quota[:, :]), ALU.is_lt))
                dve(lambda: tt(A(b), A(b), A(p), ALU.mult))
                dve(lambda: tt(A(a), A(a), A(b), ALU.add))
                before(a, p, w)
                dve(lambda: tt(flat(p), flat(p), c("first_slot"), ALU.add))
                dve(lambda: tt(A(p), A(p), A(a), ALU.mult))
                for k, (hot, weight) in enumerate(((hot1, m1), (hot2, m2))):
                    dve(lambda: tt(A(b), A(hot), A(p), ALU.mult))
                    dve(lambda: v.tensor_reduce(m[:, :], te(b), AX.X, ALU.add))
                    dve(lambda: ts(m[:, :], m[:, :], float(SKIP), None, ALU.add))
                    dve(lambda: v.tensor_copy(self.slot[:, k, :], m[:, :]))
                    dve(lambda: tt(A(b), A(hot), A(a), ALU.mult))
                    dve(lambda: v.tensor_reduce(r[:, :], te(b), AX.X, ALU.add))
                    dve(lambda: tt(self.weight[:, k, :], weight[:, :], r[:, :], ALU.mult))
                    dve(lambda: tt(m[:, :], m[:, :], r[:, :], ALU.mult))
                    dve(lambda: v.tensor_copy(self.fetch[:, k, :], m[:, :]))

    def scatter(self, name, disp):
        nc, U, J = self.nc, 2, 4
        with ExitStack() as tmp:
            xs = [self.temp(tmp, f"xs{u}", [P, J, D], F32) for u in range(U)]
            at = [self.temp(tmp, f"at{u}", [P, TOPK, J], I32) for u in range(U)]
            with Phase(self, name, TILES // (U * J)) as ph:
                groups = []
                for u in range(U):
                    tile = ph.i * (U * J) + u * J
                    x = ph.dma("sp", f"xs{u}", lambda: nc.sync.dma_start(xs[u][:, :, :], self.rows("xn", tile * P, J * P)), *ph.free(f"sent{u}"))
                    a = ph.pool(lambda: nc.gpsimd.tensor_copy(at[u][:, :, :], self.slot[:, :, bass.ds(tile, J)]), *ph.free(f"sent{u}"))
                    sent = []
                    for j in range(J):
                        for k in range(TOPK):
                            sent.append(ph.dma("pool", f"rows{u}", lambda: nc.gpsimd.indirect_dma_start(
                                out=self.dram[disp][:, :], out_offset=bass.IndirectOffsetOnAxis(ap=at[u][:, k, j:j + 1], axis=0),
                                in_=xs[u][:, j, :], in_offset=None, bounds_check=SLOTS - 1, oob_is_err=False), x, a))
                    groups.append(sent[-1])
                for u in range(U):
                    ph.release(f"sent{u}", ph.relay("sp", groups[u]))

    def experts(self, name, disp, eo):
        nc, U, W = self.nc, 2, 256
        CH = CAP // W
        v = nc.vector
        with ExitStack() as tmp:
            sb = lambda n, s: self.temp(tmp, n, s, F32)
            wg = [sb(f"wg{u}", [P, KD, F]) for u in range(U)]
            wu = [sb(f"wu{u}", [P, KD, F]) for u in range(U)]
            wd = [sb(f"wd{u}", [P, FB, D]) for u in range(U)]
            d = [sb(f"d{u}", [P, 2, D]) for u in range(2)]
            dT = [sb(f"dT{u}", [P, KD, W]) for u in range(2)]
            act = [sb(f"act{u}", [P, FB, W]) for u in range(2)]
            th = [sb(f"th{u}", [P, 512]) for u in range(2)]
            eo_sb = [sb(f"eo{u}", [P, 2, D]) for u in range(2)]
            with Phase(self, name, E // U) as ph:
                def down(n, acts):
                    u, par = n // CH, n % 2
                    bank = self.bank[:, 4 + par, :]
                    for s in range(2):
                        for f in range(FB):
                            m = ph.pe(lambda: nc.tensor.matmul(bank[:, s * D:(s + 1) * D], act[par][:, f, s * P:(s + 1) * P], wd[u][:, f, :],
                                                               start=f == 0, stop=f == FB - 1), acts[f // 2], *ph.free(f"down bank{par}"), weights[u][2])
                    ph.release(f"act{par}", m)
                    if n % CH == CH - 1:
                        ph.release(f"wd{u}", m)
                    e = ph.act(lambda: nc.scalar.activation(eo_sb[par][:, :, :].rearrange("p s d -> p (s d)"), bank, ACT.Copy, scale=0.5),
                               m, *ph.free(f"eo{par}"))
                    ph.release(f"down bank{par}", e)
                    row = (ph.i * U + u) * CAP + n % CH * W
                    o = ph.dma("act", f"eo{par}", lambda: nc.scalar.dma_start(self.rows(eo, row, W), eo_sb[par][:, :, :]), e)
                    ph.release(f"eo{par}", o)

                weights = []
                for u in range(U):
                    e = ph.i * U + u
                    g = ph.dma("sp", f"wg{u}", lambda: nc.sync.dma_start(wg[u][:, :, :], self.rows("wg", e * D, D)), *ph.free(f"wg{u}"))
                    w = ph.dma("sp", f"wu{u}", lambda: nc.sync.dma_start(wu[u][:, :, :], self.rows("wu", e * D, D)), *ph.free(f"wg{u}"))
                    if u == 0:
                        dw = ph.dma("sp", f"wd{u}", lambda: nc.sync.dma_start(wd[u][:, :, :], self.rows("wd", e * F, F)), *ph.free(f"wd{u}"))
                        weights.append((g, w, dw))
                    else:
                        weights.append((g, w, None))

                def load_rows(n):
                    par = n % 2
                    row = (ph.i * U + n // CH) * CAP + n % CH * W
                    return ph.dma("sp", f"d{par}", lambda: nc.sync.dma_start(d[par][:, :, :], self.rows(disp, row, W)), *ph.free(f"d{par}"))

                pending = None
                for n in range(U * CH):
                    u, par = n // CH, n % 2
                    x = load_rows(n)
                    if n == 1:
                        dw = ph.dma("sp", "wd1", lambda: nc.sync.dma_start(wd[1][:, :, :], self.rows("wd", (ph.i * U + 1) * F, F)), *ph.free("wd1"))
                        weights[1] = weights[1][:2] + (dw,)
                    for s in range(2):
                        for k in range(KD):
                            t = ph.pe(lambda: nc.tensor.transpose(self.bank[:, 6 + par, k * W + s * P:k * W + (s + 1) * P], d[par][:, s, k * P:(k + 1) * P],
                                                                  self.c("ident")), x, *ph.free(f"dT bank{par}"))
                    ph.release(f"d{par}", t)
                    tr = ph.dve(lambda: v.tensor_copy(dT[par][:, :, :].rearrange("p k w -> p (k w)"), self.bank[:, 6 + par, :]), t, *ph.free(f"dT{par}"))
                    ph.release(f"dT bank{par}", tr)
                    acts = []
                    for r in range(FB // 2):
                        if r == 1 and pending:
                            down(*pending)
                        q = r % 2
                        gb, ub = self.bank[:, q, :], self.bank[:, 2 + q, :]
                        done = {}
                        for which, bank, wt in (("g", gb, wg), ("u", ub, wu)):
                            for f in range(2):
                                for k in range(KD):
                                    fb = 2 * r + f
                                    m = ph.pe(lambda: nc.tensor.matmul(bank[:, f * W:(f + 1) * W], wt[u][:, k, fb * P:(fb + 1) * P], dT[par][:, k, :],
                                                                       start=k == 0, stop=k == KD - 1),
                                              tr, weights[u][0 if which == "g" else 1], *ph.free(f"{which} bank{q}"))
                            done[which] = m
                        out = act[par][:, 2 * r:2 * r + 2, :].rearrange("p f w -> p (f w)")
                        h = ph.act(lambda: nc.scalar.activation(th[q][:, :], gb, ACT.Tanh, scale=0.5), done["g"], *ph.free(f"th{q}"))
                        a = ph.dve(lambda: v.scalar_tensor_tensor(th[q][:, :], th[q][:, :], 1.0, gb, ALU.add, ALU.mult), h)
                        b = ph.dve(lambda: v.tensor_tensor(out, th[q][:, :], ub, ALU.mult), a, done["u"], *ph.free(f"act{par}"))
                        ph.release(f"g bank{q}", a)
                        ph.release(f"u bank{q}", b)
                        ph.release(f"th{q}", b)
                        acts.append(b)
                    ph.release(f"dT{par}", m)
                    if n % CH == CH - 1:
                        ph.release(f"wg{u}", m)
                    pending = (n, acts)
                down(*pending)

    def combine(self, tmp, ph, tag, x, e, w, steps, out):
        v = self.nc.vector
        a = ph.dve(lambda: v.tensor_scalar(e[0], e[0], w[0], None, ALU.mult), *steps)
        a = ph.dve(lambda: v.scalar_tensor_tensor(e[0], e[1], w[1], e[0], ALU.mult, ALU.add), a)
        return ph.dve(lambda: v.scalar_tensor_tensor(out, e[0], RES, x, ALU.mult, ALU.add), a)

    def finish(self, eo):
        nc, U = self.nc, 4
        with ExitStack() as tmp:
            sb = lambda n, s, d=F32: self.temp(tmp, n, s, d)
            x = [sb(f"fx{u}", [P, D]) for u in range(U)]
            e = [[sb(f"fe{u}{k}", [P, D]) for k in range(TOPK)] for u in range(U)]
            y = [sb(f"fy{u}", [P, D]) for u in range(U)]
            at = sb("fat", [P, TOPK, U], I32)
            wt = sb("fwt", [P, TOPK, U])
            with Phase(self, "finish", TILES // U) as ph:
                tile = ph.i * U
                a = ph.pool(lambda: nc.gpsimd.tensor_copy(at[:, :, :], self.fetch[:, :, bass.ds(tile, U)]), *ph.free("at"))
                w = ph.pool(lambda: nc.gpsimd.tensor_copy(wt[:, :, :], self.weight[:, :, bass.ds(tile, U)]), *ph.free("wt"))
                for u in range(U):
                    rows = self.dram["x2"][bass.ds((tile + u) * P, P), :]
                    xs = ph.dma("sp", f"x{u}", lambda: nc.sync.dma_start(x[u][:, :], rows), *ph.free(f"x{u}"))
                    g = [ph.dma("pool", f"e{u}", lambda: nc.gpsimd.indirect_dma_start(
                        out=e[u][k][:, :], out_offset=None, in_=self.dram[eo][:, :],
                        in_offset=bass.IndirectOffsetOnAxis(ap=at[:, k, u:u + 1], axis=0)), a, *ph.free(f"e{u}")) for k in range(TOPK)]
                    o = self.combine(None, ph, "", x[u][:, :], (e[u][0][:, :], e[u][1][:, :]), (wt[:, 0, u:u + 1], wt[:, 1, u:u + 1]),
                                     (xs, *g, w, *ph.free(f"y{u}")), y[u][:, :])
                    ph.release(f"x{u}", o)
                    ph.release(f"e{u}", o)
                    rows_out = self.dram["out"][bass.ds((tile + u) * P, P), :]
                    s = ph.dma("sp", f"y{u}", lambda: nc.sync.dma_start(rows_out, y[u][:, :]), o)
                    ph.release(f"y{u}", s)
                ph.release("at", o)
                ph.release("wt", o)

    def attention(self, eo):
        nc, v, g_, sc = self.nc, self.nc.vector, self.nc.gpsimd, self.nc.scalar
        c, bank = self.c, self.bank
        with ExitStack() as tmp:
            sb = lambda n, s, d=F32: self.temp(tmp, n, s, d)
            two = lambda n, s, d=F32: [sb(f"{n}{q}", s, d) for q in range(2)]
            one = lambda n, s, d=F32: [sb(n, s, d)] * 2
            x_in, e0, e1, x1, xa = (two(n, [P, D]) for n in ("x_in", "e0", "e1", "x1", "xa"))
            at, wt = two("at", [P, TOPK], I32), two("wt", [P, TOPK])
            st, mv, small = two("st", [P, 6]), two("mv", [P, 2]), two("small", [P, 4])
            h, junk = one("h", [P, D]), one("junk", [P, D])
            hT = one("hT", [P, KD, P])
            th, sq = one("th", [P, 512]), one("sq", [P, 512])
            qk, vg, gg = one("qk", [P, 2 * H, HD]), one("vg", [P, 2 * H, HD]), two("gg", [P, H, HD])
            tiny, ba = one("tiny", [P, 10, H]), one("ba", [P, 2 * H])
            rq, ro = one("rq", [P, 2 * H]), one("ro", [P, H])
            gamma = two("gamma", [P, 3 * H])
            gv, gx, dc = one("gv", [P, H, HD]), one("gx", [P, H, HD]), one("dc", [P, H, HD])
            dm = one("dm", [P, H, P])
            kb, nw, qg, vb, kc = (one(n, [P, H, HD]) for n in ("kb", "nw", "qg", "vb", "kc_"))
            kc = two("kc", [P, H, HD])
            bq, kT, qgT = one("bq", [P, 2, 2, P]), one("kT", [P, 2, P]), two("qgT", [P, 2, P])
            NT, Y, X, R = one("NT", [P, H, P]), one("Y", [P, H, P]), one("X", [P, H, P]), one("R", [P, H, P])
            Bt, WT = two("Bt", [P, H, P]), two("WT", [P, 2, P])
            us, sm, os_, og, ogT = one("us", [P, H * HD]), one("sm", [P, 2, P]), one("os", [P, D]), one("og", [P, D]), one("ogT", [P, KD, P])
            x1a, h2, h2T, aT = one("x1a", [P, D]), one("h2", [P, D]), one("h2T", [P, KD, P]), one("aT", [P, FB, P])
            x2, xn2, xn2T = two("x2", [P, D]), two("xn2", [P, D]), one("xn2T", [P, KD, P])
            S = [sb(f"S{b}", [P, 2, P]) for b in range(B)]
            flat = lambda t: t[:, :, :].rearrange("p a b -> p (a b)")
            over_hd = lambda t: t.unsqueeze(2).to_broadcast([P, t.shape[1], HD])
            per4 = lambda m: m.unsqueeze(1).to_broadcast([P, HG, P])

            with Phase(self, "zero_state") as ph:
                for b in range(B):
                    ph.dve(lambda: v.memset(S[b][:, :, :], 0.0))

            with Phase(self, "attention", T // P) as ph:
                state = {}

                def row(b):
                    return ph.i * P + b * T

                def tile(b):
                    return ph.i + b * (T // P)

                def norm(x, out, q, steps, free):
                    s = ph.dve(lambda: v.bn_stats(st[q][:, :], x), *steps, *ph.free(f"st{q}"))
                    s = ph.dve(lambda: v.bn_aggr(mv[q][:, :], st[q][:, :]), s, *ph.free(f"mv{q}"), plain=True)
                    ph.release(f"st{q}", s)
                    r = self.rsqrt(ph, small[q][:, 0:1], mv[q][:, 1:2], 1.0, 1e-5, s, *ph.free(f"small0{q}"))
                    n = ph.dve(lambda: v.tensor_scalar(out, x, mv[q][:, 0:1], small[q][:, 0:1], ALU.subtract, ALU.mult), r, *free)
                    ph.release(f"mv{q}", n)
                    ph.release(f"small0{q}", n)
                    return n

                def rms(x, out, q, steps, free):
                    a = ph.act(lambda: sc.activation(junk[q][:, :], x, ACT.Square, accum_out=small[q][:, 1:2]), *steps, *ph.free("junk"), *ph.free(f"small1{q}"))
                    ph.release("junk", a)
                    r = self.rsqrt(ph, small[q][:, 1:2], small[q][:, 1:2], 1.0 / D, 1e-6, a)
                    n = ph.dve(lambda: v.tensor_scalar(out, x, small[q][:, 1:2], None, ALU.mult), r, *free)
                    ph.release(f"small1{q}", n)
                    return n

                def transpose(x, out, bank_no, name, steps, scale=None):
                    for k in range(KD):
                        t = ph.pe(lambda: nc.tensor.transpose(bank[:, bank_no, k * P:(k + 1) * P], x[:, k * P:(k + 1) * P], c("ident")), *steps, *ph.free(f"bank{bank_no}"))
                    if scale is None:
                        e = ph.act(lambda: sc.activation(flat(out), bank[:, bank_no, 0:KD * P], ACT.Copy), t, *ph.free(name))
                    else:
                        for k in range(KD):
                            e = ph.act(lambda: sc.activation(out[:, k, :], bank[:, bank_no, k * P:(k + 1) * P], ACT.Copy, scale=scale[:, k:k + 1]), t, *ph.free(name))
                    ph.release(f"bank{bank_no}", e)
                    return t, e

                def block_a(b):
                    q = b % 2
                    ia = ph.pool(lambda: g_.tensor_copy(at[q][:, :], self.fetch[:, :, bass.ds(tile(b), 1)].rearrange("p k t -> p (k t)")), *ph.free(f"at{q}"))
                    iw = ph.pool(lambda: g_.tensor_copy(wt[q][:, :], self.weight[:, :, bass.ds(tile(b), 1)].rearrange("p k t -> p (k t)")), *ph.free(f"wt{q}"))
                    xs = ph.dma("sp", f"x{q}", lambda: nc.sync.dma_start(x_in[q][:, :], self.dram["x"][bass.ds(row(b), P), :]), *ph.free(f"x_in{q}"))
                    for k, e in enumerate((e0[q], e1[q])):
                        got = ph.dma("pool", f"e{q}", lambda: g_.indirect_dma_start(
                            out=e[:, :], out_offset=None, in_=self.dram[eo][:, :],
                            in_offset=bass.IndirectOffsetOnAxis(ap=at[q][:, k:k + 1], axis=0)), ia, *ph.free(f"e{q}"))
                    x = self.combine(None, ph, "", x_in[q][:, :], (e0[q][:, :], e1[q][:, :]), (wt[q][:, 0:1], wt[q][:, 1:2]),
                                     (xs, got, iw, *ph.free(f"x1{q}")), x1[q][:, :])
                    ph.release(f"x_in{q}", x)
                    ph.release(f"e{q}", x)
                    ph.release(f"wt{q}", x)
                    ph.release(f"at{q}", x)
                    n = norm(x1[q][:, :], xa[q][:, :], q, (x,), ph.free(f"xa{q}"))
                    n2 = rms(xa[q][:, :], h[q][:, :], q, (n,), ph.free("h"))
                    t, e = transpose(h[q], hT[q], 7, "hT", (n2,), self.ln1)
                    ph.release("h", t)
                    for w, no, width in ((self.w_qk, 4, 512), (self.w_vg, 5, 512), (self.w_ba, 6, 2 * H)):
                        for k in range(KD):
                            m = ph.pe(lambda: nc.tensor.matmul(bank[:, no, 0:width], hT[q][:, k, :], w[:, k, :], start=k == 0, stop=k == KD - 1),
                                      e, *ph.free(f"bank{no}"))
                        state[no] = m
                    ph.release("hT", m)
                    tn = lambda n: tiny[q][:, n, :]
                    y_, z_, s_, w_, p_, g, beta, half_beta, ng = (tn(n) for n in range(9))
                    m = ph.dve(lambda: v.tensor_copy(ba[q][:, :], bank[:, 6, 0:2 * H]), m, *ph.free("tiny"))
                    tb = ph.act(lambda: sc.activation(beta, ba[q][:, 0:H], ACT.Tanh, scale=0.5), m)
                    d = lambda make, *s: ph.dve(make, *s)
                    x = d(lambda: v.tensor_tensor(y_, ba[q][:, H:], self.dt_bias[:, :], ALU.add), m)
                    x = d(lambda: v.scalar_tensor_tensor(z_, y_, -1.0, y_, ALU.mult, ALU.min), x)
                    z = ph.act(lambda: sc.activation(z_, z_, ACT.Exp), x)
                    x = d(lambda: v.tensor_scalar(s_, z_, 2.0, None, ALU.add), z)
                    x = d(lambda: v.reciprocal(s_, s_), x)
                    x = d(lambda: v.tensor_tensor(s_, s_, z_, ALU.mult), x)
                    x = d(lambda: v.tensor_tensor(w_, s_, s_, ALU.mult), x)
                    x = d(lambda: v.tensor_scalar(p_, w_, 1.0 / 17, None, ALU.mult), x)
                    for n in range(15, 1, -2):
                        x = d(lambda: v.scalar_tensor_tensor(p_, p_, 1.0 / n, w_, ALU.add, ALU.mult), x)
                    x = d(lambda: v.scalar_tensor_tensor(p_, p_, 1.0, s_, ALU.add, ALU.mult), x)
                    x = d(lambda: v.tensor_scalar(y_, y_, 0.0, None, ALU.max), x)
                    x = d(lambda: v.scalar_tensor_tensor(p_, p_, 2.0, y_, ALU.mult, ALU.add), x)
                    x = d(lambda: v.tensor_tensor(g, p_, self.decay[:, :], ALU.mult), x)
                    gs = d(lambda: v.tensor_scalar(g, g, G_LEAST, None, ALU.max), x)
                    x = d(lambda: v.tensor_scalar(beta, beta, 0.5, 0.5, ALU.mult, ALU.add), tb)
                    bs = d(lambda: v.tensor_scalar(half_beta, beta, 0.5, None, ALU.mult), x)
                    pv = ph.pool(lambda: g_.tensor_tensor(gv[q][:, :, :], over_hd(g), c("within").unsqueeze(1).to_broadcast([P, H, HD]), ALU.mult), gs, *ph.free("gv"))
                    px = ph.pool(lambda: g_.tensor_copy(gx[q][:, :, :], over_hd(g)), gs, *ph.free("gx"))
                    sums = bank[:, 6, 16:16 + 3 * H]
                    ph.pe(lambda: nc.tensor.matmul(sums[:, 0:H], c("upto"), g, start=True, stop=True), gs)
                    ph.pe(lambda: nc.tensor.matmul(sums[:, H:2 * H], c("after"), g, start=True, stop=True), gs)
                    for n in range(2):
                        m = ph.pe(lambda: nc.tensor.matmul(sums[:, 2 * H + NC * n:2 * H + NC * (n + 1)], gx[q][:, HG * n:HG * (n + 1), :].rearrange("p a b -> p (a b)"),
                                                           c("chunk"), start=True, stop=True), px)
                    ms = ph.pe(lambda: nc.tensor.matmul(bank[:, 6, 128:128 + H * HD], c("after"), flat(gv[q]), start=True, stop=True), pv)
                    ph.release("gv", ms)
                    ph.release("gx", ms)
                    ga = ph.act(lambda: sc.activation(gamma[q][:, :], sums, ACT.Exp), ms, *ph.free(f"gamma{q}"))
                    gd = ph.act(lambda: sc.activation(flat(dc[q]), bank[:, 6, 128:128 + H * HD], ACT.Exp), ms, *ph.free("dc"))
                    ph.release("bank6", gd)
                    dms = ph.pool(lambda: g_.tensor_tensor(dm[q][:, :, :].rearrange("p h (c i) -> p h c i", c=NC),
                                                           dc[q][:, :, :].unsqueeze(2).to_broadcast([P, H, NC, HD]),
                                                           c("causal").rearrange("p (c i) -> p c i", c=NC).unsqueeze(1).to_broadcast([P, H, NC, HD]), ALU.mult),
                                  gd, *ph.free("dm"))
                    ph.release("dc", dms)
                    silu = []
                    for no, out, name in ((4, qk[q], "qk"), (5, vg[q], "vg")):
                        a = ph.act(lambda: sc.activation(th[q][:, :], bank[:, no, :], ACT.Tanh, scale=0.5), state[no], *ph.free("th"))
                        a = ph.dve(lambda: v.scalar_tensor_tensor(flat(out), th[q][:, :], 1.0, bank[:, no, :], ALU.add, ALU.mult), a, *ph.free(name))
                        ph.release("th", a)
                        ph.release(f"bank{no}", a)
                        silu.append(a)
                    a = ph.act(lambda: sc.activation(sq[q][:, :], flat(qk[q]), ACT.Square), silu[0], *ph.free("sq"))
                    a = ph.dve(lambda: v.tensor_reduce(rq[q][:, :], sq[q][:, :].rearrange("p (h k) -> p h k", k=HD), AX.X, ALU.add), a, *ph.free("rq"))
                    ph.release("sq", a)
                    a = self.rsqrt(ph, rq[q][:, :], rq[q][:, :], 1.0, 4e-6, a)
                    a = ph.dve(lambda: v.tensor_tensor(qk[q][:, :, :], qk[q][:, :, :], over_hd(rq[q][:, :]), ALU.mult), a)
                    ph.release("rq", a)
                    qn, kn, vv, gate = qk[q][:, 0:H, :], qk[q][:, H:, :], vg[q][:, 0:H, :], vg[q][:, H:, :]
                    down, up = gamma[q][:, 0:H], gamma[q][:, H:2 * H]
                    ps = lambda out, x, y, *s: ph.pool(lambda: g_.tensor_tensor(out[:, :, :], x, over_hd(y), ALU.mult), *s)
                    skb = ps(kb[q], kn, beta, a, bs, *ph.free("kb"))
                    sqg = ps(qg[q], qn, down, a, ga, *ph.free("qg"))
                    skc = ps(kc[q], kn, up, a, ga, *ph.free(f"kc{q}"))
                    svb = ps(vb[q], vv, half_beta, silu[1], bs, *ph.free("vb"))
                    x = ph.dve(lambda: v.tensor_scalar(ng, down, -1.0, None, ALU.mult), ga)
                    snw = ps(nw[q], kb[q][:, :, :], ng, skb, x, *ph.free("nw"))
                    ph.release("tiny", snw, ms)
                    sgg = ph.pool(lambda: g_.tensor_tensor(gg[q][:, :, :], gate, self.onorm[:, :].unsqueeze(1).to_broadcast([P, H, HD]), ALU.mult), silu[1], *ph.free(f"gg{q}"))
                    ph.release("vg", sgg, svb)
                    f2 = lambda t: t.rearrange("p h k -> p (h k)")
                    for n in range(2):
                        for m_, src in ((0, f2(kb[q][:, :, :])), (1, f2(qn))):
                            t0 = ph.pe(lambda: nc.tensor.transpose(bank[:, 0, (2 * n + m_) * P:(2 * n + m_ + 1) * P], src[:, n * P:(n + 1) * P], c("ident")),
                                       skb, a, *ph.free("bank0"))
                        for m_, src in ((0, f2(kn)), (1, f2(qg[q][:, :, :]))):
                            t1 = ph.pe(lambda: nc.tensor.transpose(bank[:, 1, (2 * m_ + n) * P:(2 * m_ + n + 1) * P], src[:, n * P:(n + 1) * P], c("ident")),
                                       sqg, *ph.free("bank1"))
                    ph.release("kb", t1, snw)
                    ph.release("qg", t1)
                    ph.release("qk", t1, skc)
                    x0 = ph.act(lambda: sc.activation(bq[q][:, :, :, :].rearrange("p a b t -> p (a b t)"), bank[:, 0, :], ACT.Copy), t0, *ph.free("bq"))
                    x1_ = ph.dve(lambda: v.tensor_copy(flat(kT[q]), bank[:, 1, 0:2 * P]), t1, *ph.free("kT"))
                    x2_ = ph.dve(lambda: v.tensor_copy(flat(qgT[q]), bank[:, 1, 2 * P:4 * P]), t1, *ph.free(f"qgT{q}"))
                    ph.release("bank0", x0)
                    ph.release("bank1", x2_)
                    grams = []
                    for n in range(2):
                        for r in range(HG):
                            gm = ph.pe(lambda: nc.tensor.matmul(bank[:, r, 2 * P * n:2 * P * (n + 1)], kT[q][HD * r:HD * (r + 1), n, :],
                                                                bq[q][HD * r:HD * (r + 1), n, :, :].rearrange("p a t -> p (a t)"), start=True, stop=True),
                                       x0, x1_, *ph.free(f"bank{r}"))
                        grams.append(gm)
                    ph.release("bq", gm)
                    ph.release("kT", gm)
                    for n in range(2):
                        at_ = bank[:, 0:HG, 2 * P * n:2 * P * n + P]
                        bt_ = bank[:, 0:HG, 2 * P * n + P:2 * P * (n + 1)]
                        heads = slice(HG * n, HG * (n + 1))
                        nt = ph.dve(lambda: v.scalar_tensor_tensor(NT[q][:, heads, :], at_, -1.0, dm[q][:, heads, :], ALU.mult, ALU.mult), grams[1], dms, *ph.free("NT"))
                        bt = ph.dve(lambda: v.tensor_tensor(Bt[q][:, heads, :], bt_, dm[q][:, heads, :], ALU.mult), grams[1], dms, *ph.free(f"Bt{q}"))
                    for r in range(HG):
                        ph.release(f"bank{r}", bt)
                    ph.release("dm", bt)
                    ready = {}
                    for n in range(2):
                        heads = slice(HG * n, HG * (n + 1))
                        y = ph.pool(lambda: g_.tensor_copy(Y[q][:, heads, :], per4(c("ident"))), *ph.free("Y"))
                        ready[n] = ph.dve(lambda: v.copy_predicated(Y[q][:, heads, :], per4(self.level[:, 0, :]), NT[q][:, heads, :]), y, nt, plain=True)
                    f3 = lambda t: t.rearrange("p h k -> p (h k)")
                    for s in range(1, LEVELS):
                        for n in range(2):
                            for r in range(HG):
                                hd = HG * n + r
                                t = ph.pe(lambda: nc.tensor.transpose(bank[:, n, r * P:(r + 1) * P], Y[q][:, hd, :], c("ident")), ready[n], *ph.free(f"bank{n}"))
                            e = ph.act(lambda: sc.activation(f3(X[q][:, HG * n:HG * (n + 1), :]), bank[:, n, :], ACT.Copy), t, *ph.free(f"X{n}"))
                            for r in range(HG):
                                hd = HG * n + r
                                m = ph.pe(lambda: nc.tensor.matmul(bank[:, n, r * P:(r + 1) * P], NT[q][:, hd, :], X[q][:, hd, :], start=True, stop=True), e)
                            ph.release(f"X{n}", m)
                            e = ph.act(lambda: sc.activation(f3(R[q][:, HG * n:HG * (n + 1), :]), bank[:, n, :], ACT.Copy), m, *ph.free(f"R{n}"))
                            ph.release(f"bank{n}", e)
                            for r in range(HG):
                                hd = HG * n + r
                                m = ph.pe(lambda: nc.tensor.matmul(bank[:, 2 + n, r * P:(r + 1) * P], R[q][:, hd, :], Y[q][:, hd, :], start=True, stop=True), e, *ph.free(f"bank{2 + n}"))
                            ph.release(f"R{n}", m)
                            ready[n] = ph.dve(lambda: v.copy_predicated(Y[q][:, HG * n:HG * (n + 1), :], per4(self.level[:, s, :]),
                                                                        bank[:, 2 + n, :].rearrange("p (r t) -> p r t", r=HG)), m, plain=True)
                            ph.release(f"bank{2 + n}", ready[n])
                    ph.release("NT", m)
                    for n in range(2):
                        for r in range(HG):
                            hd = HG * n + r
                            m = ph.pe(lambda: nc.tensor.matmul(bank[HD * r:HD * (r + 1), 4, n * P:(n + 1) * P], nw[q][:, hd, :], Y[q][:, hd, :], start=True, stop=True),
                                      ready[n], snw, *ph.free("bank4"))
                    ph.release("nw", m)
                    w = ph.act(lambda: sc.activation(flat(WT[q]), bank[:, 4, 0:2 * P], ACT.Copy), m, *ph.free(f"WT{q}"))
                    ph.release("bank4", w)
                    for hd in range(H):
                        m = ph.pe(lambda: nc.tensor.matmul(bank[:, 5, hd * HD:(hd + 1) * HD], Y[q][:, hd, :], vb[q][:, hd, :], start=hd == 0, stop=False, skip_group_check=True),
                                  svb, *ph.free("bank5"))
                    ph.release("vb", m)
                    ph.release("Y", m)
                    state.update(w=w, u=m, skc=skc, sgg=sgg, ga=ga, bt=bt, qgt=x2_)

                def block_b(b, got):
                    q = b % 2
                    prev = ph.free(f"S{b}")
                    for ch in range(NC):
                        part = slice(C * ch, C * (ch + 1))
                        for n in range(2):
                            mo = ph.pe(lambda: nc.tensor.matmul(bank[part, 7, n * P:(n + 1) * P], qgT[q][:, n, part], S[b][:, n, :], start=n == 0, stop=False, skip_group_check=True),
                                       got["qgt"], *prev, *ph.free("bank7"))
                        for n in range(2):
                            mu = ph.pe(lambda: nc.tensor.matmul(bank[part, 5, n * P:(n + 1) * P], WT[q][:, n, part], S[b][:, n, :], start=False, stop=True, skip_group_check=True),
                                       got["w"], *prev)
                        u = ph.act(lambda: sc.activation(us[q][part, :], bank[part, 5, 0:D], ACT.Copy), mu, *ph.free("us"))
                        for n in range(2):
                            ms = ph.pe(lambda: nc.tensor.matmul(bank[:, 6, n * P:(n + 1) * P], kc[q][part, HG * n:HG * (n + 1), :].rearrange("p a b -> p (a b)"),
                                                                us[q][part, n * P:(n + 1) * P], start=True, stop=True), u, got["skc"], *ph.free("bank6"))
                        x = ph.dve(lambda: v.tensor_tensor(sm[q][:, :, :], bank[:, 6, 0:2 * P].rearrange("p (n t) -> p n t", n=2),
                                                           c("diag").unsqueeze(1).to_broadcast([P, 2, P]), ALU.mult), ms, *ph.free("sm"))
                        ph.release("bank6", x)
                        for n in range(2):
                            x = ph.dve(lambda: v.scalar_tensor_tensor(S[b][:, n, :], S[b][:, n, :], gamma[q][:, 2 * H + NC * n + ch:2 * H + NC * n + ch + 1],
                                                                      sm[q][:, n, :], ALU.mult, ALU.add), x, mu, got["ga"])
                        ph.release("sm", x)
                        prev = (x,)
                    ph.release(f"S{b}", x)
                    ph.release(f"kc{q}", ms)
                    ph.release(f"WT{q}", mu)
                    ph.release(f"qgT{q}", mo)
                    ph.release(f"gamma{q}", x)
                    ph.release("bank5", u)
                    for hd in range(H):
                        m = ph.pe(lambda: nc.tensor.matmul(bank[:, 7, hd * HD:(hd + 1) * HD], Bt[q][:, hd, :], us[q][:, hd * HD:(hd + 1) * HD], start=False, stop=True,
                                                           skip_group_check=True), u, got["bt"])
                    ph.release("us", m)
                    ph.release(f"Bt{q}", m)
                    o = bank[:, 7, 0:D]
                    a = ph.act(lambda: sc.activation(os_[q][:, :], o, ACT.Square), m, *ph.free("os"))
                    a = ph.dve(lambda: v.tensor_reduce(ro[q][:, :], os_[q][:, :].rearrange("p (h k) -> p h k", k=HD), AX.X, ALU.add), a, *ph.free("ro"))
                    ph.release("os", a)
                    a = self.rsqrt(ph, ro[q][:, :], ro[q][:, :], 1.0 / HD, 1e-6, a)
                    o3 = og[q][:, :].rearrange("p (h k) -> p h k", k=HD)
                    a = ph.dve(lambda: v.tensor_tensor(o3, o.rearrange("p (h k) -> p h k", k=HD), over_hd(ro[q][:, :]), ALU.mult), a, *ph.free("og"))
                    ph.release("bank7", a)
                    ph.release("ro", a)
                    a = ph.dve(lambda: v.tensor_tensor(o3, o3, gg[q][:, :, :], ALU.mult), a, got["sgg"])
                    ph.release(f"gg{q}", a)
                    t, e = transpose(og[q], ogT[q], 4, "ogT", (a,))
                    ph.release("og", t)
                    for k in range(KD):
                        m = ph.pe(lambda: nc.tensor.matmul(bank[:, 5, 0:D], ogT[q][:, k, :], self.w_o[:, k, :], start=k == 0, stop=k == KD - 1), e, *ph.free("bank5"))
                    ph.release("ogT", m)
                    a = ph.dve(lambda: v.scalar_tensor_tensor(x1a[q][:, :], bank[:, 5, 0:D], RES * 0.5, xa[q][:, :], ALU.mult, ALU.add), m, *ph.free("x1a"))
                    ph.release("bank5", a)
                    ph.release(f"xa{q}", a)
                    n2 = rms(x1a[q][:, :], h2[q][:, :], q, (a,), ph.free("h2"))
                    t, e = transpose(h2[q], h2T[q], 4, "h2T", (n2,), self.ln2)
                    ph.release("h2", t)
                    acts = []
                    for n in range(2):
                        for f in range(4):
                            for k in range(KD):
                                fb = 4 * n + f
                                m = ph.pe(lambda: nc.tensor.matmul(bank[:, 6 + n, f * P:(f + 1) * P], self.w_fc[:, k, fb * P:(fb + 1) * P], h2T[q][:, k, :],
                                                                   start=k == 0, stop=k == KD - 1), e, *ph.free(f"bank{6 + n}"))
                        a = ph.act(lambda: sc.activation(th[q][:, :], bank[:, 6 + n, :], ACT.Tanh, scale=0.5), m, *ph.free("th"))
                        a = ph.dve(lambda: v.scalar_tensor_tensor(aT[q][:, 4 * n:4 * n + 4, :].rearrange("p f t -> p (f t)"), th[q][:, :], 1.0, bank[:, 6 + n, :],
                                                                  ALU.add, ALU.mult), a, *ph.free("aT"))
                        ph.release("th", a)
                        ph.release(f"bank{6 + n}", a)
                        acts.append(a)
                    ph.release("h2T", m)
                    for f in range(FB):
                        m = ph.pe(lambda: nc.tensor.matmul(bank[:, 5, 0:D], aT[q][:, f, :], self.w_p[:, f, :], start=f == 0, stop=f == FB - 1), acts[f // 4], *ph.free("bank5"))
                    ph.release("aT", m)
                    a = ph.dve(lambda: v.scalar_tensor_tensor(x2[q][:, :], bank[:, 5, 0:D], RES * 0.5, x1a[q][:, :], ALU.mult, ALU.add), m, *ph.free(f"x2{q}"))
                    ph.release("bank5", a)
                    ph.release("x1a", a)
                    a = ph.dve(lambda: v.tensor_tensor(x2[q][:, :], x2[q][:, :], x1[q][:, :], ALU.add), a)
                    ph.release(f"x1{q}", a)
                    kept = ph.dma("sp", f"x2{q}", lambda: nc.sync.dma_start(self.dram["x2"][bass.ds(row(b), P), :], x2[q][:, :]), a)
                    n = norm(x2[q][:, :], xn2[q][:, :], q, (a,), ph.free(f"xn2{q}"))
                    ph.release(f"x2{q}", kept, n)
                    kept = ph.dma("sp", f"xn2{q}", lambda: nc.sync.dma_start(self.dram["xn"][bass.ds(row(b), P), :], xn2[q][:, :]), n)
                    t, e = transpose(xn2[q], xn2T[q], 4, "xn2T", (n,))
                    ph.release(f"xn2{q}", kept, t)
                    for k in range(KD):
                        m = ph.pe(lambda: nc.tensor.matmul(bank[:, 5, 0:E], xn2T[q][:, k, :], self.router[:, k, :], start=k == 0, stop=k == KD - 1), e, *ph.free("bank5"))
                    ph.release("xn2T", m)
                    l = ph.dve(lambda: v.tensor_copy(self.logits[:, :, bass.ds(tile(b), 1)].rearrange("p e t -> p (e t)"), bank[:, 5, 0:E]), m)
                    ph.release("bank5", l)

                for b in range(B):
                    block_a(b)
                    block_b(b, dict(state))

    def build(self):
        self.start()
        self.route_first()
        self.choose("choose1")
        self.scatter("scatter1", "disp1")
        self.experts("experts1", "disp1", "eo")
        self.attention("eo")
        self.choose("choose2")
        self.scatter("scatter2", "disp2")
        self.experts("experts2", "disp2", "eo2")
        self.finish("eo2")


DRAM_IN = {
    "x": (N, D), "ln1_w": (D,), "qw": (D, D), "kw": (D, D), "vw": (D, D), "bw": (D, H), "aw": (D, H), "A_log": (H,), "dt_bias": (H,),
    "gw": (D, D), "onorm_w": (HD,), "ow": (D, D), "ln2_w": (D,), "fcw": (D, F), "pw": (F, D),
    "router_t": (D, E), "wg": (E * D, F), "wu": (E * D, F), "wd": (E * F, D),
}
SCRATCH = {"xn": (N, D), "disp1": (SLOTS, D), "disp2": (SLOTS, D), "eo": (SLOTS, D), "eo2": (SLOTS, D), "x2": (N, D)}


def build(nc, book, parts=None):
    const, _, level = constants()
    dram = {n: nc.dram_tensor(f"in_{n}", s, F32, kind="ExternalInput").ap() for n, s in DRAM_IN.items()}
    dram["const"] = nc.dram_tensor("in_const", const.shape, F32, kind="ExternalInput").ap()
    dram["level"] = nc.dram_tensor("in_level", level.shape, I32, kind="ExternalInput").ap()
    for n, s in SCRATCH.items():
        dram[n] = nc.dram_tensor(f"tmp_{n}", s, F32, kind="Internal").ap()
    dram["out"] = nc.dram_tensor("out", (N, D), F32, kind="ExternalOutput").ap()
    with ExitStack() as ctx:
        p = Program(nc, book, ctx, dram)
        (parts or Program.build)(p)
    return nc


def layout(inputs):
    a = {n: np.ascontiguousarray(inputs["L0_attn_" + n]) for n in DRAM_IN if "L0_attn_" + n in inputs}
    a["x"] = a["x"].reshape(N, D)
    a["router_t"] = np.ascontiguousarray(np.transpose(inputs["L0_ffn_router_w"]))
    for n in ("wg", "wu", "wd"):
        w = np.ascontiguousarray(inputs["L0_ffn_" + n])
        a[n] = w.reshape(w.shape[0] * w.shape[1], w.shape[2])
    const, _, level = constants()
    a["const"], a["level"] = const, level
    return {f"in_{n}": x for n, x in a.items()}


def kernel(**inputs):
    import concourse.bacc as bacc
    from concourse.bass_utils import run_bass_kernel_spmd

    book = {}
    build(bacc.Bacc("TRN2", target_bir_lowering=False, num_devices=1), book)
    nc = build(bacc.Bacc("TRN2", target_bir_lowering=False, num_devices=1), book)
    r = run_bass_kernel_spmd(nc, [layout(inputs)], core_ids=[0])
    return r.results[0]["out"].reshape(B, T, D)
```

```python
from contextlib import ExitStack

import concourse.bass as bass
import numpy as np
from concourse import mybir
from concourse.alu_op_type import AluOpType as ALU

ACT = mybir.ActivationFunctionType
AX = mybir.AxisListType
F32 = mybir.dt.float32
I32 = mybir.dt.int32

P = 128
B, T, D = 4, 2048, 256
N = B * T
TILES = N // P
KD = D // P
E, TOPK, CAP = 8, 2, max(1, int(1.25 * N / 8))
F = 1024
FB = F // P
H, HD = 8, 32
C = 32
NC = P // C
HG = 4
LEVELS = 5
SLOTS = E * CAP
AHEAD = 4
SKIP = SLOTS
G_LEAST = -200.0
RES = 0.5


def constants():
    p = np.arange(P)
    same = (p[:, None] // C) == (p[None, :] // C)
    cols = {
        "ident": np.eye(P),
        "ones": np.ones((P, P)),
        "before": p[:, None] < p[None, :],
        "upto": same & (p[:, None] <= p[None, :]),
        "after": same & (p[:, None] > p[None, :]),
        "within": (p[:, None] % C) <= np.arange(C)[None, :],
        "causal": (same & (p[:, None] <= p[None, :])),
        "diag": same,
        "chunk": (p[:, None] // C) == np.arange(NC)[None, :],
        "minus_half": np.full((P, 16), -0.5),
        "expert_less_8": np.broadcast_to(np.arange(E)[None, :, None] - 8.0, (P, E, TILES)).reshape(P, -1),
        "first_slot": np.broadcast_to((np.arange(E) * CAP)[None, :, None] - float(SKIP), (P, E, TILES)).reshape(P, -1),
        "column": np.broadcast_to(np.arange(P)[None, :], (P, P)),
        "token": np.arange(TILES)[None, :] * P + p[:, None],
        "not_first_tile": np.broadcast_to((np.arange(TILES) != 0)[None, None, :], (P, E, TILES)).reshape(P, -1),
    }
    at, where, parts = 0, {}, []
    for name, a in cols.items():
        where[name] = (at, a.shape[1])
        parts.append(a.astype(np.float32))
        at += a.shape[1]
    levels = [((p[:, None] >> (s + 1)) == (p[None, :] >> (s + 1))) & ((p[:, None] >> s) % 2 == 0) & ((p[None, :] >> s) % 2 == 1)
              for s in range(LEVELS)]
    return np.concatenate(parts, 1), where, np.concatenate(levels, 1).astype(np.int32)


class Step:

    def __init__(self, meter, k, turn=0):
        self.meter, self.k, self.turn = meter, k, turn


class Meter:

    def __init__(self, sem, name, unit, each_turn):
        self.sem, self.name, self.unit, self.each_turn, self.k = sem, name, unit, each_turn, 0
        self.ahead = 0 if name.startswith("swdma") else 1


class Phase:

    def __init__(self, prog, name, turns=0, settle=True):
        self.ends_settled = settle
        self.nc, self.book, self.name, self.turns = prog.nc, prog.book, name, turns
        self.semaphore = lambda n: prog.ctx.enter_context(prog.nc.semaphore(f"{name}_{n}"))
        self.loop = ExitStack()
        self.engines = {"pe": self.nc.tensor, "act": self.nc.scalar, "dve": self.nc.vector, "pool": self.nc.gpsimd, "sp": self.nc.sync}
        self.meters, self.waited, self.owners = {}, {}, {}

    def __enter__(self):
        for name, (unit, each_turn) in sorted(self.book.get((self.name, "meters"), {}).items()):
            m = self.meters[name] = Meter(self.semaphore(name), name, unit, each_turn)
            if self.turns and m.ahead:
                self.nc.sync.sem_inc(m.sem, unit * each_turn)
        self.passed = self.semaphore("passed")
        self.i = self.loop.enter_context(self.nc.Fori(0, self.turns)) if self.turns else 0
        return self

    def meter(self, name, unit):
        if name not in self.meters:
            self.meters[name] = Meter(self.semaphore(name), name, unit, 1)
        return self.meters[name]

    def wait(self, engine, *steps, plain=False):
        need = {}
        for s in steps:
            m = s.meter
            assert s.turn == 0 or m.ahead
            at = s.k + (m.each_turn if self.turns else 0) * (m.ahead + s.turn)
            if at > max(need.get(m.name, 0), self.waited.get((engine, m.name), 0)):
                need[m.name] = at
        for name, at in need.items():
            m = self.meters[name]
            self.waited[engine, name] = at
            self.engines[engine].wait_ge(m.sem, self.i * (m.unit * m.each_turn) + m.unit * at if self.turns else m.unit * at)
            if plain and self.turns:
                self.engines[engine].sem_inc(self.passed, 1)

    def run(self, engine, make, *steps, plain=False):
        self.wait(engine, *steps, plain=plain or engine == "pool")
        m = self.meter(engine, 1)
        m.k += 1
        make().then_inc(m.sem, 1)
        return Step(m, m.k)

    def dma(self, queue, buffer, make, *steps):
        self.wait(queue, *steps, plain=queue in ("pool", "sp"))
        m = self.meter(("swdma_" if queue == "pool" else "dma_") + buffer, 16)
        m.k += 1
        make().then_inc(m.sem, 16)
        return Step(m, m.k)

    def relay(self, engine, *steps):
        self.wait(engine, *steps, plain=engine in ("pool", "sp"))
        m = self.meter(engine, 1)
        m.k += 1
        self.engines[engine].sem_inc(m.sem, 1)
        return Step(m, m.k)

    def pe(self, make, *steps):
        return self.run("pe", make, *steps)

    def act(self, make, *steps):
        return self.run("act", make, *steps)

    def dve(self, make, *steps, plain=False):
        return self.run("dve", make, *steps, plain=plain)

    def pool(self, make, *steps):
        return self.run("pool", make, *steps)

    def release(self, buffer, *steps):
        self.owners[buffer] = steps

    def free(self, buffer):
        if buffer in self.owners or not self.turns:
            return self.owners.get(buffer, ())
        last = self.book.get((self.name, "owners"), {}).get(buffer, ())
        return tuple(Step(self.meters[name], k, -1) for name, k in last)

    def __exit__(self, *error):
        self.loop.close()
        if error[0] is not None:
            return
        self.book[self.name, "owners"] = {b: [(s.meter.name, s.k) for s in steps] for b, steps in self.owners.items()}
        self.book[self.name, "meters"] = {n: (m.unit, m.k) for n, m in self.meters.items()}
        if self.ends_settled:
            self.settle()
        self.nc.all_engine_barrier()

    def settle(self):
        for m in self.meters.values():
            if m.unit == 16:
                self.nc.sync.wait_ge(m.sem, 16 * m.k * (self.turns + m.ahead if self.turns else 1))


class Program:
    def __init__(self, nc, book, ctx, dram):
        self.nc, self.book, self.ctx, self.dram = nc, book, ctx, dram
        self.sync, self.tensor, self.vector, self.scalar, self.gpsimd = nc.sync, nc.tensor, nc.vector, nc.scalar, nc.gpsimd
        self.temps = 0
        sb = self.sb
        self.bank = ctx.enter_context(nc.psum_tensor("bank", [P, 8, 512], F32))
        _, self.where, _ = constants()
        width = sum(w for _, w in self.where.values())
        self.const = sb("const", [P, width])
        self.level = sb("level", [P, LEVELS, P], I32)
        self.router = sb("router", [P, KD, E])
        self.w_qk, self.w_vg, self.w_ba = sb("w_qk", [P, KD, 2 * D]), sb("w_vg", [P, KD, 2 * D]), sb("w_ba", [P, KD, 2 * H])
        self.w_o, self.w_fc, self.w_p = sb("w_o", [P, KD, D]), sb("w_fc", [P, KD, F]), sb("w_p", [P, FB, D])
        self.ln1, self.ln2 = sb("ln1", [P, KD]), sb("ln2", [P, KD])
        self.onorm = sb("onorm", [P, HD])
        self.decay, self.dt_bias = sb("decay", [P, H]), sb("dt_bias", [P, H])
        self.logits = sb("logits", [P, E, TILES])
        self.slot = sb("slot", [P, TOPK, TILES], I32)
        self.fetch = sb("fetch", [P, TOPK, TILES], I32)
        self.weight = sb("weight", [P, TOPK, TILES])
        self.source = sb("source", [P, SLOTS // P + AHEAD], I32)

    def sb(self, name, shape, dtype=F32):
        return self.ctx.enter_context(self.nc.sbuf_tensor(name, shape, dtype))

    def temp(self, stack, name, shape, dtype=F32):
        self.temps += 1
        return stack.enter_context(self.nc.sbuf_tensor(f"{name}_{self.temps}", shape, dtype))

    def c(self, name):
        at, width = self.where[name]
        return self.const[:, at:at + width]

    def rows(self, name, first, count):
        return self.dram[name][bass.ds(first, count), :].rearrange("(j p) d -> p j d", p=P)

    def load(self, ph, dst, src, **how):
        return ph.dma("sp", "const", lambda: self.nc.sync.dma_start(dst, src, **how))

    def start(self):
        dram = self.dram
        with Phase(self, "start") as ph:
            self.load(ph, self.const[:, :], dram["const"])
            self.load(ph, self.router[:, :, :], dram["router_t"].rearrange("(k p) f -> p k f", p=P))

    def load_block(self, ph):
        nc, dram, load = self.nc, self.dram, lambda *a, **how: self.load(ph, *a, **how)
        blocks = lambda name: dram[name].rearrange("(k p) f -> p k f", p=P)
        load(self.dt_bias[:, :], dram["dt_bias"].partition_broadcast(P))
        last = ph.dma("sp", "decay", lambda: nc.sync.dma_start(self.decay[:, :], dram["A_log"].partition_broadcast(P)))
        e = ph.act(lambda: nc.scalar.activation(self.decay[:, :], self.decay[:, :], ACT.Exp), last)
        ph.dve(lambda: nc.vector.tensor_scalar(self.decay[:, :], self.decay[:, :], -1.0, None, ALU.mult), e)
        load(self.level[:, :, :], dram["level"].rearrange("p (s i) -> p s i", s=LEVELS))
        for w, a, b in ((self.w_qk, "qw", "kw"), (self.w_vg, "vw", "gw"), (self.w_ba, "bw", "aw")):
            half = w.shape[2] // 2
            load(w[:, :, 0:half], blocks(a))
            load(w[:, :, half:], blocks(b))
        load(self.w_o[:, :, :], blocks("ow"))
        load(self.w_fc[:, :, :], blocks("fcw"))
        load(self.w_p[:, :, :], blocks("pw"))
        load(self.ln1[:, :], dram["ln1_w"].rearrange("(k p) -> p k", p=P), allow_slow_non_contiguous=True)
        load(self.ln2[:, :], dram["ln2_w"].rearrange("(k p) -> p k", p=P), allow_slow_non_contiguous=True)
        load(self.onorm[:, :], dram["onorm_w"].partition_broadcast(P))

    def route_first(self):
        nc = self.nc
        J, U = 4, 2
        with ExitStack() as tmp:
            sb = lambda n, s: self.temp(tmp, n, s, F32)
            x4 = [sb(f"x4_{u}", [P, J, D]) for u in range(U)]
            xn = [sb(f"xn_{u}", [P, J, D]) for u in range(U)]
            xt = [sb(f"xt_{u}", [P, J, KD, P]) for u in range(U)]
            st = [sb(f"st_{u}", [P, J, 6]) for u in range(U)]
            mv = [sb(f"mv_{u}", [P, J, 2]) for u in range(U)]
            rs = [sb(f"rs_{u}", [P, J]) for u in range(U)]
            with Phase(self, "route1", TILES // (J * U)) as ph:
                for u in range(U):
                    row = ph.i * (J * U * P) + u * J * P
                    x = ph.dma("sp", f"x{u}", lambda: nc.sync.dma_start(x4[u][:, :, :], self.rows("x", row, J * P)), *ph.free(f"x4_{u}"))
                    for j in range(J):
                        s = ph.dve(lambda: nc.vector.bn_stats(st[u][:, j, :], x4[u][:, j, :]), x, *ph.free(f"st{u}"))
                    for j in range(J):
                        s = ph.dve(lambda: nc.vector.bn_aggr(mv[u][:, j, :], st[u][:, j, :]), s, *ph.free(f"mv{u}"), plain=True)
                    r = self.rsqrt(ph, rs[u][:, :], mv[u][:, :, 1], 1.0, 1e-5, s, *ph.free(f"mv{u}"))
                    ph.release(f"st{u}", s)
                    for j in range(J):
                        n = ph.dve(lambda: nc.vector.tensor_scalar(xn[u][:, j, :], x4[u][:, j, :], mv[u][:, j, 0:1], rs[u][:, j:j + 1],
                                                                   ALU.subtract, ALU.mult), r, *ph.free(f"xn{u}"))
                    ph.release(f"x4_{u}", n)
                    ph.release(f"mv{u}", n)
                    kept = ph.dma("sp", f"xn{u}", lambda: nc.sync.dma_start(self.rows("xn", row, J * P), xn[u][:, :, :]), n)
                    for j in range(J):
                        for k in range(KD):
                            o = self.bank[:, 2 * u + j // 2, (j % 2 * KD + k) * P:(j % 2 * KD + k + 1) * P]
                            t = ph.pe(lambda: nc.tensor.transpose(o, xn[u][:, j, k * P:(k + 1) * P], self.c("ident")), n, *ph.free(f"xt bank{u}"))
                    ph.release(f"xn{u}", kept, t)
                    for j in range(0, J, 2):
                        e = ph.act(lambda: nc.scalar.activation(xt[u][:, j:j + 2, :, :].rearrange("p j k t -> p (j k t)"), self.bank[:, 2 * u + j // 2, :], ACT.Copy),
                                   t, *ph.free(f"xt{u}"))
                    ph.release(f"xt bank{u}", e)
                    for j in range(J):
                        for k in range(KD):
                            m = ph.pe(lambda: nc.tensor.matmul(self.bank[:, 4 + u, j * E:(j + 1) * E], xt[u][:, j, k, :], self.router[:, k, :],
                                                               start=k == 0, stop=k == KD - 1), e, *ph.free(f"logit bank{u}"))
                    ph.release(f"xt{u}", m)
                    l = ph.dve(lambda: nc.vector.tensor_copy(self.logits[:, :, bass.ds(ph.i * (J * U) + u * J, J)],
                                                             self.bank[:, 4 + u, 0:J * E].rearrange("p (j e) -> p e j", e=E)), m, )
                    ph.release(f"logit bank{u}", l)

    def rsqrt(self, ph, out, in_, scale, eps, *steps):
        nc = self.nc
        a = ph.pool(lambda: nc.gpsimd.tensor_scalar(out, in_, scale, eps, ALU.mult, ALU.add), *steps)
        half = self.c("minus_half")[:, 0:out.free_size()]
        return ph.pool(lambda: nc.gpsimd.tensor_tensor(out, out, half, ALU.pow), a)

    def choose(self, name, alongside=lambda ph: None):
        nc, v, c = self.nc, self.nc.vector, self.c
        with ExitStack() as tmp:
            sb = lambda n, s, d=F32: self.temp(tmp, n, s, d)
            full = lambda n: sb(n, [P, E, TILES])
            p, hot1, hot2, w, a, b, s = (full(n) for n in ("p", "hot1", "hot2", "w", "a", "b", "s"))
            m, r, m1, m2 = (sb(n, [P, TILES]) for n in ("m", "r", "m1", "m2"))
            per = lambda n, d=F32: sb(n, [P, E], d)
            cand, least, more, count, quota = per("cand", I32), per("least", I32), per("more", I32), per("count"), per("quota")
            flat = lambda t: t[:, :, :].rearrange("p e t -> p (e t)")
            te = lambda t: t[:, :, :].rearrange("p e t -> p t e")
            over_e = lambda t: t[:, :].unsqueeze(1).to_broadcast([P, E, TILES])
            over_t = lambda t: t.unsqueeze(2).to_broadcast([P, E, TILES])
            bank = [self.bank[:, n, :] for n in range(4)]
            psum = lambda n: bank[n].rearrange("p (e t) -> p e t", e=E)
            less8 = c("expert_less_8").rearrange("p (e t) -> p e t", e=E)
            tt, ts, stt = v.tensor_tensor, v.tensor_scalar, v.scalar_tensor_tensor
            with Phase(self, name) as ph:
                alongside(ph)
                last = [()]

                def dve(make, *steps):
                    last[0] = (ph.dve(make, *last[0], *steps),)
                    return last[0][0]

                A = lambda t: t[:, :, :]
                dve(lambda: v.tensor_reduce(m[:, :], te(self.logits), AX.X, ALU.max))
                x = dve(lambda: tt(A(p), A(self.logits), over_e(m), ALU.subtract))
                x = ph.act(lambda: nc.scalar.activation(A(p), A(p), ACT.Exp), x)
                dve(lambda: v.tensor_reduce(m[:, :], te(p), AX.X, ALU.add), x)
                dve(lambda: v.reciprocal(r[:, :], m[:, :]))
                dve(lambda: tt(A(p), A(p), over_e(r), ALU.mult))
                for best, hot in ((m1, hot1), (m2, hot2)):
                    dve(lambda: v.tensor_reduce(best[:, :], te(p), AX.X, ALU.max))
                    dve(lambda: tt(A(a), A(p), over_e(best), ALU.is_equal))
                    dve(lambda: tt(A(a), A(a), less8, ALU.mult))
                    dve(lambda: v.tensor_reduce(m[:, :], te(a), AX.X, ALU.min))
                    dve(lambda: tt(A(hot), less8, over_e(m), ALU.is_equal))
                    if best is m1:
                        dve(lambda: stt(flat(p), flat(hot), -2.0, flat(p), ALU.mult, ALU.add))
                dve(lambda: stt(r[:, :], m1[:, :], 1e-6, m2[:, :], ALU.add, ALU.add))
                dve(lambda: v.reciprocal(r[:, :], r[:, :]))
                dve(lambda: tt(m1[:, :], m1[:, :], r[:, :], ALU.mult))
                dve(lambda: tt(m2[:, :], m2[:, :], r[:, :], ALU.mult))
                dve(lambda: tt(A(a), A(hot1), over_e(m1), ALU.mult))
                dve(lambda: tt(A(w), A(hot2), over_e(m2), ALU.mult))
                dve(lambda: tt(A(w), A(w), A(a), ALU.add))
                dve(lambda: tt(A(s), A(hot1), A(hot2), ALU.add))

                def total(src, out_bank, width, lhs="ones"):
                    x = last[0][0]
                    return ph.pe(lambda: nc.tensor.matmul(bank[out_bank][:, 0:width], c(lhs), src, start=True, stop=True), x)

                dve(lambda: v.memset(least[:, :], 0))
                for bit in range(29, -1, -1):
                    dve(lambda: v.tensor_scalar(cand[:, :], least[:, :], 1 << bit, None, ALU.bitwise_or))
                    dve(lambda: tt(A(a), A(w), over_t(cand[:, :].bitcast(F32)), ALU.is_ge))
                    dve(lambda: v.tensor_reduce(count[:, :], A(a), AX.X, ALU.add))
                    x = total(count[:, :], 0, E)
                    dve(lambda: ts(more[:, :], bank[0][:, 0:E], float(CAP), None, ALU.is_ge), x)
                    dve(lambda: v.copy_predicated(least[:, :], more[:, :], cand[:, :]))
                floor = over_t(least[:, :].bitcast(F32))
                dve(lambda: tt(A(a), A(w), floor, ALU.is_gt))
                dve(lambda: v.tensor_reduce(count[:, :], A(a), AX.X, ALU.add))
                x = total(count[:, :], 0, E)
                dve(lambda: ts(quota[:, :], bank[0][:, 0:E], -1.0, float(CAP), ALU.mult, ALU.add), x)
                dve(lambda: tt(A(b), A(w), floor, ALU.is_equal))
                dve(lambda: tt(A(b), A(b), A(s), ALU.mult))

                def before(mask, out, tmp_):
                    total(flat(mask), 1, E * TILES, "before")
                    x = total(flat(mask), 2, E * TILES)
                    dve(lambda: v.tensor_copy(flat(tmp_), bank[2]), x)
                    dve(lambda: v.tensor_tensor_scan(flat(out), c("not_first_tile"), flat(tmp_), 0.0, ALU.mult, ALU.add))
                    dve(lambda: tt(A(out), A(out), A(tmp_), ALU.subtract))
                    dve(lambda: tt(A(out), A(out), psum(1), ALU.add), x)

                before(b, p, w)
                dve(lambda: tt(A(p), A(p), over_t(quota[:, :]), ALU.is_lt))
                dve(lambda: tt(A(b), A(b), A(p), ALU.mult))
                dve(lambda: tt(A(a), A(a), A(b), ALU.add))
                before(a, p, w)
                dve(lambda: tt(flat(p), flat(p), c("first_slot"), ALU.add))
                dve(lambda: tt(A(p), A(p), A(a), ALU.mult))
                for k, (hot, weight) in enumerate(((hot1, m1), (hot2, m2))):
                    dve(lambda: tt(A(b), A(hot), A(p), ALU.mult))
                    dve(lambda: v.tensor_reduce(m[:, :], te(b), AX.X, ALU.add))
                    dve(lambda: ts(m[:, :], m[:, :], float(SKIP), None, ALU.add))
                    dve(lambda: v.tensor_copy(self.slot[:, k, :], m[:, :]))
                    dve(lambda: tt(A(b), A(hot), A(a), ALU.mult))
                    dve(lambda: v.tensor_reduce(r[:, :], te(b), AX.X, ALU.add))
                    dve(lambda: tt(self.weight[:, k, :], weight[:, :], r[:, :], ALU.mult))
                    dve(lambda: tt(m[:, :], m[:, :], r[:, :], ALU.mult))
                    dve(lambda: v.tensor_copy(self.fetch[:, k, :], m[:, :]))

    def invert(self, name, alongside=lambda ph: None):
        nc, v, c, J = self.nc, self.nc.vector, self.c, 8
        ROUNDS, QUEUE = TILES // J, 4
        with ExitStack() as tmp:
            sb = lambda n, s, d=F32: self.temp(tmp, n, s, d)
            whole = sb("whole", [P, TOPK, TILES], I32)
            lo, hi = sb("lo", [P, TOPK, TILES]), sb("hi", [P, TOPK, TILES])
            lo_j, hi_j, token_j = sb("lo_j", [P, TOPK, J]), sb("hi_j", [P, TOPK, J]), sb("token_j", [P, J])
            is_p = [sb(f"is_p{u}", [P, P]) for u in range(QUEUE)]
            at_a = [sb(f"at_a{u}", [P, SLOTS // P]) for u in range(QUEUE)]
            table = self.bank[:, 0, 0:SLOTS // P]
            with Phase(self, name + "_places", settle=False) as ph:
                first = ph
                alongside(ph)
                for out, op, by in ((lo, ALU.bitwise_and, P - 1), (hi, ALU.logical_shift_right, P.bit_length() - 1)):
                    x = ph.dve(lambda: v.tensor_scalar(whole[:, :, :], self.slot[:, :, :], by, None, op), *ph.free("whole"))
                    x = ph.dve(lambda: v.tensor_copy(out[:, :, :], whole[:, :, :]), x)
                    ph.release("whole", x)
                z = ph.dve(lambda: v.memset(is_p[0][:, :], 0.0))
                z = ph.dve(lambda: v.memset(at_a[0][:, :], 0.0), z)
                ph.pe(lambda: nc.tensor.matmul(table, is_p[0][:, :], at_a[0][:, :], start=True, stop=False, skip_group_check=True), z)
            with Phase(self, name, ROUNDS) as ph:
                at = ph.i * J
                y = ph.dve(lambda: v.tensor_copy(lo_j[:, :, :], lo[:, :, bass.ds(at, J)]), *ph.free("_j"))
                y = ph.dve(lambda: v.tensor_copy(hi_j[:, :, :], hi[:, :, bass.ds(at, J)]), *ph.free("_j"))
                y = ph.dve(lambda: v.tensor_copy(token_j[:, :], c("token")[:, bass.ds(at, J)]), *ph.free("_j"))
                for n in range(J * TOPK):
                    j, k, u = n // TOPK, n % TOPK, n % QUEUE
                    a = ph.dve(lambda: v.tensor_scalar(is_p[u][:, :], c("column"), lo_j[:, k, j:j + 1], None, ALU.is_equal), y, *ph.free(f"pair{u}"))
                    a = ph.dve(lambda: v.tensor_scalar(at_a[u][:, :], c("column")[:, 0:SLOTS // P], hi_j[:, k, j:j + 1], token_j[:, j:j + 1], ALU.is_equal, ALU.mult),
                               y, *ph.free(f"pair{u}"))
                    m = ph.pe(lambda: nc.tensor.matmul(table, is_p[u][:, :], at_a[u][:, :], start=False, stop=True, skip_group_check=True), a)
                    ph.release(f"pair{u}", m)
                ph.release("_j", a)
            with Phase(self, name + "_table") as ph:
                z = ph.dve(lambda: v.memset(self.source[:, :], 0))
                ph.dve(lambda: v.tensor_copy(self.source[:, 0:SLOTS // P], table), z)
                first.settle()

    def experts(self, name, eo):
        nc, U, W = self.nc, 2, 256
        CH, S = CAP // W, W // P
        LAST = U * CH
        v = nc.vector
        assert AHEAD == 2 * S and LAST % 2 == 0
        with ExitStack() as tmp:
            sb = lambda n, s: self.temp(tmp, n, s, F32)
            wg = [sb(f"wg{u}", [P, KD, F]) for u in range(U)]
            wu = [sb(f"wu{u}", [P, KD, F]) for u in range(U)]
            wd = [sb(f"wd{u}", [P, FB, D]) for u in range(U)]
            d = [sb(f"d{u}", [P, S, D]) for u in range(2)]
            dT = [sb(f"dT{u}", [P, KD, W]) for u in range(2)]
            act = [sb(f"act{u}", [P, FB, W]) for u in range(2)]
            th = [sb(f"th{u}", [P, 512]) for u in range(2)]
            eo_sb = [sb(f"eo{u}", [P, S, D]) for u in range(2)]
            at = self.temp(tmp, "from", [P, LAST * S + AHEAD], I32)

            def load(ph, dst, which, u, expert, rows):
                return ph.dma("sp", f"{which}{u}", lambda: nc.sync.dma_start(dst[u][:, :, :], self.rows(which, expert * rows, rows)), *ph.free(f"{which}{u}"))

            def first_weights(ph):
                load(ph, wg, "wg", 0, 0, D), load(ph, wu, "wu", 0, 0, D), load(ph, wd, "wd", 0, 0, F)

            def gather(ph, n, *steps):
                for s in range(S):
                    g = ph.dma("pool", f"d{n % 2}", lambda: nc.gpsimd.indirect_dma_start(
                        out=d[n % 2][:, s, :], out_offset=None, in_=self.dram["xn"][:, :],
                        in_offset=bass.IndirectOffsetOnAxis(ap=at[:, n * S + s:n * S + s + 1], axis=0)), *steps, *ph.free(f"d{n % 2}"))
                return g

            self.invert(name + "_invert", first_weights)
            with Phase(self, name + "_first") as ph:
                tokens = ph.pool(lambda: nc.gpsimd.tensor_copy(at[:, 0:AHEAD], self.source[:, 0:AHEAD]))
                gather(ph, 0, tokens), gather(ph, 1, tokens)
            with Phase(self, name, E // U) as ph:
                def down(n, acts):
                    u, par = n // CH, n % 2
                    bank = self.bank[:, 4 + par, :]
                    for s in range(S):
                        for f in range(FB):
                            m = ph.pe(lambda: nc.tensor.matmul(bank[:, s * D:(s + 1) * D], act[par][:, f, s * P:(s + 1) * P], wd[u][:, f, :],
                                                               start=f == 0, stop=f == FB - 1), acts[f // 2], *ph.free(f"down bank{par}"), *wd_here[u])
                    ph.release(f"act{par}", m)
                    if n % CH == CH - 1:
                        ph.release(f"wd{u}", m)
                    e = ph.act(lambda: nc.scalar.activation(eo_sb[par][:, :, :].rearrange("p s d -> p (s d)"), bank, ACT.Copy, scale=0.5),
                               m, *ph.free(f"eo{par}"))
                    ph.release(f"down bank{par}", e)
                    row = (ph.i * U + u) * CAP + n % CH * W
                    o = ph.dma("act", f"eo{par}", lambda: nc.scalar.dma_start(self.rows(eo, row, W), eo_sb[par][:, :, :]), e)
                    ph.release(f"eo{par}", o)

                second = ph.i * U + 1
                wg_here = [ph.free("wg0 loaded"), (load(ph, wg, "wg", 1, second, D),)]
                wu_here = [ph.free("wu0 loaded"), (load(ph, wu, "wu", 1, second, D),)]
                wd_here = [ph.free("wd0 loaded"), (load(ph, wd, "wd", 1, second, F),)]
                rows_here = {0: ph.free("rows 0 seen"), 1: ph.free("rows 1 seen")}
                tokens = ph.pool(lambda: nc.gpsimd.tensor_copy(at[:, :], self.source[:, bass.ds(ph.i * (U * CAP // P), LAST * S + AHEAD)]), *ph.free("from"))
                pending = None
                for n in range(LAST):
                    u, par = n // CH, n % 2
                    for s in range(S):
                        for k in range(KD):
                            t = ph.pe(lambda: nc.tensor.transpose(self.bank[:, 6 + par, k * W + s * P:k * W + (s + 1) * P], d[par][:, s, k * P:(k + 1) * P],
                                                                  self.c("ident")), *rows_here[n], *ph.free(f"dT bank{par}"))
                    ph.release(f"d{par}", t)
                    rows_here[n + 2] = (gather(ph, n + 2, tokens),)
                    tr = ph.dve(lambda: v.tensor_copy(dT[par][:, :, :].rearrange("p k w -> p (k w)"), self.bank[:, 6 + par, :]), t, *ph.free(f"dT{par}"))
                    ph.release(f"dT bank{par}", tr)
                    acts = []
                    for r in range(FB // 2):
                        if r == 1 and pending:
                            down(*pending)
                        q = r % 2
                        gb, ub = self.bank[:, q, :], self.bank[:, 2 + q, :]
                        done = {}
                        for which, bank, wt, here in (("g", gb, wg, wg_here), ("u", ub, wu, wu_here)):
                            for f in range(2):
                                for k in range(KD):
                                    fb = 2 * r + f
                                    m = ph.pe(lambda: nc.tensor.matmul(bank[:, f * W:(f + 1) * W], wt[u][:, k, fb * P:(fb + 1) * P], dT[par][:, k, :],
                                                                       start=k == 0, stop=k == KD - 1),
                                              tr, *here[u], *ph.free(f"{which} bank{q}"))
                            done[which] = m
                        out = act[par][:, 2 * r:2 * r + 2, :].rearrange("p f w -> p (f w)")
                        h = ph.act(lambda: nc.scalar.activation(th[q][:, :], gb, ACT.Tanh, scale=0.5), done["g"], *ph.free(f"th{q}"))
                        a = ph.dve(lambda: v.scalar_tensor_tensor(th[q][:, :], th[q][:, :], 1.0, gb, ALU.add, ALU.mult), h)
                        b = ph.dve(lambda: v.tensor_tensor(out, th[q][:, :], ub, ALU.mult), a, done["u"], *ph.free(f"act{par}"))
                        ph.release(f"g bank{q}", a)
                        ph.release(f"u bank{q}", b)
                        ph.release(f"th{q}", b)
                        acts.append(b)
                    ph.release(f"dT{par}", m)
                    if n % CH == CH - 1:
                        ph.release(f"wg{u}", m)
                        ph.release(f"wu{u}", m)
                    if n == CH:
                        after = (ph.i * U + U) % E
                        ph.release("wg0 loaded", load(ph, wg, "wg", 0, after, D))
                        ph.release("wu0 loaded", load(ph, wu, "wu", 0, after, D))
                        ph.release("wd0 loaded", load(ph, wd, "wd", 0, after, F))
                    pending = (n, acts)
                down(*pending)
                for n in range(2):
                    seen = ph.relay("sp", *rows_here[LAST + n])
                    ph.release(f"rows {n} seen", seen)
                ph.release("from", seen)

    def combine(self, ph, x, e, w, steps, out):
        v = self.nc.vector
        a = ph.dve(lambda: v.tensor_scalar(e[0], e[0], w[0], None, ALU.mult), *steps)
        a = ph.dve(lambda: v.scalar_tensor_tensor(e[0], e[1], w[1], e[0], ALU.mult, ALU.add), a)
        return ph.dve(lambda: v.scalar_tensor_tensor(out, e[0], RES, x, ALU.mult, ALU.add), a)

    def finish(self, eo):
        nc, G, U = self.nc, 2, 4
        with ExitStack() as tmp:
            sb = lambda n, s, d=F32: self.temp(tmp, n, s, d)
            x = [sb(f"fx{u}", [P, D]) for u in range(G * U)]
            e = [[sb(f"fe{u}{k}", [P, D]) for k in range(TOPK)] for u in range(G * U)]
            y = [sb(f"fy{u}", [P, D]) for u in range(G * U)]
            at = [sb(f"fat{g}", [P, TOPK, U], I32) for g in range(G)]
            wt = [sb(f"fwt{g}", [P, TOPK, U]) for g in range(G)]
            with Phase(self, "finish", TILES // (G * U)) as ph:
                for n in range(G * U):
                    g, u = n // U, n % U
                    tile = ph.i * (G * U) + n
                    if u == 0:
                        a = ph.pool(lambda: nc.gpsimd.tensor_copy(at[g][:, :, :], self.fetch[:, :, bass.ds(tile, U)]), *ph.free(f"group{g}"))
                        w = ph.pool(lambda: nc.gpsimd.tensor_copy(wt[g][:, :, :], self.weight[:, :, bass.ds(tile, U)]), *ph.free(f"group{g}"))
                    xs = ph.dma("sp", f"x{n}", lambda: nc.sync.dma_start(x[n][:, :], self.dram["x2"][bass.ds(tile * P, P), :]), *ph.free(f"used{n}"))
                    got = [ph.dma("pool", f"e{n}", lambda: nc.gpsimd.indirect_dma_start(
                        out=e[n][k][:, :], out_offset=None, in_=self.dram[eo][:, :],
                        in_offset=bass.IndirectOffsetOnAxis(ap=at[g][:, k, u:u + 1], axis=0)), a, *ph.free(f"used{n}")) for k in range(TOPK)]
                    o = self.combine(ph, x[n][:, :], (e[n][0][:, :], e[n][1][:, :]), (wt[g][:, 0, u:u + 1], wt[g][:, 1, u:u + 1]),
                                     (xs, *got, w, *ph.free(f"y{n}")), y[n][:, :])
                    ph.release(f"used{n}", o)
                    ph.release(f"group{g}", o)
                    s = ph.dma("act", f"y{n}", lambda: nc.scalar.dma_start(self.dram["out"][bass.ds(tile * P, P), :], y[n][:, :]), o)
                    ph.release(f"y{n}", s)

    def attention(self, eo):
        nc, v, g_, sc = self.nc, self.nc.vector, self.nc.gpsimd, self.nc.scalar
        c, bank = self.c, self.bank
        with ExitStack() as tmp:
            sb = lambda n, s, d=F32: self.temp(tmp, n, s, d)
            two = lambda n, s, d=F32: [sb(f"{n}{q}", s, d) for q in range(2)] * 2
            four = lambda n, s, d=F32: [sb(f"{n}{q}", s, d) for q in range(B)]
            one = lambda n, s, d=F32: [sb(n, s, d)] * B
            x_in, e0, e1 = (two(n, [P, D]) for n in ("x_in", "e0", "e1"))
            at, wt = two("at", [P, TOPK], I32), two("wt", [P, TOPK])
            x1, xa, gg = four("x1", [P, D]), four("xa", [P, D]), four("gg", [P, H, HD])
            nw, vb, kc = (four(n, [P, H, HD]) for n in ("nw", "vb", "kc"))
            gamma, qgT = four("gamma", [P, 3 * H]), four("qgT", [P, 2, P])
            st, mv, small, junk, th = ({z: sb(n + z, s) for z in "fbr"} for n, s in
                                       (("st", [P, 6]), ("mv", [P, 2]), ("small", [P, 4]), ("junk", [P, D]), ("th", [P, 512])))
            h, hT, sq = one("h", [P, D]), one("hT", [P, KD, P]), one("sq", [P, 512])
            qk, vg = one("qk", [P, 2 * H, HD]), one("vg", [P, 2 * H, HD])
            tiny, ba = one("tiny", [P, 10, H]), one("ba", [P, 2 * H])
            rq, ro = one("rq", [P, 2 * H]), one("ro", [P, H])
            gv, gx, dc = one("gv", [P, H, HD]), one("gx", [P, H, HD]), one("dc", [P, H, HD])
            kb, qg = one("kb", [P, H, HD]), one("qg", [P, H, HD])
            dm, bq, kT = two("dm", [P, H, P]), two("bq", [P, HG, 2, 2 * P]), two("kT", [P, 2, P])
            NT, X, R = one("NT", [P, H, P]), one("X", [P, H, P]), one("R", [P, H, P])
            Y, Bt, WT = two("Y", [P, H, P]), two("Bt", [P, H, P]), one("WT", [P, 2, P])
            us, sm, os_, og, ogT = one("us", [P, H * HD]), one("sm", [P, 2, P]), one("os", [P, D]), one("og", [P, D]), one("ogT", [P, KD, P])
            x1a, h2, h2T, aT = one("x1a", [P, D]), one("h2", [P, D]), one("h2T", [P, KD, P]), one("aT", [P, FB, P])
            x2, xn2, xn2T = two("x2", [P, D]), two("xn2", [P, D]), one("xn2T", [P, KD, P])
            S = [sb(f"S{b}", [P, 2, P]) for b in range(B)]
            flat = lambda t: t[:, :, :].rearrange("p a b -> p (a b)")
            over_hd = lambda t: t.unsqueeze(2).to_broadcast([P, t.shape[1], HD])
            per4 = lambda m: m.unsqueeze(1).to_broadcast([P, HG, P])

            def stages(ph):

                row = lambda n: (ph.i + n // B) * P + n % B * T
                tile = lambda n: (ph.i + n // B) + n % B * (T // P)

                def norm(x, out, z, steps, free):
                    s = ph.dve(lambda: v.bn_stats(st[z][:, :], x), *steps, *ph.free(f"st{z}"))
                    s = ph.dve(lambda: v.bn_aggr(mv[z][:, :], st[z][:, :]), s, *ph.free(f"mv{z}"), plain=True)
                    ph.release(f"st{z}", s)
                    r = self.rsqrt(ph, small[z][:, 0:1], mv[z][:, 1:2], 1.0, 1e-5, s, *ph.free(f"small0{z}"))
                    n = ph.dve(lambda: v.tensor_scalar(out, x, mv[z][:, 0:1], small[z][:, 0:1], ALU.subtract, ALU.mult), r, *free)
                    ph.release(f"mv{z}", n)
                    ph.release(f"small0{z}", n)
                    return n

                def rms(x, out, z, steps, free):
                    a = ph.act(lambda: sc.activation(junk[z][:, :], x, ACT.Square, accum_out=small[z][:, 1:2]), *steps, *ph.free(f"junk{z}"), *ph.free(f"small1{z}"))
                    ph.release(f"junk{z}", a)
                    r = self.rsqrt(ph, small[z][:, 1:2], small[z][:, 1:2], 1.0 / D, 1e-6, a)
                    n = ph.dve(lambda: v.tensor_scalar(out, x, small[z][:, 1:2], None, ALU.mult), r, *free)
                    ph.release(f"small1{z}", n)
                    return n

                def transpose(x, out, no, name, steps, scale=None):
                    for k in range(KD):
                        t = ph.pe(lambda: nc.tensor.transpose(bank[:, no, k * P:(k + 1) * P], x[:, k * P:(k + 1) * P], c("ident")), *steps, *ph.free(f"bank{no}"))
                    if scale is None:
                        e = ph.act(lambda: sc.activation(flat(out), bank[:, no, 0:KD * P], ACT.Copy), t, *ph.free(name))
                    else:
                        for k in range(KD):
                            e = ph.act(lambda: sc.activation(out[:, k, :], bank[:, no, k * P:(k + 1) * P], ACT.Copy, scale=scale[:, k:k + 1]), t, *ph.free(name))
                    ph.release(f"bank{no}", e)
                    return t, e

                def fetch(n):
                    b, q = n % B, n % 2
                    ia = ph.pool(lambda: g_.tensor_copy(at[q][:, :], self.fetch[:, :, bass.ds(tile(n), 1)].rearrange("p k t -> p (k t)")), *ph.free(f"fetched{q}"))
                    iw = ph.pool(lambda: g_.tensor_copy(wt[q][:, :], self.weight[:, :, bass.ds(tile(n), 1)].rearrange("p k t -> p (k t)")), *ph.free(f"fetched{q}"))
                    xs = ph.dma("sp", f"x{q}", lambda: nc.sync.dma_start(x_in[q][:, :], self.dram["x"][bass.ds(row(n), P), :]), *ph.free(f"fetched{q}"))
                    for k, e in enumerate((e0[q], e1[q])):
                        got = ph.dma("pool", f"e{q}", lambda: g_.indirect_dma_start(
                            out=e[:, :], out_offset=None, in_=self.dram[eo][:, :],
                            in_offset=bass.IndirectOffsetOnAxis(ap=at[q][:, k:k + 1], axis=0)), ia, *ph.free(f"fetched{q}"))
                    yield 2153.65
                    ph.release(f"fetch{b}", iw, ph.relay("sp", xs, got))

                def front(n):
                    b, q = n % B, n % 2
                    x = self.combine(ph, x_in[q][:, :], (e0[q][:, :], e1[q][:, :]), (wt[q][:, 0:1], wt[q][:, 1:2]),
                                     (*ph.free(f"fetch{b}"), *ph.free(f"x1{b}")), x1[b][:, :])
                    ph.release(f"fetched{q}", x)
                    yield 1.96
                    a = norm(x1[b][:, :], xa[b][:, :], "f", (x,), ph.free(f"xa{b}"))
                    yield 1.41
                    a = rms(xa[b][:, :], h[b][:, :], "f", (a,), ph.free("h"))
                    yield 0.5
                    t, e = transpose(h[b], hT[b], 2, "hT", (a,), self.ln1)
                    ph.release("h", t)
                    yield 0.67
                    for k in range(KD):
                        m = ph.pe(lambda: nc.tensor.matmul(bank[:, 2, 0:2 * H], hT[b][:, k, :], self.w_ba[:, k, :], start=k == 0, stop=k == KD - 1),
                                  e, *ph.free("bank2"))
                    copied = ph.dve(lambda: v.tensor_copy(ba[b][:, :], bank[:, 2, 0:2 * H]), m, *ph.free("tiny"))
                    ph.release("bank2", copied)
                    yield 0.76
                    silu = []
                    for w, no, out, name in ((self.w_qk, 3, qk[b], "qk"), (self.w_vg, 2, vg[b], "vg")):
                        for k in range(KD):
                            m = ph.pe(lambda: nc.tensor.matmul(bank[:, no, :], hT[b][:, k, :], w[:, k, :], start=k == 0, stop=k == KD - 1),
                                      e, *ph.free(f"bank{no}"))
                        a = ph.act(lambda: sc.activation(th["f"][:, :], bank[:, no, :], ACT.Tanh, scale=0.5), m, *ph.free("thf"))
                        a = ph.dve(lambda: v.scalar_tensor_tensor(flat(out), th["f"][:, :], 1.0, bank[:, no, :], ALU.add, ALU.mult), a, *ph.free(name))
                        ph.release("thf", a)
                        ph.release(f"bank{no}", a)
                        silu.append(a)
                        yield 1.24
                    ph.release("hT", m)
                    y_, z_, s_, w_, p_, g, beta, half_beta, ng = (tiny[b][:, k, :] for k in range(9))
                    d = ph.dve
                    tb = ph.act(lambda: sc.activation(beta, ba[b][:, 0:H], ACT.Tanh, scale=0.5), copied)
                    x = d(lambda: v.tensor_tensor(y_, ba[b][:, H:], self.dt_bias[:, :], ALU.add), copied)
                    x = d(lambda: v.scalar_tensor_tensor(z_, y_, -1.0, y_, ALU.mult, ALU.min), x)
                    z = ph.act(lambda: sc.activation(z_, z_, ACT.Exp), x)
                    yield 1.3
                    x = d(lambda: v.tensor_scalar(s_, z_, 2.0, None, ALU.add), z)
                    x = d(lambda: v.reciprocal(s_, s_), x)
                    x = d(lambda: v.tensor_tensor(s_, s_, z_, ALU.mult), x)
                    x = d(lambda: v.tensor_tensor(w_, s_, s_, ALU.mult), x)
                    x = d(lambda: v.tensor_scalar(p_, w_, 1.0 / 17, None, ALU.mult), x)
                    yield 2.63
                    for k in range(15, 1, -2):
                        x = d(lambda: v.scalar_tensor_tensor(p_, p_, 1.0 / k, w_, ALU.add, ALU.mult), x)
                        if k == 9:
                            yield 0.05
                    yield 1.79
                    x = d(lambda: v.scalar_tensor_tensor(p_, p_, 1.0, s_, ALU.add, ALU.mult), x)
                    x = d(lambda: v.tensor_scalar(y_, y_, 0.0, None, ALU.max), x)
                    x = d(lambda: v.scalar_tensor_tensor(p_, p_, 2.0, y_, ALU.mult, ALU.add), x)
                    x = d(lambda: v.tensor_tensor(g, p_, self.decay[:, :], ALU.mult), x)
                    gs = d(lambda: v.tensor_scalar(g, g, G_LEAST, None, ALU.max), x)
                    x = d(lambda: v.tensor_scalar(beta, beta, 0.5, 0.5, ALU.mult, ALU.add), tb)
                    bs = d(lambda: v.tensor_scalar(half_beta, beta, 0.5, None, ALU.mult), x)
                    pv = ph.pool(lambda: g_.tensor_tensor(gv[b][:, :, :], over_hd(g), c("within").unsqueeze(1).to_broadcast([P, H, HD]), ALU.mult), gs, *ph.free("gv"))
                    px = ph.pool(lambda: g_.tensor_copy(gx[b][:, :, :], over_hd(g)), gs, *ph.free("gx"))
                    yield 0.6
                    a = ph.act(lambda: sc.activation(sq[b][:, :], flat(qk[b]), ACT.Square), silu[0], *ph.free("sq"))
                    a = ph.dve(lambda: v.tensor_reduce(rq[b][:, :], sq[b][:, :].rearrange("p (h k) -> p h k", k=HD), AX.X, ALU.add), a, *ph.free("rq"))
                    ph.release("sq", a)
                    a = self.rsqrt(ph, rq[b][:, :], rq[b][:, :], 1.0, 4e-6, a)
                    yield 8.46
                    qkn = ph.dve(lambda: v.tensor_tensor(qk[b][:, :, :], qk[b][:, :, :], over_hd(rq[b][:, :]), ALU.mult), a)
                    ph.release("rq", qkn)
                    sums = bank[:, 3, 16:16 + 3 * H]
                    ph.pe(lambda: nc.tensor.matmul(sums[:, 0:H], c("upto"), g, start=True, stop=True), gs, *ph.free("bank3"))
                    ph.pe(lambda: nc.tensor.matmul(sums[:, H:2 * H], c("after"), g, start=True, stop=True), gs)
                    for k in range(2):
                        m = ph.pe(lambda: nc.tensor.matmul(sums[:, 2 * H + NC * k:2 * H + NC * (k + 1)], gx[b][:, HG * k:HG * (k + 1), :].rearrange("p a b -> p (a b)"),
                                                           c("chunk"), start=True, stop=True), px)
                    ms = ph.pe(lambda: nc.tensor.matmul(bank[:, 3, 128:128 + H * HD], c("after"), flat(gv[b]), start=True, stop=True), pv)
                    ph.release("gv", ms)
                    ph.release("gx", ms)
                    ga = ph.act(lambda: sc.activation(gamma[b][:, :], sums, ACT.Exp), ms, *ph.free(f"gamma{b}"))
                    gd = ph.act(lambda: sc.activation(flat(dc[b]), bank[:, 3, 128:128 + H * HD], ACT.Exp), ms, *ph.free("dc"))
                    ph.release("bank3", gd)
                    yield 0.52
                    dms = ph.pool(lambda: g_.tensor_tensor(dm[b][:, :, :].rearrange("p h (c i) -> p h c i", c=NC),
                                                           dc[b][:, :, :].unsqueeze(2).to_broadcast([P, H, NC, HD]),
                                                           c("causal").rearrange("p (c i) -> p c i", c=NC).unsqueeze(1).to_broadcast([P, H, NC, HD]), ALU.mult),
                                  gd, *ph.free(f"dm{q}"))
                    ph.release("dc", dms)
                    qn, kn, vv, gate = qk[b][:, 0:H, :], qk[b][:, H:, :], vg[b][:, 0:H, :], vg[b][:, H:, :]
                    down, up = gamma[b][:, 0:H], gamma[b][:, H:2 * H]
                    on = {"pool": (ph.pool, g_), "dve": (ph.dve, v)}
                    times = lambda engine, out, x, y, *s: on[engine][0](lambda: on[engine][1].tensor_tensor(out[:, :, :], x, over_hd(y), ALU.mult), *s)
                    skb = times("dve", kb[b], kn, beta, qkn, bs, *ph.free("kb"))
                    sqg = times("dve", qg[b], qn, down, qkn, ga, *ph.free("qg"))
                    yield 17.95
                    x = ph.dve(lambda: v.tensor_scalar(ng, down, -1.0, None, ALU.mult), ga)
                    snw = times("dve", nw[b], kb[b][:, :, :], ng, skb, x, *ph.free(f"nw{b}"))
                    skc = times("pool", kc[b], kn, up, qkn, ga, *ph.free(f"kc{b}"))
                    svb = times("pool", vb[b], vv, half_beta, silu[1], bs, *ph.free(f"vb{b}"))
                    ph.release("tiny", snw, ms, svb)
                    sgg = ph.pool(lambda: g_.tensor_tensor(gg[b][:, :, :], gate, self.onorm[:, :].unsqueeze(1).to_broadcast([P, H, HD]), ALU.mult), silu[1], *ph.free(f"gg{b}"))
                    ph.release("vg", sgg, svb)
                    yield 63.29
                    f2 = lambda t: t.rearrange("p h k -> p (h k)")
                    for k in range(2):
                        for m_, src in ((0, f2(kb[b][:, :, :])), (1, f2(qn))):
                            t0 = ph.pe(lambda: nc.tensor.transpose(bank[:, 2, (2 * k + m_) * P:(2 * k + m_ + 1) * P], src[:, k * P:(k + 1) * P], c("ident")),
                                       skb, qkn, *ph.free("bank2"))
                    for r in range(HG):
                        mine = slice(HD * r, HD * (r + 1))
                        x0 = ph.act(lambda: sc.activation(bq[b][mine, r, :, :].rearrange("p k t -> p (k t)"), bank[mine, 2, :], ACT.Copy), t0, *ph.free(f"bq{q}"))
                    ph.release("bank2", x0)
                    for k in range(2):
                        for m_, src in ((0, f2(kn)), (1, f2(qg[b][:, :, :]))):
                            t1 = ph.pe(lambda: nc.tensor.transpose(bank[:, 3, (2 * m_ + k) * P:(2 * m_ + k + 1) * P], src[:, k * P:(k + 1) * P], c("ident")),
                                       sqg, *ph.free("bank3"))
                    ph.release("kb", t0, snw)
                    ph.release("qg", t1)
                    ph.release("qk", t1, skc)
                    y1 = ph.dve(lambda: v.tensor_copy(flat(kT[b]), bank[:, 3, 0:2 * P]), t1, *ph.free(f"kT{q}"))
                    y2 = ph.dve(lambda: v.tensor_copy(flat(qgT[b]), bank[:, 3, 2 * P:4 * P]), t1, *ph.free(f"qgT{b}"))
                    ph.release("bank3", y2)
                    ph.release(f"front{b}", x0, y2, dms, snw, svb, skc, sgg, ga)
                    yield 1548.23

                def solve(n):
                    b, q = n % B, n % 2
                    ready_in = ph.free(f"front{b}")
                    nt = {}
                    for k in range(2):
                        for r in range(HG):
                            gm = ph.pe(lambda: nc.tensor.matmul(bank[:, 2 * k + r // 2, r % 2 * 2 * P:(r % 2 + 1) * 2 * P], kT[b][:, k, :],
                                                                bq[b][:, r, k, :], start=True, stop=True),
                                       *ready_in, *ph.free(f"bank{2 * k + r // 2}"))
                        heads = slice(HG * k, HG * (k + 1))
                        gram = bank[:, 2 * k:2 * k + 2, :].rearrange("p n (r a t) -> p a (n r) t", r=2, a=2)
                        nt[k] = ph.dve(lambda: v.scalar_tensor_tensor(NT[b][:, heads, :], gram[:, 0, :, :], -1.0, dm[b][:, heads, :],
                                                                      ALU.mult, ALU.mult), gm, *ready_in, *ph.free("NT"))
                        bt = ph.dve(lambda: v.tensor_tensor(Bt[b][:, heads, :], gram[:, 1, :, :], dm[b][:, heads, :], ALU.mult),
                                    gm, *ready_in, *ph.free(f"Bt{q}"))
                        ph.release(f"bank{2 * k}", bt)
                        ph.release(f"bank{2 * k + 1}", bt)
                        yield 2.56
                    ph.release(f"bq{q}", gm)
                    ph.release(f"kT{q}", gm)
                    ph.release(f"dm{q}", bt)
                    ready = {}
                    for k in range(2):
                        heads = slice(HG * k, HG * (k + 1))
                        y = ph.pool(lambda: g_.tensor_copy(Y[b][:, heads, :], per4(c("ident"))), *ph.free(f"Y{q}"))
                        ready[k] = ph.dve(lambda: v.copy_predicated(Y[b][:, heads, :], per4(self.level[:, 0, :]), NT[b][:, heads, :]), y, nt[k], plain=True)
                    yield 1.18
                    f3 = lambda t: t.rearrange("p h k -> p (h k)")
                    got = {}
                    for s in range(1, LEVELS):
                        for k in range(2):
                            for r in range(HG):
                                t = ph.pe(lambda: nc.tensor.transpose(bank[:, k, r * P:(r + 1) * P], Y[b][:, HG * k + r, :], c("ident")), ready[k], *ph.free(f"bank{k}"))
                            got[k] = ph.act(lambda: sc.activation(f3(X[b][:, HG * k:HG * (k + 1), :]), bank[:, k, :], ACT.Copy), t, *ph.free(f"X{k}"))
                            yield 0.83
                        for k in range(2):
                            for r in range(HG):
                                m = ph.pe(lambda: nc.tensor.matmul(bank[:, k, r * P:(r + 1) * P], NT[b][:, HG * k + r, :], X[b][:, HG * k + r, :], start=True, stop=True), got[k])
                            ph.release(f"X{k}", m)
                            got[k] = ph.act(lambda: sc.activation(f3(R[b][:, HG * k:HG * (k + 1), :]), bank[:, k, :], ACT.Copy), m, *ph.free(f"R{k}"))
                            yield 1.24
                        for k in range(2):
                            for r in range(HG):
                                m = ph.pe(lambda: nc.tensor.matmul(bank[:, k, r * P:(r + 1) * P], R[b][:, HG * k + r, :], Y[b][:, HG * k + r, :], start=True, stop=True), got[k])
                            ph.release(f"R{k}", m)
                            ready[k] = ph.dve(lambda: v.copy_predicated(Y[b][:, HG * k:HG * (k + 1), :], per4(self.level[:, s, :]),
                                                                        bank[:, k, :].rearrange("p (r t) -> p r t", r=HG)), m, plain=True)
                            ph.release(f"bank{k}", ready[k])
                            yield 0.45
                    ph.release("NT", m)
                    ph.release(f"solve{b}", ready[1], bt)

                def back(n):
                    b, q = n % B, n % 2
                    got = (*ph.free(f"front{b}"), *ph.free(f"solve{b}"))
                    for k in range(2):
                        for r in range(HG):
                            m = ph.pe(lambda: nc.tensor.matmul(bank[HD * r:HD * (r + 1), 4, k * P:(k + 1) * P], nw[b][:, HG * k + r, :], Y[b][:, HG * k + r, :], start=True, stop=True),
                                      *got, *ph.free("bank4"))
                    ph.release(f"nw{b}", m)
                    w = ph.act(lambda: sc.activation(flat(WT[b]), bank[:, 4, 0:2 * P], ACT.Copy), m, *ph.free("WT"))
                    ph.release("bank4", w)
                    yield 1.68
                    for hd in range(H):
                        m = ph.pe(lambda: nc.tensor.matmul(bank[:, 5, hd * HD:(hd + 1) * HD], Y[b][:, hd, :], vb[b][:, hd, :], start=hd == 0, stop=False, skip_group_check=True),
                                  *got, *ph.free("bank5"))
                    ph.release(f"vb{b}", m)
                    ph.release(f"Y{q}", m)
                    yield 0.25
                    prev = ph.free(f"S{b}")
                    for ch in range(NC):
                        part = slice(C * ch, C * (ch + 1))
                        for k in range(2):
                            mu = ph.pe(lambda: nc.tensor.matmul(bank[part, 5, k * P:(k + 1) * P], WT[b][:, k, part], S[b][:, k, :], start=False, stop=True, skip_group_check=True),
                                       w, *prev)
                        u = ph.act(lambda: sc.activation(us[b][part, :], bank[part, 5, 0:D], ACT.Copy), mu, *ph.free("us"))
                        for k in range(2):
                            mo = ph.pe(lambda: nc.tensor.matmul(bank[part, 7, k * P:(k + 1) * P], qgT[b][:, k, part], S[b][:, k, :], start=k == 0, stop=False, skip_group_check=True),
                                       *prev, *ph.free("bank7"))
                        yield 1.6
                        for k in range(2):
                            ms = ph.pe(lambda: nc.tensor.matmul(bank[:, 6, k * P:(k + 1) * P], kc[b][part, HG * k:HG * (k + 1), :].rearrange("p a b -> p (a b)"),
                                                                us[b][part, k * P:(k + 1) * P], start=True, stop=True), u, *ph.free("bank6"))
                        x = ph.dve(lambda: v.tensor_tensor(sm[b][:, :, :], bank[:, 6, 0:2 * P].rearrange("p (n t) -> p n t", n=2),
                                                           c("diag").unsqueeze(1).to_broadcast([P, 2, P]), ALU.mult), ms, *ph.free("sm"))
                        ph.release("bank6", x)
                        for k in range(2):
                            x = ph.dve(lambda: v.scalar_tensor_tensor(S[b][:, k, :], S[b][:, k, :], gamma[b][:, 2 * H + NC * k + ch:2 * H + NC * k + ch + 1],
                                                                      sm[b][:, k, :], ALU.mult, ALU.add), x, mo)
                        ph.release("sm", x)
                        prev = (x,)
                        yield 2.73
                    ph.release(f"S{b}", x)
                    ph.release(f"kc{b}", ms)
                    ph.release("WT", mu)
                    ph.release(f"qgT{b}", mo)
                    ph.release(f"gamma{b}", x)
                    ph.release("bank5", u)
                    for hd in range(H):
                        m = ph.pe(lambda: nc.tensor.matmul(bank[:, 7, hd * HD:(hd + 1) * HD], Bt[b][:, hd, :], us[b][:, hd * HD:(hd + 1) * HD], start=False, stop=True,
                                                           skip_group_check=True), u)
                    ph.release("us", m)
                    ph.release(f"Bt{q}", m)
                    o = bank[:, 7, 0:D]
                    a = ph.act(lambda: sc.activation(os_[b][:, :], o, ACT.Square), m, *ph.free("os"))
                    a = ph.dve(lambda: v.tensor_reduce(ro[b][:, :], os_[b][:, :].rearrange("p (h k) -> p h k", k=HD), AX.X, ALU.add), a, *ph.free("ro"))
                    ph.release("os", a)
                    a = self.rsqrt(ph, ro[b][:, :], ro[b][:, :], 1.0 / HD, 1e-6, a)
                    yield 2.29
                    o3 = og[b][:, :].rearrange("p (h k) -> p h k", k=HD)
                    a = ph.dve(lambda: v.tensor_tensor(o3, o.rearrange("p (h k) -> p h k", k=HD), over_hd(ro[b][:, :]), ALU.mult), a, *ph.free("og"))
                    ph.release("bank7", a)
                    ph.release("ro", a)
                    a = ph.dve(lambda: v.tensor_tensor(o3, o3, gg[b][:, :, :], ALU.mult), a)
                    ph.release(f"gg{b}", a)
                    t, e = transpose(og[b], ogT[b], 4, "ogT", (a,))
                    ph.release("og", t)
                    yield 1.1
                    for k in range(KD):
                        m = ph.pe(lambda: nc.tensor.matmul(bank[:, 5, 0:D], ogT[b][:, k, :], self.w_o[:, k, :], start=k == 0, stop=k == KD - 1), e, *ph.free("bank5"))
                    ph.release("ogT", m)
                    a = ph.dve(lambda: v.scalar_tensor_tensor(x1a[b][:, :], bank[:, 5, 0:D], RES * 0.5, xa[b][:, :], ALU.mult, ALU.add), m, *ph.free("x1a"))
                    ph.release("bank5", a)
                    ph.release(f"xa{b}", a)
                    yield 0.05
                    a = rms(x1a[b][:, :], h2[b][:, :], "b", (a,), ph.free("h2"))
                    yield 2.93
                    t, e = transpose(h2[b], h2T[b], 4, "h2T", (a,), self.ln2)
                    ph.release("h2", t)
                    yield 17.0
                    acts = []
                    for k2 in range(2):
                        for f in range(4):
                            for k in range(KD):
                                fb = 4 * k2 + f
                                m = ph.pe(lambda: nc.tensor.matmul(bank[:, 6 + k2, f * P:(f + 1) * P], self.w_fc[:, k, fb * P:(fb + 1) * P], h2T[b][:, k, :],
                                                                   start=k == 0, stop=k == KD - 1), e, *ph.free(f"bank{6 + k2}"))
                        a = ph.act(lambda: sc.activation(th["b"][:, :], bank[:, 6 + k2, :], ACT.Tanh, scale=0.5), m, *ph.free("thb"))
                        a = ph.dve(lambda: v.scalar_tensor_tensor(aT[b][:, 4 * k2:4 * k2 + 4, :].rearrange("p f t -> p (f t)"), th["b"][:, :], 1.0, bank[:, 6 + k2, :],
                                                                  ALU.add, ALU.mult), a, *ph.free("aT"))
                        ph.release("thb", a)
                        ph.release(f"bank{6 + k2}", a)
                        acts.append(a)
                        yield 377.86
                    ph.release("h2T", m)
                    for f in range(FB):
                        m = ph.pe(lambda: nc.tensor.matmul(bank[:, 5, 0:D], aT[b][:, f, :], self.w_p[:, f, :], start=f == 0, stop=f == FB - 1), acts[f // 4], *ph.free("bank5"))
                        if f == FB // 2 - 1:
                            yield 7.52
                    ph.release("aT", m)
                    a = ph.dve(lambda: v.scalar_tensor_tensor(x2[b][:, :], bank[:, 5, 0:D], RES * 0.5, x1a[b][:, :], ALU.mult, ALU.add), m,
                               *ph.free(f"x2 read{q}"), *ph.free(f"x2 kept{q}"))
                    ph.release("bank5", a)
                    ph.release("x1a", a)
                    a = ph.dve(lambda: v.tensor_tensor(x2[b][:, :], x2[b][:, :], x1[b][:, :], ALU.add), a)
                    ph.release(f"x1{b}", a)
                    kept = ph.dma("sp", f"x2{q}", lambda: nc.sync.dma_start(self.dram["x2"][bass.ds(row(n), P), :], x2[b][:, :]), a)
                    ph.release(f"to route{q}", a)
                    ph.release(f"x2 kept{q}", kept)
                    yield 1.02

                def route(n):
                    b, q = n % B, n % 2
                    a = norm(x2[b][:, :], xn2[b][:, :], "r", ph.free(f"to route{q}"), ph.free(f"xn2{q}"))
                    ph.release(f"x2 read{q}", a)
                    kept = ph.dma("sp", f"xn2{q}", lambda: nc.sync.dma_start(self.dram["xn"][bass.ds(row(n), P), :], xn2[b][:, :]), a)
                    yield 1.55
                    t, e = transpose(xn2[b], xn2T[b], 6, "xn2T", (a,))
                    ph.release(f"xn2{q}", kept, t)
                    yield 2.01
                    for k in range(KD):
                        m = ph.pe(lambda: nc.tensor.matmul(bank[:, 6, KD * P:KD * P + E], xn2T[b][:, k, :], self.router[:, k, :], start=k == 0, stop=k == KD - 1), e, *ph.free("bank6"))
                    ph.release("xn2T", m)
                    a = ph.dve(lambda: v.tensor_copy(self.logits[:, :, bass.ds(tile(n), 1)].rearrange("p e t -> p (e t)"), bank[:, 6, KD * P:KD * P + E]), m)
                    ph.release("bank6", a)
                    yield 42.81

                return fetch, front, solve, back, route

            def together(*streams):
                live = [[0.0, k, s] for k, s in enumerate(streams)]
                while live:
                    one_ = min(live, key=lambda t: t[:2])
                    cost = next(one_[2], None)
                    if cost is None:
                        live.remove(one_)
                    else:
                        one_[0] += cost

            with Phase(self, "attention_first") as ph:
                fetch, front, solve, back, route = stages(ph)
                for t in (*(flat(s) for s in S), x2[0][:, :], x2[1][:, :], *(bq[q][:, :, :, :].rearrange("p r k t -> p (r k t)") for q in range(2))):
                    z = ph.dve(lambda: v.memset(t, 0.0))
                for q in range(2):
                    ph.release(f"bq{q}", z)
                together(fetch(0))
                together(fetch(1), front(0))
                together(fetch(2), front(1), solve(0))
            with Phase(self, "attention", T // P) as ph:
                fetch, front, solve, back, route = stages(ph)
                for b in range(B):
                    together(route(b - 1), back(b), solve(b + 1), front(b + 2), fetch(b + 3))
            with Phase(self, "attention_last") as ph:
                together(stages(ph)[-1](TILES - 1))

    def build(self):
        self.start()
        self.route_first()
        self.choose("choose1", self.load_block)
        self.experts("experts1", "eo")
        self.attention("eo")
        self.choose("choose2")
        self.experts("experts2", "eo2")
        self.finish("eo2")


DRAM_IN = {
    "x": (N, D), "ln1_w": (D,), "qw": (D, D), "kw": (D, D), "vw": (D, D), "bw": (D, H), "aw": (D, H), "A_log": (H,), "dt_bias": (H,),
    "gw": (D, D), "onorm_w": (HD,), "ow": (D, D), "ln2_w": (D,), "fcw": (D, F), "pw": (F, D),
    "router_t": (D, E), "wg": (E * D, F), "wu": (E * D, F), "wd": (E * F, D),
}
SCRATCH = {"xn": (N, D), "eo": (SLOTS, D), "eo2": (SLOTS, D), "x2": (N, D)}


def build(nc, book, parts=None):
    const, _, level = constants()
    dram = {n: nc.dram_tensor(f"in_{n}", s, F32, kind="ExternalInput").ap() for n, s in DRAM_IN.items()}
    dram["const"] = nc.dram_tensor("in_const", const.shape, F32, kind="ExternalInput").ap()
    dram["level"] = nc.dram_tensor("in_level", level.shape, I32, kind="ExternalInput").ap()
    for n, s in SCRATCH.items():
        dram[n] = nc.dram_tensor(f"tmp_{n}", s, F32, kind="Internal").ap()
    dram["out"] = nc.dram_tensor("out", (N, D), F32, kind="ExternalOutput").ap()
    with ExitStack() as ctx:
        p = Program(nc, book, ctx, dram)
        (parts or Program.build)(p)
    return nc


def layout(inputs):
    a = {n: np.ascontiguousarray(inputs["L0_attn_" + n]) for n in DRAM_IN if "L0_attn_" + n in inputs}
    a["x"] = a["x"].reshape(N, D)
    a["router_t"] = np.ascontiguousarray(np.transpose(inputs["L0_ffn_router_w"]))
    for n in ("wg", "wu", "wd"):
        w = np.ascontiguousarray(inputs["L0_ffn_" + n])
        a[n] = w.reshape(w.shape[0] * w.shape[1], w.shape[2])
    const, _, level = constants()
    a["const"], a["level"] = const, level
    return {f"in_{n}": x for n, x in a.items()}


def kernel(**inputs):
    import concourse.bacc as bacc
    from concourse.bass_utils import run_bass_kernel_spmd

    book = {}
    build(bacc.Bacc("TRN2", target_bir_lowering=False, num_devices=1), book)
    nc = build(bacc.Bacc("TRN2", target_bir_lowering=False, num_devices=1), book)
    r = run_bass_kernel_spmd(nc, [layout(inputs)], core_ids=[0])
    return r.results[0]["out"].reshape(B, T, D)
```

```python
from contextlib import ExitStack

import concourse.bass as bass
import numpy as np
from concourse import mybir
from concourse.alu_op_type import AluOpType as ALU

ACT = mybir.ActivationFunctionType
AX = mybir.AxisListType
F32 = mybir.dt.float32
I32 = mybir.dt.int32
F32R = mybir.dt.float32r

P = 128
B, T, D = 4, 2048, 256
N = B * T
TILES = N // P
KD = D // P
E, TOPK, CAP = 8, 2, max(1, int(1.25 * N / 8))
F = 1024
FB = F // P
H, HD = 8, 32
C = 32
NC = P // C
HG = 4
LEVELS = 5
SLOTS = E * CAP
AHEAD = 4
SKIP = SLOTS
G_LEAST = -200.0
RES = 0.5


def constants():
    p = np.arange(P)
    same = (p[:, None] // C) == (p[None, :] // C)
    cols = {
        "ident": np.eye(P),
        "ones": np.ones((P, P)),
        "before": p[:, None] < p[None, :],
        "upto": same & (p[:, None] <= p[None, :]),
        "after": same & (p[:, None] > p[None, :]),
        "within": (p[:, None] % C) <= np.arange(C)[None, :],
        "causal": (same & (p[:, None] <= p[None, :])),
        "diag": same,
        "chunk": (p[:, None] // C) == np.arange(NC)[None, :],
        "minus_half": np.full((P, 16), -0.5),
        "expert_less_8": np.broadcast_to(np.arange(E)[None, :, None] - 8.0, (P, E, TILES)).reshape(P, -1),
        "first_slot": np.broadcast_to((np.arange(E) * CAP)[None, :, None] - float(SKIP), (P, E, TILES)).reshape(P, -1),
        "column": np.broadcast_to(np.arange(P)[None, :], (P, P)),
        "token": np.arange(TILES)[None, :] * P + p[:, None],
        "not_first_tile": np.broadcast_to((np.arange(TILES) != 0)[None, None, :], (P, E, TILES)).reshape(P, -1),
    }
    at, where, parts = 0, {}, []
    for name, a in cols.items():
        where[name] = (at, a.shape[1])
        parts.append(a.astype(np.float32))
        at += a.shape[1]
    levels = [((p[:, None] >> (s + 1)) == (p[None, :] >> (s + 1))) & ((p[:, None] >> s) % 2 == 0) & ((p[None, :] >> s) % 2 == 1)
              for s in range(LEVELS)]
    return np.concatenate(parts, 1), where, np.concatenate(levels, 1).astype(np.int32)


class Step:

    def __init__(self, meter, k, turn=0):
        self.meter, self.k, self.turn = meter, k, turn


class Meter:

    def __init__(self, sem, name, unit, each_turn):
        self.sem, self.name, self.unit, self.each_turn, self.k = sem, name, unit, each_turn, 0
        self.ahead = 0 if name.startswith("swdma") else 1


class Phase:

    def __init__(self, prog, name, turns=0):
        self.nc, self.book, self.name, self.turns = prog.nc, prog.book, name, turns
        self.semaphore = lambda n: prog.ctx.enter_context(prog.nc.semaphore(f"{name}_{n}"))
        self.loop = ExitStack()
        self.engines = {"pe": self.nc.tensor, "act": self.nc.scalar, "dve": self.nc.vector, "pool": self.nc.gpsimd, "sp": self.nc.sync}
        self.meters, self.waited, self.owners = {}, {}, {}

    def __enter__(self):
        for name, (unit, each_turn) in sorted(self.book.get((self.name, "meters"), {}).items()):
            m = self.meters[name] = Meter(self.semaphore(name), name, unit, each_turn)
            if self.turns and m.ahead:
                self.nc.sync.sem_inc(m.sem, unit * each_turn)
        self.passed = self.semaphore("passed")
        self.i = self.loop.enter_context(self.nc.Fori(0, self.turns)) if self.turns else 0
        return self

    def meter(self, name, unit):
        if name not in self.meters:
            self.meters[name] = Meter(self.semaphore(name), name, unit, 1)
        return self.meters[name]

    def wait(self, engine, *steps, plain=False):
        need = {}
        for s in steps:
            m = s.meter
            assert s.turn == 0 or m.ahead
            at = s.k + (m.each_turn if self.turns else 0) * (m.ahead + s.turn)
            if at > max(need.get(m.name, 0), self.waited.get((engine, m.name), 0)):
                need[m.name] = at
        for name, at in need.items():
            m = self.meters[name]
            self.waited[engine, name] = at
            self.engines[engine].wait_ge(m.sem, self.i * (m.unit * m.each_turn) + m.unit * at if self.turns else m.unit * at)
            if plain and self.turns:
                self.engines[engine].sem_inc(self.passed, 1)

    def run(self, engine, make, *steps, plain=False):
        self.wait(engine, *steps, plain=plain or engine == "pool")
        m = self.meter(engine, 1)
        m.k += 1
        make().then_inc(m.sem, 1)
        return Step(m, m.k)

    def dma(self, queue, buffer, make, *steps):
        self.wait(queue, *steps, plain=queue in ("pool", "sp"))
        m = self.meter(("swdma_" if queue == "pool" else "dma_") + buffer, 16)
        m.k += 1
        make().then_inc(m.sem, 16)
        return Step(m, m.k)

    def relay(self, engine, *steps):
        self.wait(engine, *steps, plain=engine in ("pool", "sp"))
        m = self.meter(engine, 1)
        m.k += 1
        self.engines[engine].sem_inc(m.sem, 1)
        return Step(m, m.k)

    def pe(self, make, *steps):
        return self.run("pe", make, *steps)

    def act(self, make, *steps):
        return self.run("act", make, *steps)

    def dve(self, make, *steps, plain=False):
        return self.run("dve", make, *steps, plain=plain)

    def pool(self, make, *steps):
        return self.run("pool", make, *steps)

    def release(self, buffer, *steps):
        self.owners[buffer] = steps

    def free(self, buffer):
        if buffer in self.owners or not self.turns:
            return self.owners.get(buffer, ())
        last = self.book.get((self.name, "owners"), {}).get(buffer, ())
        return tuple(Step(self.meters[name], k, -1) for name, k in last)

    def __exit__(self, *error):
        self.loop.close()
        if error[0] is not None:
            return
        self.book[self.name, "owners"] = {b: [(s.meter.name, s.k) for s in steps] for b, steps in self.owners.items()}
        self.book[self.name, "meters"] = {n: (m.unit, m.k) for n, m in self.meters.items()}
        for m in self.meters.values():
            if m.unit == 16:
                self.nc.sync.wait_ge(m.sem, 16 * m.k * (self.turns + m.ahead if self.turns else 1))
        self.nc.all_engine_barrier()


class Program:
    def __init__(self, nc, book, ctx, dram):
        self.nc, self.book, self.ctx, self.dram = nc, book, ctx, dram
        self.sync, self.tensor, self.vector, self.scalar, self.gpsimd = nc.sync, nc.tensor, nc.vector, nc.scalar, nc.gpsimd
        self.temps = 0
        sb = self.sb
        self.bank = ctx.enter_context(nc.psum_tensor("bank", [P, 8, 512], F32))
        _, self.where, _ = constants()
        width = sum(w for _, w in self.where.values())
        self.const = sb("const", [P, width])
        self.level = sb("level", [P, LEVELS, P], I32)
        self.router = sb("router", [P, KD, E])
        self.w_qk, self.w_vg, self.w_ba = sb("w_qk", [P, KD, 2 * D]), sb("w_vg", [P, KD, 2 * D]), sb("w_ba", [P, KD, 2 * H])
        self.w_o, self.w_fc, self.w_p = sb("w_o", [P, KD, D]), sb("w_fc", [P, KD, F]), sb("w_p", [P, FB, D])
        self.ln1, self.ln2 = sb("ln1", [P, KD]), sb("ln2", [P, KD])
        self.onorm = sb("onorm", [P, HD])
        self.decay, self.dt_bias = sb("decay", [P, H]), sb("dt_bias", [P, H])
        self.logits = sb("logits", [P, E, TILES])
        self.slot = sb("slot", [P, TOPK, TILES], I32)
        self.fetch = sb("fetch", [P, TOPK, TILES], I32)
        self.weight = sb("weight", [P, TOPK, TILES])
        self.source = sb("source", [P, SLOTS // P + AHEAD], I32)

    def sb(self, name, shape, dtype=F32):
        return self.ctx.enter_context(self.nc.sbuf_tensor(name, shape, dtype))

    def temp(self, stack, name, shape, dtype=F32):
        self.temps += 1
        return stack.enter_context(self.nc.sbuf_tensor(f"{name}_{self.temps}", shape, dtype))

    def c(self, name):
        at, width = self.where[name]
        return self.const[:, at:at + width]

    def rows(self, name, first, count):
        return self.dram[name][bass.ds(first, count), :].rearrange("(j p) d -> p j d", p=P)

    def load(self, ph, dst, src, **how):
        return ph.dma("sp", "const", lambda: self.nc.sync.dma_start(dst, src, **how))

    def start(self):
        dram = self.dram
        with Phase(self, "start") as ph:
            self.load(ph, self.const[:, :], dram["const"])
            self.load(ph, self.router[:, :, :], dram["router_t"].rearrange("(k p) f -> p k f", p=P))

    def load_block(self, ph):
        nc, dram, load = self.nc, self.dram, lambda *a, **how: self.load(ph, *a, **how)
        blocks = lambda name: dram[name].rearrange("(k p) f -> p k f", p=P)
        load(self.dt_bias[:, :], dram["dt_bias"].partition_broadcast(P))
        last = ph.dma("sp", "decay", lambda: nc.sync.dma_start(self.decay[:, :], dram["A_log"].partition_broadcast(P)))
        e = ph.act(lambda: nc.scalar.activation(self.decay[:, :], self.decay[:, :], ACT.Exp), last)
        ph.dve(lambda: nc.vector.tensor_scalar(self.decay[:, :], self.decay[:, :], -1.0, None, ALU.mult), e)
        load(self.level[:, :, :], dram["level"].rearrange("p (s i) -> p s i", s=LEVELS))
        for w, a, b in ((self.w_qk, "qw", "kw"), (self.w_vg, "vw", "gw"), (self.w_ba, "bw", "aw")):
            half = w.shape[2] // 2
            load(w[:, :, 0:half], blocks(a))
            load(w[:, :, half:], blocks(b))
        load(self.w_o[:, :, :], blocks("ow"))
        load(self.w_fc[:, :, :], blocks("fcw"))
        load(self.w_p[:, :, :], blocks("pw"))
        load(self.ln1[:, :], dram["ln1_w"].rearrange("(k p) -> p k", p=P), allow_slow_non_contiguous=True)
        load(self.ln2[:, :], dram["ln2_w"].rearrange("(k p) -> p k", p=P), allow_slow_non_contiguous=True)
        load(self.onorm[:, :], dram["onorm_w"].partition_broadcast(P))

    def route_first(self):
        nc = self.nc
        J, U = 4, 4
        with ExitStack() as tmp:
            sb = lambda n, s: self.temp(tmp, n, s, F32)
            x4 = [sb(f"x4_{u}", [P, J, D]) for u in range(U)]
            xn = [sb(f"xn_{u}", [P, J, D]) for u in range(U)]
            xt = [sb(f"xt_{u}", [P, J, KD, P]) for u in range(U)]
            st = [sb(f"st_{u}", [P, J, 6]) for u in range(U)]
            mv = [sb(f"mv_{u}", [P, J, 2]) for u in range(U)]
            rs = [sb(f"rs_{u}", [P, J]) for u in range(U)]
            with Phase(self, "route1", TILES // (J * U)) as ph:
                row = lambda u: ph.i * (J * U * P) + u * J * P
                scale, logits = [], []
                for u in range(U):
                    x = ph.dma("sp", f"x{u}", lambda: nc.sync.dma_start(x4[u][:, :, :], self.rows("x", row(u), J * P)), *ph.free(f"x4_{u}"))
                    for j in range(J):
                        s = ph.dve(lambda: nc.vector.bn_stats(st[u][:, j, :], x4[u][:, j, :]), x, *ph.free(f"st{u}"))
                    for j in range(J):
                        s = ph.dve(lambda: nc.vector.bn_aggr(mv[u][:, j, :], st[u][:, j, :]), s, *ph.free(f"mv{u}"), plain=True)
                    ph.release(f"st{u}", s)
                    scale.append(self.rsqrt(ph, rs[u][:, :], mv[u][:, :, 1], 1.0, 1e-5, s, *ph.free(f"mv{u}")))

                def keep_logits(u):
                    l = ph.dve(lambda: nc.vector.tensor_copy(self.logits[:, :, bass.ds(ph.i * (J * U) + u * J, J)],
                                                             self.bank[:, 6 + u % 2, 0:J * E].rearrange("p (j e) -> p e j", e=E)), logits[u])
                    ph.release(f"logit bank{u % 2}", l)

                for u in range(U):
                    pair = u % 3
                    for j in range(J):
                        n = ph.dve(lambda: nc.vector.tensor_scalar(xn[u][:, j, :], x4[u][:, j, :], mv[u][:, j, 0:1], rs[u][:, j:j + 1],
                                                                   ALU.subtract, ALU.mult), scale[u], *ph.free(f"xn{u}"))
                    ph.release(f"x4_{u}", n)
                    ph.release(f"mv{u}", n)
                    if u > 0:
                        keep_logits(u - 1)
                    kept = ph.dma("act", f"xn{u}", lambda: nc.scalar.dma_start(self.rows("xn", row(u), J * P), xn[u][:, :, :]), n)
                    for j in range(J):
                        for k in range(KD):
                            o = self.bank[:, 2 * pair + j // 2, (j % 2 * KD + k) * P:(j % 2 * KD + k + 1) * P]
                            t = ph.pe(lambda: nc.tensor.transpose(o, xn[u][:, j, k * P:(k + 1) * P], self.c("ident")), n, *ph.free(f"xt banks{pair}"))
                    ph.release(f"xn{u}", kept, t)
                    for j in range(0, J, 2):
                        e = ph.act(lambda: nc.scalar.activation(xt[u][:, j:j + 2, :, :].rearrange("p j k t -> p (j k t)"), self.bank[:, 2 * pair + j // 2, :], ACT.Copy),
                                   t, *ph.free(f"xt{u}"))
                    ph.release(f"xt banks{pair}", e)
                    for j in range(J):
                        for k in range(KD):
                            m = ph.pe(lambda: nc.tensor.matmul(self.bank[:, 6 + u % 2, j * E:(j + 1) * E], xt[u][:, j, k, :], self.router[:, k, :],
                                                               start=k == 0, stop=k == KD - 1), e, *ph.free(f"logit bank{u % 2}"))
                    ph.release(f"xt{u}", m)
                    logits.append(m)
                keep_logits(U - 1)

    def rsqrt(self, ph, out, in_, scale, eps, *steps):
        nc = self.nc
        a = ph.pool(lambda: nc.gpsimd.tensor_scalar(out, in_, scale, eps, ALU.mult, ALU.add), *steps)
        half = self.c("minus_half")[:, 0:out.free_size()]
        return ph.pool(lambda: nc.gpsimd.tensor_tensor(out, out, half, ALU.pow), a)

    def choose(self, name, alongside=lambda ph: None):
        nc, v, c = self.nc, self.nc.vector, self.c
        with ExitStack() as tmp:
            sb = lambda n, s, d=F32: self.temp(tmp, n, s, d)
            full = lambda n: sb(n, [P, E, TILES])
            p, hot1, hot2, w, a, b, s = (full(n) for n in ("p", "hot1", "hot2", "w", "a", "b", "s"))
            m, r, m1, m2 = (sb(n, [P, TILES]) for n in ("m", "r", "m1", "m2"))
            per = lambda n, d=F32: sb(n, [P, E], d)
            cand, least, more, count, quota = per("cand", I32), per("least", I32), per("more", I32), per("count"), per("quota")
            flat = lambda t: t[:, :, :].rearrange("p e t -> p (e t)")
            te = lambda t: t[:, :, :].rearrange("p e t -> p t e")
            over_e = lambda t: t[:, :].unsqueeze(1).to_broadcast([P, E, TILES])
            over_t = lambda t: t.unsqueeze(2).to_broadcast([P, E, TILES])
            bank = [self.bank[:, n, :] for n in range(4)]
            psum = lambda n: bank[n].rearrange("p (e t) -> p e t", e=E)
            less8 = c("expert_less_8").rearrange("p (e t) -> p e t", e=E)
            tt, ts, stt = v.tensor_tensor, v.tensor_scalar, v.scalar_tensor_tensor
            with Phase(self, name) as ph:
                alongside(ph)
                last = [()]

                def dve(make, *steps):
                    last[0] = (ph.dve(make, *last[0], *steps),)
                    return last[0][0]

                A = lambda t: t[:, :, :]
                dve(lambda: v.tensor_reduce(m[:, :], te(self.logits), AX.X, ALU.max))
                x = dve(lambda: tt(A(p), A(self.logits), over_e(m), ALU.subtract))
                x = ph.act(lambda: nc.scalar.activation(A(p), A(p), ACT.Exp), x)
                dve(lambda: v.tensor_reduce(m[:, :], te(p), AX.X, ALU.add), x)
                dve(lambda: v.reciprocal(r[:, :], m[:, :]))
                dve(lambda: tt(A(p), A(p), over_e(r), ALU.mult))
                for best, hot in ((m1, hot1), (m2, hot2)):
                    dve(lambda: v.tensor_reduce(best[:, :], te(p), AX.X, ALU.max))
                    dve(lambda: tt(A(a), A(p), over_e(best), ALU.is_equal))
                    dve(lambda: tt(A(a), A(a), less8, ALU.mult))
                    dve(lambda: v.tensor_reduce(m[:, :], te(a), AX.X, ALU.min))
                    dve(lambda: tt(A(hot), less8, over_e(m), ALU.is_equal))
                    if best is m1:
                        dve(lambda: stt(flat(p), flat(hot), -2.0, flat(p), ALU.mult, ALU.add))
                dve(lambda: stt(r[:, :], m1[:, :], 1e-6, m2[:, :], ALU.add, ALU.add))
                dve(lambda: v.reciprocal(r[:, :], r[:, :]))
                dve(lambda: tt(m1[:, :], m1[:, :], r[:, :], ALU.mult))
                dve(lambda: tt(m2[:, :], m2[:, :], r[:, :], ALU.mult))
                dve(lambda: tt(A(a), A(hot1), over_e(m1), ALU.mult))
                dve(lambda: tt(A(w), A(hot2), over_e(m2), ALU.mult))
                dve(lambda: tt(A(w), A(w), A(a), ALU.add))
                dve(lambda: tt(A(s), A(hot1), A(hot2), ALU.add))

                def total(src, out_bank, width, lhs="ones"):
                    x = last[0][0]
                    return ph.pe(lambda: nc.tensor.matmul(bank[out_bank][:, 0:width], c(lhs), src, start=True, stop=True), x)

                dve(lambda: v.memset(least[:, :], 0))
                for bit in range(29, -1, -1):
                    dve(lambda: v.tensor_scalar(cand[:, :], least[:, :], 1 << bit, None, ALU.bitwise_or))
                    dve(lambda: tt(A(a), A(w), over_t(cand[:, :].bitcast(F32)), ALU.is_ge))
                    dve(lambda: v.tensor_reduce(count[:, :], A(a), AX.X, ALU.add))
                    x = total(count[:, :], 0, E)
                    dve(lambda: ts(more[:, :], bank[0][:, 0:E], float(CAP), None, ALU.is_ge), x)
                    dve(lambda: v.copy_predicated(least[:, :], more[:, :], cand[:, :]))
                floor = over_t(least[:, :].bitcast(F32))
                dve(lambda: tt(A(a), A(w), floor, ALU.is_gt))
                dve(lambda: v.tensor_reduce(count[:, :], A(a), AX.X, ALU.add))
                x = total(count[:, :], 0, E)
                dve(lambda: ts(quota[:, :], bank[0][:, 0:E], -1.0, float(CAP), ALU.mult, ALU.add), x)
                dve(lambda: tt(A(b), A(w), floor, ALU.is_equal))
                dve(lambda: tt(A(b), A(b), A(s), ALU.mult))

                def before(mask, out, tmp_):
                    total(flat(mask), 1, E * TILES, "before")
                    x = total(flat(mask), 2, E * TILES)
                    dve(lambda: v.tensor_copy(flat(tmp_), bank[2]), x)
                    dve(lambda: v.tensor_tensor_scan(flat(out), c("not_first_tile"), flat(tmp_), 0.0, ALU.mult, ALU.add))
                    dve(lambda: tt(A(out), A(out), A(tmp_), ALU.subtract))
                    dve(lambda: tt(A(out), A(out), psum(1), ALU.add), x)

                before(b, p, w)
                dve(lambda: tt(A(p), A(p), over_t(quota[:, :]), ALU.is_lt))
                dve(lambda: tt(A(b), A(b), A(p), ALU.mult))
                dve(lambda: tt(A(a), A(a), A(b), ALU.add))
                before(a, p, w)
                dve(lambda: tt(flat(p), flat(p), c("first_slot"), ALU.add))
                dve(lambda: tt(A(p), A(p), A(a), ALU.mult))
                for k, (hot, weight) in enumerate(((hot1, m1), (hot2, m2))):
                    dve(lambda: tt(A(b), A(hot), A(p), ALU.mult))
                    dve(lambda: v.tensor_reduce(m[:, :], te(b), AX.X, ALU.add))
                    dve(lambda: ts(m[:, :], m[:, :], float(SKIP), None, ALU.add))
                    dve(lambda: v.tensor_copy(self.slot[:, k, :], m[:, :]))
                    dve(lambda: tt(A(b), A(hot), A(a), ALU.mult))
                    dve(lambda: v.tensor_reduce(r[:, :], te(b), AX.X, ALU.add))
                    dve(lambda: tt(self.weight[:, k, :], weight[:, :], r[:, :], ALU.mult))
                    dve(lambda: tt(m[:, :], m[:, :], r[:, :], ALU.mult))
                    dve(lambda: v.tensor_copy(self.fetch[:, k, :], m[:, :]))

    def invert(self, name):
        nc, v, c, J = self.nc, self.nc.vector, self.c, 8
        ROUNDS, QUEUE = TILES // J, 4
        with ExitStack() as tmp:
            sb = lambda n, s, d=F32: self.temp(tmp, n, s, d)
            whole = sb("whole", [P, TOPK, TILES], I32)
            lo, hi = sb("lo", [P, TOPK, TILES]), sb("hi", [P, TOPK, TILES])
            lo_j, hi_j, token_j = sb("lo_j", [P, TOPK, J]), sb("hi_j", [P, TOPK, J]), sb("token_j", [P, J])
            is_p = [sb(f"is_p{u}", [P, P]) for u in range(QUEUE)]
            at_a = [sb(f"at_a{u}", [P, SLOTS // P]) for u in range(QUEUE)]
            table = self.bank[:, 0, 0:SLOTS // P]
            with Phase(self, name + "_places") as ph:
                for out, op, by in ((lo, ALU.bitwise_and, P - 1), (hi, ALU.logical_shift_right, P.bit_length() - 1)):
                    x = ph.dve(lambda: v.tensor_scalar(whole[:, :, :], self.slot[:, :, :], by, None, op), *ph.free("whole"))
                    x = ph.dve(lambda: v.tensor_copy(out[:, :, :], whole[:, :, :]), x)
                    ph.release("whole", x)
                z = ph.dve(lambda: v.memset(is_p[0][:, :], 0.0))
                z = ph.dve(lambda: v.memset(at_a[0][:, :], 0.0), z)
                ph.pe(lambda: nc.tensor.matmul(table, is_p[0][:, :], at_a[0][:, :], start=True, stop=False, skip_group_check=True), z)
            with Phase(self, name, ROUNDS) as ph:
                at = ph.i * J
                y = ph.dve(lambda: v.tensor_copy(lo_j[:, :, :], lo[:, :, bass.ds(at, J)]), *ph.free("_j"))
                y = ph.dve(lambda: v.tensor_copy(hi_j[:, :, :], hi[:, :, bass.ds(at, J)]), *ph.free("_j"))
                y = ph.dve(lambda: v.tensor_copy(token_j[:, :], c("token")[:, bass.ds(at, J)]), *ph.free("_j"))
                for n in range(J * TOPK):
                    j, k, u = n // TOPK, n % TOPK, n % QUEUE
                    a = ph.dve(lambda: v.tensor_scalar(is_p[u][:, :], c("column"), lo_j[:, k, j:j + 1], None, ALU.is_equal), y, *ph.free(f"pair{u}"))
                    a = ph.dve(lambda: v.tensor_scalar(at_a[u][:, :], c("column")[:, 0:SLOTS // P], hi_j[:, k, j:j + 1], token_j[:, j:j + 1], ALU.is_equal, ALU.mult),
                               y, *ph.free(f"pair{u}"))
                    m = ph.pe(lambda: nc.tensor.matmul(table, is_p[u][:, :], at_a[u][:, :], start=False, stop=True, skip_group_check=True), a)
                    ph.release(f"pair{u}", m)
                ph.release("_j", a)
            with Phase(self, name + "_table") as ph:
                z = ph.dve(lambda: v.memset(self.source[:, :], 0))
                ph.dve(lambda: v.tensor_copy(self.source[:, 0:SLOTS // P], table), z)

    def experts(self, name, eo, beside=lambda ph: None):
        nc, U, W = self.nc, 2, 256
        CH, S = CAP // W, W // P
        LAST = U * CH
        v = nc.vector
        assert AHEAD == 2 * S and LAST % 2 == 0
        with ExitStack() as tmp:
            sb = lambda n, s: self.temp(tmp, n, s, F32)
            pair = lambda n, s: (sb(n, s), sb(n + "_low", s))
            wg = [pair(f"wg{u}", [P, KD, F]) for u in range(U)]
            wu = [pair(f"wu{u}", [P, KD, F]) for u in range(U)]
            wd = [pair(f"wd{u}", [P, FB, D]) for u in range(U)]
            stage = sb("stage", [P, KD * F])

            def load(ph, which, expert):
                rows = F if which == "wd" else D
                return ph.dma("sp", "stage", lambda: nc.sync.dma_start(stage[:, :].rearrange("p (k f) -> p k f", k=rows // P), self.rows(which, expert * rows, rows)),
                              *ph.free("stage"))

            def cut(ph, dst, which, u, *steps):
                leading, low = (t[:, :, :].rearrange("p a b -> p (a b)") for t in dst[u])
                x = ph.pool(lambda: nc.gpsimd.tensor_copy(leading.bitcast(F32R), stage[:, :]), *steps, *ph.free(f"{which}{u}"))
                x = ph.pool(lambda: nc.gpsimd.tensor_tensor(low.bitcast(F32R), stage[:, :], leading, ALU.subtract), x)
                ph.release("stage", x)
                return x

            def first_expert(ph):
                for which, dst in (("wg", wg), ("wu", wu), ("wd", wd)):
                    cut(ph, dst, which, 0, load(ph, which, 0))
                beside(ph)

            self.choose(name + "_choose", first_expert)
            self.invert(name + "_invert")
            d = [sb(f"d{u}", [P, S, D]) for u in range(2)]
            dT = [pair(f"dT{u}", [P, KD, W]) for u in range(2)]
            act = [pair(f"act{u}", [P, FB, W]) for u in range(2)]
            th = [sb(f"th{u}", [P, 512]) for u in range(2)]
            eo_sb = [sb(f"eo{u}", [P, S, D]) for u in range(2)]
            at = self.temp(tmp, "from", [P, LAST * S + AHEAD], I32)

            def split(ph, whole, leading, low, *steps):
                x = ph.act(lambda: nc.scalar.activation(leading.bitcast(F32R), whole, ACT.Copy), *steps)
                return ph.dve(lambda: v.tensor_tensor(low.bitcast(F32R), whole, leading, ALU.subtract), x)

            def product(ph, out, left, right, first, last, *steps):
                for n, (a, b) in enumerate(((0, 0), (0, 1), (1, 0))):
                    m = ph.pe(lambda: nc.tensor.matmul(out, left[a].bitcast(F32R), right[b].bitcast(F32R), start=first and n == 0, stop=last and n == 2), *steps)
                return m

            def prepare(ph, n, *steps):
                par = n % 2
                for s in range(S):
                    for k in range(KD):
                        t = ph.pe(lambda: nc.tensor.transpose(self.bank[:, 6 + par, k * W + s * P:k * W + (s + 1) * P], d[par][:, s, k * P:(k + 1) * P],
                                                              self.c("ident")), *steps, *ph.free(f"dT bank{par}"))
                ph.release(f"d{par}", t)
                r = split(ph, self.bank[:, 6 + par, :], *(x[:, :, :].rearrange("p k w -> p (k w)") for x in dT[par]), t, *ph.free(f"dT{par}"))
                ph.release(f"dT bank{par}", r)
                return r

            def gather(ph, n, *steps):
                for s in range(S):
                    g = ph.dma("pool", f"d{n % 2}", lambda: nc.gpsimd.indirect_dma_start(
                        out=d[n % 2][:, s, :], out_offset=None, in_=self.dram["xn"][:, :],
                        in_offset=bass.IndirectOffsetOnAxis(ap=at[:, n * S + s:n * S + s + 1], axis=0)), *steps, *ph.free(f"d{n % 2}"))
                return g

            with Phase(self, name + "_first") as ph:
                tokens = ph.pool(lambda: nc.gpsimd.tensor_copy(at[:, 0:AHEAD], self.source[:, 0:AHEAD]))
                prepare(ph, 0, gather(ph, 0, tokens)), gather(ph, 1, tokens)
            with Phase(self, name, E // U) as ph:
                def down(s, n, acts):
                    u, par = n // CH, n % 2
                    bank = self.bank[:, 4 + par, :]
                    for f in range(FB):
                        m = product(ph, bank[:, s * D:(s + 1) * D], [t[:, f, s * P:(s + 1) * P] for t in act[par]], [t[:, f, :] for t in wd[u]],
                                    f == 0, f == FB - 1, acts[f // 2], *ph.free(f"down bank{par}"), *wd_here[u])
                    if s < S - 1:
                        return
                    ph.release(f"act{par}", m)
                    if n % CH == CH - 1:
                        ph.release(f"wd{u}", m)
                    e = ph.act(lambda: nc.scalar.activation(eo_sb[par][:, :, :].rearrange("p s d -> p (s d)"), bank, ACT.Copy, scale=0.5),
                               m, *ph.free(f"eo{par}"))
                    ph.release(f"down bank{par}", e)
                    row = (ph.i * U + u) * CAP + n % CH * W
                    o = ph.dma("act", f"eo{par}", lambda: nc.scalar.dma_start(self.rows(eo, row, W), eo_sb[par][:, :, :]), e)
                    ph.release(f"eo{par}", o)

                parts = [(which, dst, [ph.free(f"{which}0 cut")]) for which, dst in (("wg", wg), ("wu", wu), ("wd", wd))]
                wg_here, wu_here, wd_here = (here for _, _, here in parts)
                coming = (ph.i * U + 1, (ph.i * U + U) % E)
                ready = ph.free("first prepared")
                rows_here = {1: ph.free("rows seen")}
                tokens = ph.pool(lambda: nc.gpsimd.tensor_copy(at[:, :], self.source[:, bass.ds(ph.i * (U * CAP // P), LAST * S + AHEAD)]), *ph.free("from"))
                rows_here[2] = (gather(ph, 2, tokens),)
                pending = None
                for n in range(LAST):
                    u, par = n // CH, n % 2
                    chunk_ready = ready
                    acts = []
                    for r in range(FB // 2):
                        if pending and r in (1, 2):
                            down(r - 1, *pending)
                        if r == 2:
                            ready = (prepare(ph, n + 1, *rows_here[n + 1]),)
                            if n + 3 < LAST + 2:
                                rows_here[n + 3] = (gather(ph, n + 3, tokens),)
                        q = r % 2
                        gb, ub = self.bank[:, q, :], self.bank[:, 2 + q, :]
                        done = {}
                        for which, bank, wt, here in (("g", gb, wg, wg_here), ("u", ub, wu, wu_here)):
                            for f in range(2):
                                for k in range(KD):
                                    fb = 2 * r + f
                                    m = product(ph, bank[:, f * W:(f + 1) * W], [t[:, k, fb * P:(fb + 1) * P] for t in wt[u]], [t[:, k, :] for t in dT[par]],
                                                k == 0, k == KD - 1, *chunk_ready, *here[u], *ph.free(f"{which} bank{q}"))
                            done[which] = m
                        h = ph.act(lambda: nc.scalar.activation(th[q][:, :], gb, ACT.Tanh, scale=0.5), done["g"], *ph.free(f"th{q}"))
                        a = ph.dve(lambda: v.scalar_tensor_tensor(th[q][:, :], th[q][:, :], 1.0, gb, ALU.add, ALU.mult), h)
                        b = ph.dve(lambda: v.tensor_tensor(th[q][:, :], th[q][:, :], ub, ALU.mult), a, done["u"])
                        ph.release(f"g bank{q}", a)
                        ph.release(f"u bank{q}", b)
                        b = split(ph, th[q][:, :], *(t[:, 2 * r:2 * r + 2, :].rearrange("p f w -> p (f w)") for t in act[par]), b, *ph.free(f"act{par}"))
                        ph.release(f"th{q}", b)
                        acts.append(b)
                    ph.release(f"dT{par}", m)
                    if n % CH == CH - 1:
                        ph.release(f"wg{u}", m)
                        ph.release(f"wu{u}", m)
                    step = n % CH
                    if 1 <= step <= 3:
                        which, dst, here = parts[step - 1]
                        cut_ = cut(ph, dst, which, 1 - u, come)
                        if u == 0:
                            here.append((cut_,))
                        else:
                            ph.release(f"{which}0 cut", cut_)
                    if step < 3:
                        come = load(ph, parts[step][0], coming[u])
                    pending = (n, acts)
                down(0, *pending), down(1, *pending)
                ph.release("first prepared", *ready)
                seen = ph.relay("sp", *rows_here[LAST + 1])
                ph.release("rows seen", seen)
                ph.release("from", seen)

    def combine(self, ph, x, e, w, steps, out):
        v = self.nc.vector
        a = ph.dve(lambda: v.tensor_scalar(e[0], e[0], w[0], None, ALU.mult), *steps)
        a = ph.dve(lambda: v.scalar_tensor_tensor(e[0], e[1], w[1], e[0], ALU.mult, ALU.add), a)
        return ph.dve(lambda: v.scalar_tensor_tensor(out, e[0], RES, x, ALU.mult, ALU.add), a)

    def finish(self, eo):
        nc, G, U = self.nc, 2, 4
        with ExitStack() as tmp:
            sb = lambda n, s, d=F32: self.temp(tmp, n, s, d)
            x = [sb(f"fx{u}", [P, D]) for u in range(G * U)]
            e = [[sb(f"fe{u}{k}", [P, D]) for k in range(TOPK)] for u in range(G * U)]
            y = [sb(f"fy{u}", [P, D]) for u in range(G * U)]
            at = [sb(f"fat{g}", [P, TOPK, U], I32) for g in range(G)]
            wt = [sb(f"fwt{g}", [P, TOPK, U]) for g in range(G)]
            with Phase(self, "finish", TILES // (G * U)) as ph:
                for n in range(G * U):
                    g, u = n // U, n % U
                    tile = ph.i * (G * U) + n
                    if u == 0:
                        a = ph.pool(lambda: nc.gpsimd.tensor_copy(at[g][:, :, :], self.fetch[:, :, bass.ds(tile, U)]), *ph.free(f"group{g}"))
                        w = ph.pool(lambda: nc.gpsimd.tensor_copy(wt[g][:, :, :], self.weight[:, :, bass.ds(tile, U)]), *ph.free(f"group{g}"))
                    xs = ph.dma("sp", f"x{n}", lambda: nc.sync.dma_start(x[n][:, :], self.dram["x2"][bass.ds(tile * P, P), :]), *ph.free(f"used{n}"))
                    got = [ph.dma("pool", f"e{n}", lambda: nc.gpsimd.indirect_dma_start(
                        out=e[n][k][:, :], out_offset=None, in_=self.dram[eo][:, :],
                        in_offset=bass.IndirectOffsetOnAxis(ap=at[g][:, k, u:u + 1], axis=0)), a, *ph.free(f"used{n}")) for k in range(TOPK)]
                    o = self.combine(ph, x[n][:, :], (e[n][0][:, :], e[n][1][:, :]), (wt[g][:, 0, u:u + 1], wt[g][:, 1, u:u + 1]),
                                     (xs, *got, w, *ph.free(f"y{n}")), y[n][:, :])
                    ph.release(f"used{n}", o)
                    ph.release(f"group{g}", o)
                    s = ph.dma("act", f"y{n}", lambda: nc.scalar.dma_start(self.dram["out"][bass.ds(tile * P, P), :], y[n][:, :]), o)
                    ph.release(f"y{n}", s)

    def attention(self, eo):
        nc, v, g_, sc = self.nc, self.nc.vector, self.nc.gpsimd, self.nc.scalar
        c, bank = self.c, self.bank
        with ExitStack() as tmp:
            sb = lambda n, s, d=F32: self.temp(tmp, n, s, d)
            two = lambda n, s, d=F32: [sb(f"{n}{q}", s, d) for q in range(2)] * 2
            four = lambda n, s, d=F32: [sb(f"{n}{q}", s, d) for q in range(B)]
            one = lambda n, s, d=F32: [sb(n, s, d)] * B
            x_in, e0, e1 = (two(n, [P, D]) for n in ("x_in", "e0", "e1"))
            at, wt = two("at", [P, TOPK], I32), two("wt", [P, TOPK])
            x1, xa, gg = four("x1", [P, D]), four("xa", [P, D]), four("gg", [P, H, HD])
            nw, vb, kc = (four(n, [P, H, HD]) for n in ("nw", "vb", "kc"))
            gamma, qgT = four("gamma", [P, 3 * H]), four("qgT", [P, 2, P])
            st, mv, small, junk, th = ({z: sb(n + z, s) for z in "fbr"} for n, s in
                                       (("st", [P, 6]), ("mv", [P, 2]), ("small", [P, 4]), ("junk", [P, D]), ("th", [P, 512])))
            h, hT, sq = one("h", [P, D]), two("hT", [P, KD, P]), one("sq", [P, 512])
            qk, vg = one("qk", [P, 2 * H, HD]), one("vg", [P, 2 * H, HD])
            tiny, ba = one("tiny", [P, 10, H]), one("ba", [P, 2 * H])
            rq, ro = one("rq", [P, 2 * H]), one("ro", [P, H])
            gv, gx, dc = one("gv", [P, H, HD]), one("gx", [P, H, HD]), one("dc", [P, H, HD])
            kb, qg = one("kb", [P, H, HD]), one("qg", [P, H, HD])
            dm, bq, kT = two("dm", [P, H, P]), two("bq", [P, HG, 2, 2 * P]), two("kT", [P, 2, P])
            NT, X, R = one("NT", [P, H, P]), one("X", [P, H, P]), one("R", [P, H, P])
            Y, Bt, WT = two("Y", [P, H, P]), two("Bt", [P, H, P]), one("WT", [P, 2, P])
            us, sm, os_, og, ogT = one("us", [P, H * HD]), one("sm", [P, 2, P]), one("os", [P, D]), one("og", [P, D]), one("ogT", [P, KD, P])
            x1a, h2, h2T, aT = one("x1a", [P, D]), one("h2", [P, D]), one("h2T", [P, KD, P]), one("aT", [P, FB, P])
            x2, xn2, xn2T = two("x2", [P, D]), two("xn2", [P, D]), one("xn2T", [P, KD, P])
            S = [sb(f"S{b}", [P, 2, P]) for b in range(B)]
            flat = lambda t: t[:, :, :].rearrange("p a b -> p (a b)")
            over_hd = lambda t: t.unsqueeze(2).to_broadcast([P, t.shape[1], HD])
            per4 = lambda m: m.unsqueeze(1).to_broadcast([P, HG, P])

            def stages(ph):

                row = lambda n: (ph.i + n // B) * P + n % B * T
                tile = lambda n: (ph.i + n // B) + n % B * (T // P)

                def norm(x, out, z, steps, free):
                    s = ph.dve(lambda: v.bn_stats(st[z][:, :], x), *steps, *ph.free(f"st{z}"))
                    s = ph.dve(lambda: v.bn_aggr(mv[z][:, :], st[z][:, :]), s, *ph.free(f"mv{z}"), plain=True)
                    ph.release(f"st{z}", s)
                    r = self.rsqrt(ph, small[z][:, 0:1], mv[z][:, 1:2], 1.0, 1e-5, s, *ph.free(f"small0{z}"))
                    n = ph.dve(lambda: v.tensor_scalar(out, x, mv[z][:, 0:1], small[z][:, 0:1], ALU.subtract, ALU.mult), r, *free)
                    ph.release(f"mv{z}", n)
                    ph.release(f"small0{z}", n)
                    return n

                def rms(x, out, z, steps, free):
                    a = ph.act(lambda: sc.activation(junk[z][:, :], x, ACT.Square, accum_out=small[z][:, 1:2]), *steps, *ph.free(f"junk{z}"), *ph.free(f"small1{z}"))
                    ph.release(f"junk{z}", a)
                    r = self.rsqrt(ph, small[z][:, 1:2], small[z][:, 1:2], 1.0 / D, 1e-6, a)
                    n = ph.dve(lambda: v.tensor_scalar(out, x, small[z][:, 1:2], None, ALU.mult), r, *free)
                    ph.release(f"small1{z}", n)
                    return n

                def transpose(x, out, no, name, steps, scale=None):
                    for k in range(KD):
                        t = ph.pe(lambda: nc.tensor.transpose(bank[:, no, k * P:(k + 1) * P], x[:, k * P:(k + 1) * P], c("ident")), *steps, *ph.free(f"bank{no}"))
                    if scale is None:
                        e = ph.act(lambda: sc.activation(flat(out), bank[:, no, 0:KD * P], ACT.Copy), t, *ph.free(name))
                    else:
                        for k in range(KD):
                            e = ph.act(lambda: sc.activation(out[:, k, :], bank[:, no, k * P:(k + 1) * P], ACT.Copy, scale=scale[:, k:k + 1]), t, *ph.free(name))
                    ph.release(f"bank{no}", e)
                    return t, e

                def fetch(n):
                    b, q = n % B, n % 2
                    yield 4.4
                    ia = ph.pool(lambda: g_.tensor_copy(at[q][:, :], self.fetch[:, :, bass.ds(tile(n), 1)].rearrange("p k t -> p (k t)")), *ph.free(f"fetched{q}"))
                    iw = ph.pool(lambda: g_.tensor_copy(wt[q][:, :], self.weight[:, :, bass.ds(tile(n), 1)].rearrange("p k t -> p (k t)")), *ph.free(f"fetched{q}"))
                    xs = ph.dma("sp", f"x{q}", lambda: nc.sync.dma_start(x_in[q][:, :], self.dram["x"][bass.ds(row(n), P), :]), *ph.free(f"fetched{q}"))
                    for k, e in enumerate((e0[q], e1[q])):
                        got = ph.dma("pool", f"e{q}", lambda: g_.indirect_dma_start(
                            out=e[:, :], out_offset=None, in_=self.dram[eo][:, :],
                            in_offset=bass.IndirectOffsetOnAxis(ap=at[q][:, k:k + 1], axis=0)), ia, *ph.free(f"fetched{q}"))
                    yield 4.27
                    ph.release(f"fetch{b}", iw, ph.relay("sp", xs, got))

                def head(n):
                    b, q = n % B, n % 2
                    yield 5.0
                    x = self.combine(ph, x_in[q][:, :], (e0[q][:, :], e1[q][:, :]), (wt[q][:, 0:1], wt[q][:, 1:2]),
                                     (*ph.free(f"fetch{b}"), *ph.free(f"x1{b}")), x1[b][:, :])
                    ph.release(f"fetched{q}", x)
                    yield 1.01
                    a = norm(x1[b][:, :], xa[b][:, :], "f", (x,), ph.free(f"xa{b}"))
                    yield 3.34
                    a = rms(xa[b][:, :], h[b][:, :], "f", (a,), ph.free("h"))
                    yield 3.02
                    t, e = transpose(h[b], hT[b], 4, f"hT{q}", (a,), self.ln1)
                    ph.release("h", t)
                    ph.release(f"head{b}", e)
                    yield 0.89

                def front(n):
                    b, q = n % B, n % 2
                    e = ph.free(f"head{b}")
                    yield 12.5
                    for k in range(KD):
                        m = ph.pe(lambda: nc.tensor.matmul(bank[:, 2, 0:2 * H], hT[b][:, k, :], self.w_ba[:, k, :], start=k == 0, stop=k == KD - 1),
                                  *e, *ph.free("bank2"))
                    copied = ph.dve(lambda: v.tensor_copy(ba[b][:, :], bank[:, 2, 0:2 * H]), m, *ph.free("tiny"))
                    ph.release("bank2", copied)
                    yield 1.9
                    silu = []
                    for w, no, out, name in ((self.w_qk, 3, qk[b], "qk"), (self.w_vg, 2, vg[b], "vg")):
                        for k in range(KD):
                            m = ph.pe(lambda: nc.tensor.matmul(bank[:, no, :], hT[b][:, k, :], w[:, k, :], start=k == 0, stop=k == KD - 1),
                                      *e, *ph.free(f"bank{no}"))
                        yield 0.24
                        a = ph.act(lambda: sc.activation(th["f"][:, :], bank[:, no, :], ACT.Tanh, scale=0.5), m, *ph.free("thf"))
                        a = ph.dve(lambda: v.scalar_tensor_tensor(flat(out), th["f"][:, :], 1.0, bank[:, no, :], ALU.add, ALU.mult), a, *ph.free(name))
                        ph.release("thf", a)
                        ph.release(f"bank{no}", a)
                        silu.append(a)
                        yield 1.4
                    ph.release(f"hT{q}", m)
                    y_, z_, s_, w_, p_, g, beta, half_beta, ng = (tiny[b][:, k, :] for k in range(9))
                    d = ph.dve
                    tb = ph.act(lambda: sc.activation(beta, ba[b][:, 0:H], ACT.Tanh, scale=0.5), copied)
                    x = d(lambda: v.tensor_tensor(y_, ba[b][:, H:], self.dt_bias[:, :], ALU.add), copied)
                    x = d(lambda: v.scalar_tensor_tensor(z_, y_, -1.0, y_, ALU.mult, ALU.min), x)
                    z = ph.act(lambda: sc.activation(z_, z_, ACT.Exp), x)
                    yield 1.84
                    x = d(lambda: v.tensor_scalar(s_, z_, 2.0, None, ALU.add), z)
                    x = d(lambda: v.reciprocal(s_, s_), x)
                    x = d(lambda: v.tensor_tensor(s_, s_, z_, ALU.mult), x)
                    x = d(lambda: v.tensor_tensor(w_, s_, s_, ALU.mult), x)
                    x = d(lambda: v.tensor_scalar(p_, w_, 1.0 / 17, None, ALU.mult), x)
                    yield 3.47
                    for k in range(15, 1, -2):
                        x = d(lambda: v.scalar_tensor_tensor(p_, p_, 1.0 / k, w_, ALU.add, ALU.mult), x)
                        if k == 9:
                            yield 0.15
                    yield 1.06
                    x = d(lambda: v.scalar_tensor_tensor(p_, p_, 1.0, s_, ALU.add, ALU.mult), x)
                    x = d(lambda: v.tensor_scalar(y_, y_, 0.0, None, ALU.max), x)
                    x = d(lambda: v.scalar_tensor_tensor(p_, p_, 2.0, y_, ALU.mult, ALU.add), x)
                    x = d(lambda: v.tensor_tensor(g, p_, self.decay[:, :], ALU.mult), x)
                    gs = d(lambda: v.tensor_scalar(g, g, G_LEAST, None, ALU.max), x)
                    x = d(lambda: v.tensor_scalar(beta, beta, 0.5, 0.5, ALU.mult, ALU.add), tb)
                    bs = d(lambda: v.tensor_scalar(half_beta, beta, 0.5, None, ALU.mult), x)
                    pv = ph.pool(lambda: g_.tensor_tensor(gv[b][:, :, :], over_hd(g), c("within").unsqueeze(1).to_broadcast([P, H, HD]), ALU.mult), gs, *ph.free("gv"))
                    px = ph.pool(lambda: g_.tensor_copy(gx[b][:, :, :], over_hd(g)), gs, *ph.free("gx"))
                    yield 2.56
                    a = ph.act(lambda: sc.activation(sq[b][:, :], flat(qk[b]), ACT.Square), silu[0], *ph.free("sq"))
                    a = ph.dve(lambda: v.tensor_reduce(rq[b][:, :], sq[b][:, :].rearrange("p (h k) -> p h k", k=HD), AX.X, ALU.add), a, *ph.free("rq"))
                    ph.release("sq", a)
                    a = self.rsqrt(ph, rq[b][:, :], rq[b][:, :], 1.0, 4e-6, a)
                    yield 5.14
                    qkn = ph.dve(lambda: v.tensor_tensor(qk[b][:, :, :], qk[b][:, :, :], over_hd(rq[b][:, :]), ALU.mult), a)
                    ph.release("rq", qkn)
                    sums = bank[:, 3, 16:16 + 3 * H]
                    ph.pe(lambda: nc.tensor.matmul(sums[:, 0:H], c("upto"), g, start=True, stop=True), gs, *ph.free("bank3"))
                    ph.pe(lambda: nc.tensor.matmul(sums[:, H:2 * H], c("after"), g, start=True, stop=True), gs)
                    for k in range(2):
                        m = ph.pe(lambda: nc.tensor.matmul(sums[:, 2 * H + NC * k:2 * H + NC * (k + 1)], gx[b][:, HG * k:HG * (k + 1), :].rearrange("p a b -> p (a b)"),
                                                           c("chunk"), start=True, stop=True), px)
                    ms = ph.pe(lambda: nc.tensor.matmul(bank[:, 3, 128:128 + H * HD], c("after"), flat(gv[b]), start=True, stop=True), pv)
                    ph.release("gv", ms)
                    ph.release("gx", ms)
                    ga = ph.act(lambda: sc.activation(gamma[b][:, :], sums, ACT.Exp), ms, *ph.free(f"gamma{b}"))
                    gd = ph.act(lambda: sc.activation(flat(dc[b]), bank[:, 3, 128:128 + H * HD], ACT.Exp), ms, *ph.free("dc"))
                    ph.release("bank3", gd)
                    yield 2.15
                    dms = ph.pool(lambda: g_.tensor_tensor(dm[b][:, :, :].rearrange("p h (c i) -> p h c i", c=NC),
                                                           dc[b][:, :, :].unsqueeze(2).to_broadcast([P, H, NC, HD]),
                                                           c("causal").rearrange("p (c i) -> p c i", c=NC).unsqueeze(1).to_broadcast([P, H, NC, HD]), ALU.mult),
                                  gd, *ph.free(f"dm{q}"))
                    ph.release("dc", dms)
                    qn, kn, vv, gate = qk[b][:, 0:H, :], qk[b][:, H:, :], vg[b][:, 0:H, :], vg[b][:, H:, :]
                    down, up = gamma[b][:, 0:H], gamma[b][:, H:2 * H]
                    on = {"pool": (ph.pool, g_), "dve": (ph.dve, v)}
                    times = lambda engine, out, x, y, *s: on[engine][0](lambda: on[engine][1].tensor_tensor(out[:, :, :], x, over_hd(y), ALU.mult), *s)
                    skb = times("dve", kb[b], kn, beta, qkn, bs, *ph.free("kb"))
                    sqg = times("dve", qg[b], qn, down, qkn, ga, *ph.free("qg"))
                    yield 15
                    x = ph.dve(lambda: v.tensor_scalar(ng, down, -1.0, None, ALU.mult), ga)
                    snw = times("dve", nw[b], kb[b][:, :, :], ng, skb, x, *ph.free(f"nw{b}"))
                    yield 0.05
                    skc = times("pool", kc[b], kn, up, qkn, ga, *ph.free(f"kc{b}"))
                    svb = times("pool", vb[b], vv, half_beta, silu[1], bs, *ph.free(f"vb{b}"))
                    ph.release("tiny", snw, ms, svb)
                    sgg = ph.pool(lambda: g_.tensor_tensor(gg[b][:, :, :], gate, self.onorm[:, :].unsqueeze(1).to_broadcast([P, H, HD]), ALU.mult), silu[1], *ph.free(f"gg{b}"))
                    ph.release("vg", sgg, svb)
                    yield 10.4
                    f2 = lambda t: t.rearrange("p h k -> p (h k)")
                    for k in range(2):
                        for m_, src in ((0, f2(kb[b][:, :, :])), (1, f2(qn))):
                            t0 = ph.pe(lambda: nc.tensor.transpose(bank[:, 2, (2 * k + m_) * P:(2 * k + m_ + 1) * P], src[:, k * P:(k + 1) * P], c("ident")),
                                       skb, qkn, *ph.free("bank2"))
                    yield 1.77
                    for r in range(HG):
                        mine = slice(HD * r, HD * (r + 1))
                        x0 = ph.act(lambda: sc.activation(bq[b][mine, r, :, :].rearrange("p k t -> p (k t)"), bank[mine, 2, :], ACT.Copy), t0, *ph.free(f"bq{q}"))
                    ph.release("bank2", x0)
                    for k in range(2):
                        for m_, src in ((0, f2(kn)), (1, f2(qg[b][:, :, :]))):
                            t1 = ph.pe(lambda: nc.tensor.transpose(bank[:, 3, (2 * m_ + k) * P:(2 * m_ + k + 1) * P], src[:, k * P:(k + 1) * P], c("ident")),
                                       sqg, *ph.free("bank3"))
                    ph.release("kb", t0, snw)
                    ph.release("qg", t1)
                    ph.release("qk", t1, skc)
                    yield 0.3
                    y1 = ph.dve(lambda: v.tensor_copy(flat(kT[b]), bank[:, 3, 0:2 * P]), t1, *ph.free(f"kT{q}"))
                    y2 = ph.dve(lambda: v.tensor_copy(flat(qgT[b]), bank[:, 3, 2 * P:4 * P]), t1, *ph.free(f"qgT{b}"))
                    ph.release("bank3", y2)
                    ph.release(f"front{b}", x0, y2, dms, snw, svb, skc, sgg, ga)
                    yield 12.65

                def solve(n):
                    b, q = n % B, n % 2
                    yield 0.08
                    ready_in = ph.free(f"front{b}")
                    ones = [ph.pool(lambda: g_.tensor_copy(Y[b][:, HG * k:HG * (k + 1), :], per4(c("ident"))), *ph.free(f"Y{q}")) for k in range(2)]
                    yield 0.5
                    nt = {}
                    for k in range(2):
                        for r in range(HG):
                            gm = ph.pe(lambda: nc.tensor.matmul(bank[:, 2 * k + r // 2, r % 2 * 2 * P:(r % 2 + 1) * 2 * P], kT[b][:, k, :],
                                                                bq[b][:, r, k, :], start=True, stop=True),
                                       *ready_in, *ph.free(f"bank{2 * k + r // 2}"))
                        heads = slice(HG * k, HG * (k + 1))
                        gram = bank[:, 2 * k:2 * k + 2, :].rearrange("p n (r a t) -> p a (n r) t", r=2, a=2)
                        nt[k] = ph.dve(lambda: v.scalar_tensor_tensor(NT[b][:, heads, :], gram[:, 0, :, :], -1.0, dm[b][:, heads, :],
                                                                      ALU.mult, ALU.mult), gm, *ready_in, *ph.free("NT"))
                        bt = ph.dve(lambda: v.tensor_tensor(Bt[b][:, heads, :], gram[:, 1, :, :], dm[b][:, heads, :], ALU.mult),
                                    gm, *ready_in, *ph.free(f"Bt{q}"))
                        ph.release(f"bank{2 * k}", bt)
                        ph.release(f"bank{2 * k + 1}", bt)
                        yield 1.79
                    ph.release(f"bq{q}", gm)
                    ph.release(f"kT{q}", gm)
                    ph.release(f"dm{q}", bt)
                    ready = {}
                    for k in range(2):
                        heads = slice(HG * k, HG * (k + 1))
                        ready[k] = ph.dve(lambda: v.copy_predicated(Y[b][:, heads, :], per4(self.level[:, 0, :]), NT[b][:, heads, :]), ones[k], nt[k], plain=True)
                        yield 1.23
                    yield 0.7
                    f3 = lambda t: t.rearrange("p h k -> p (h k)")
                    got = {}
                    for s in range(1, LEVELS):
                        for k in range(2):
                            for r in range(HG):
                                if r == 2:
                                    yield 0.05
                                t = ph.pe(lambda: nc.tensor.transpose(bank[:, k, r * P:(r + 1) * P], Y[b][:, HG * k + r, :], c("ident")), ready[k], *ph.free(f"bank{k}"))
                            got[k] = ph.act(lambda: sc.activation(f3(X[b][:, HG * k:HG * (k + 1), :]), bank[:, k, :], ACT.Copy), t, *ph.free(f"X{k}"))
                            yield 0.83
                        for k in range(2):
                            for r in range(HG):
                                if r == 2:
                                    yield 0.07
                                m = ph.pe(lambda: nc.tensor.matmul(bank[:, k, r * P:(r + 1) * P], NT[b][:, HG * k + r, :], X[b][:, HG * k + r, :], start=True, stop=True), got[k])
                            ph.release(f"X{k}", m)
                            got[k] = ph.act(lambda: sc.activation(f3(R[b][:, HG * k:HG * (k + 1), :]), bank[:, k, :], ACT.Copy), m, *ph.free(f"R{k}"))
                            yield 1.49
                        for k in range(2):
                            for r in range(HG):
                                if r == 2:
                                    yield 0.32
                                m = ph.pe(lambda: nc.tensor.matmul(bank[:, k, r * P:(r + 1) * P], R[b][:, HG * k + r, :], Y[b][:, HG * k + r, :], start=True, stop=True), got[k])
                            ph.release(f"R{k}", m)
                            ready[k] = ph.dve(lambda: v.copy_predicated(Y[b][:, HG * k:HG * (k + 1), :], per4(self.level[:, s, :]),
                                                                        bank[:, k, :].rearrange("p (r t) -> p r t", r=HG)), m, plain=True)
                            ph.release(f"bank{k}", ready[k])
                            yield 0.6
                    ph.release("NT", m)
                    ph.release(f"solve{b}", ready[1], bt)

                def back(n):
                    b, q = n % B, n % 2
                    yield 0.08
                    got = (*ph.free(f"front{b}"), *ph.free(f"solve{b}"))
                    for k in range(2):
                        for r in range(HG):
                            m = ph.pe(lambda: nc.tensor.matmul(bank[HD * r:HD * (r + 1), 4, k * P:(k + 1) * P], nw[b][:, HG * k + r, :], Y[b][:, HG * k + r, :], start=True, stop=True),
                                      *got, *ph.free("bank4"))
                    ph.release(f"nw{b}", m)
                    w = ph.act(lambda: sc.activation(flat(WT[b]), bank[:, 4, 0:2 * P], ACT.Copy), m, *ph.free("WT"))
                    ph.release("bank4", w)
                    yield 3.15
                    for hd in range(H):
                        m = ph.pe(lambda: nc.tensor.matmul(bank[:, 5, hd * HD:(hd + 1) * HD], Y[b][:, hd, :], vb[b][:, hd, :], start=hd == 0, stop=False, skip_group_check=True),
                                  *got, *ph.free("bank5"))
                    ph.release(f"vb{b}", m)
                    ph.release(f"Y{q}", m)
                    yield 1.41
                    prev = ph.free(f"S{b}")
                    for ch in range(NC):
                        part = slice(C * ch, C * (ch + 1))
                        for k in range(2):
                            mu = ph.pe(lambda: nc.tensor.matmul(bank[part, 5, k * P:(k + 1) * P], WT[b][:, k, part], S[b][:, k, :], start=False, stop=True, skip_group_check=True),
                                       w, *prev)
                        u = ph.act(lambda: sc.activation(us[b][part, :], bank[part, 5, 0:D], ACT.Copy), mu, *ph.free("us"))
                        yield 0.22
                        for k in range(2):
                            mo = ph.pe(lambda: nc.tensor.matmul(bank[part, 7, k * P:(k + 1) * P], qgT[b][:, k, part], S[b][:, k, :], start=k == 0, stop=False, skip_group_check=True),
                                       *prev, *ph.free("bank7"))
                        yield 1.1
                        for k in range(2):
                            ms = ph.pe(lambda: nc.tensor.matmul(bank[:, 6, k * P:(k + 1) * P], kc[b][part, HG * k:HG * (k + 1), :].rearrange("p a b -> p (a b)"),
                                                                us[b][part, k * P:(k + 1) * P], start=True, stop=True), u, *ph.free("bank6"))
                        x = ph.dve(lambda: v.tensor_tensor(sm[b][:, :, :], bank[:, 6, 0:2 * P].rearrange("p (n t) -> p n t", n=2),
                                                           c("diag").unsqueeze(1).to_broadcast([P, 2, P]), ALU.mult), ms, *ph.free("sm"))
                        ph.release("bank6", x)
                        for k in range(2):
                            x = ph.dve(lambda: v.scalar_tensor_tensor(S[b][:, k, :], S[b][:, k, :], gamma[b][:, 2 * H + NC * k + ch:2 * H + NC * k + ch + 1],
                                                                      sm[b][:, k, :], ALU.mult, ALU.add), x, mo)
                        ph.release("sm", x)
                        prev = (x,)
                        yield 1.69
                    ph.release(f"S{b}", x)
                    ph.release(f"kc{b}", ms)
                    ph.release("WT", mu)
                    ph.release(f"qgT{b}", mo)
                    ph.release(f"gamma{b}", x)
                    ph.release("bank5", u)
                    yield 2.32
                    for hd in range(H):
                        m = ph.pe(lambda: nc.tensor.matmul(bank[:, 7, hd * HD:(hd + 1) * HD], Bt[b][:, hd, :], us[b][:, hd * HD:(hd + 1) * HD], start=False, stop=True,
                                                           skip_group_check=True), u)
                    ph.release("us", m)
                    ph.release(f"Bt{q}", m)
                    o = bank[:, 7, 0:D]
                    a = ph.act(lambda: sc.activation(os_[b][:, :], o, ACT.Square), m, *ph.free("os"))
                    a = ph.dve(lambda: v.tensor_reduce(ro[b][:, :], os_[b][:, :].rearrange("p (h k) -> p h k", k=HD), AX.X, ALU.add), a, *ph.free("ro"))
                    ph.release("os", a)
                    a = self.rsqrt(ph, ro[b][:, :], ro[b][:, :], 1.0 / HD, 1e-6, a)
                    yield 5.16
                    o3 = og[b][:, :].rearrange("p (h k) -> p h k", k=HD)
                    a = ph.dve(lambda: v.tensor_tensor(o3, o.rearrange("p (h k) -> p h k", k=HD), over_hd(ro[b][:, :]), ALU.mult), a, *ph.free("og"))
                    ph.release("bank7", a)
                    ph.release("ro", a)
                    a = ph.dve(lambda: v.tensor_tensor(o3, o3, gg[b][:, :, :], ALU.mult), a)
                    ph.release(f"gg{b}", a)
                    t, e = transpose(og[b], ogT[b], 4, "ogT", (a,))
                    ph.release("og", t)
                    yield 3.54
                    for k in range(KD):
                        m = ph.pe(lambda: nc.tensor.matmul(bank[:, 5, 0:D], ogT[b][:, k, :], self.w_o[:, k, :], start=k == 0, stop=k == KD - 1), e, *ph.free("bank5"))
                    ph.release("ogT", m)
                    yield 1.45
                    a = ph.dve(lambda: v.scalar_tensor_tensor(x1a[b][:, :], bank[:, 5, 0:D], RES * 0.5, xa[b][:, :], ALU.mult, ALU.add), m, *ph.free("x1a"))
                    ph.release("bank5", a)
                    ph.release(f"xa{b}", a)
                    yield 0.96
                    a = rms(x1a[b][:, :], h2[b][:, :], "b", (a,), ph.free("h2"))
                    yield 3.05
                    t, e = transpose(h2[b], h2T[b], 4, "h2T", (a,), self.ln2)
                    ph.release("h2", t)
                    yield 9.5
                    acts = []
                    for k2 in range(2):
                        for f in range(4):
                            for k in range(KD):
                                fb = 4 * k2 + f
                                m = ph.pe(lambda: nc.tensor.matmul(bank[:, 6 + k2, f * P:(f + 1) * P], self.w_fc[:, k, fb * P:(fb + 1) * P], h2T[b][:, k, :],
                                                                   start=k == 0, stop=k == KD - 1), e, *ph.free(f"bank{6 + k2}"))
                        yield 15
                        a = ph.act(lambda: sc.activation(th["b"][:, :], bank[:, 6 + k2, :], ACT.Tanh, scale=0.5), m, *ph.free("thb"))
                        a = ph.dve(lambda: v.scalar_tensor_tensor(aT[b][:, 4 * k2:4 * k2 + 4, :].rearrange("p f t -> p (f t)"), th["b"][:, :], 1.0, bank[:, 6 + k2, :],
                                                                  ALU.add, ALU.mult), a, *ph.free("aT"))
                        ph.release("thb", a)
                        ph.release(f"bank{6 + k2}", a)
                        acts.append(a)
                        yield 9.69
                    ph.release("h2T", m)
                    for f in range(FB):
                        m = ph.pe(lambda: nc.tensor.matmul(bank[:, 5, 0:D], aT[b][:, f, :], self.w_p[:, f, :], start=f == 0, stop=f == FB - 1), acts[f // 4], *ph.free("bank5"))
                        if f % 2 == 1:
                            yield 2.42
                    ph.release("aT", m)
                    a = ph.dve(lambda: v.scalar_tensor_tensor(x2[b][:, :], bank[:, 5, 0:D], RES * 0.5, x1a[b][:, :], ALU.mult, ALU.add), m,
                               *ph.free(f"x2 read{q}"), *ph.free(f"x2 kept{q}"))
                    ph.release("bank5", a)
                    ph.release("x1a", a)
                    a = ph.dve(lambda: v.tensor_tensor(x2[b][:, :], x2[b][:, :], x1[b][:, :], ALU.add), a)
                    ph.release(f"x1{b}", a)
                    kept = ph.dma("sp", f"x2{q}", lambda: nc.sync.dma_start(self.dram["x2"][bass.ds(row(n), P), :], x2[b][:, :]), a)
                    ph.release(f"to route{q}", a)
                    ph.release(f"x2 kept{q}", kept)
                    yield 3.79

                def route(n):
                    b, q = n % B, n % 2
                    yield 0.05
                    a = norm(x2[b][:, :], xn2[b][:, :], "r", ph.free(f"to route{q}"), ph.free(f"xn2{q}"))
                    ph.release(f"x2 read{q}", a)
                    kept = ph.dma("sp", f"xn2{q}", lambda: nc.sync.dma_start(self.dram["xn"][bass.ds(row(n), P), :], xn2[b][:, :]), a)
                    yield 2.8
                    t, e = transpose(xn2[b], xn2T[b], 6, "xn2T", (a,))
                    ph.release(f"xn2{q}", kept, t)
                    yield 15
                    for k in range(KD):
                        m = ph.pe(lambda: nc.tensor.matmul(bank[:, 6, KD * P:KD * P + E], xn2T[b][:, k, :], self.router[:, k, :], start=k == 0, stop=k == KD - 1), e, *ph.free("bank6"))
                    ph.release("xn2T", m)
                    a = ph.dve(lambda: v.tensor_copy(self.logits[:, :, bass.ds(tile(n), 1)].rearrange("p e t -> p (e t)"), bank[:, 6, KD * P:KD * P + E]), m)
                    ph.release("bank6", a)
                    yield 1.29

                return fetch, head, front, solve, back, route

            def together(*streams):
                live = [[0.0, k, s] for k, s in enumerate(streams)]
                while live:
                    one_ = min(live, key=lambda t: t[:2])
                    cost = next(one_[2], None)
                    if cost is None:
                        live.remove(one_)
                    else:
                        one_[0] += cost

            def ahead(*streams):
                for s in streams:
                    yield from s

            with Phase(self, "attention_first") as ph:
                fetch, head, front, solve, back, route = stages(ph)
                for t in (*(flat(s) for s in S), x2[0][:, :], x2[1][:, :], *(bq[q][:, :, :, :].rearrange("p r k t -> p (r k t)") for q in range(2))):
                    z = ph.dve(lambda: v.memset(t, 0.0))
                for q in range(2):
                    ph.release(f"bq{q}", z)
                together(fetch(0))
                together(fetch(1), head(0))
                together(fetch(2), head(1), front(0))
                together(head(2), front(1), solve(0))
            with Phase(self, "attention", T // P) as ph:
                fetch, head, front, solve, back, route = stages(ph)
                for b in range(B):
                    together(route(b - 1), back(b), solve(b + 1), front(b + 2), ahead(fetch(b + 3), head(b + 3)))
            with Phase(self, "attention_last") as ph:
                together(stages(ph)[-1](TILES - 1))

    def build(self):
        self.start()
        self.route_first()
        self.experts("experts1", "eo", self.load_block)
        self.attention("eo")
        self.experts("experts2", "eo2")
        self.finish("eo2")


DRAM_IN = {
    "x": (N, D), "ln1_w": (D,), "qw": (D, D), "kw": (D, D), "vw": (D, D), "bw": (D, H), "aw": (D, H), "A_log": (H,), "dt_bias": (H,),
    "gw": (D, D), "onorm_w": (HD,), "ow": (D, D), "ln2_w": (D,), "fcw": (D, F), "pw": (F, D),
    "router_t": (D, E), "wg": (E * D, F), "wu": (E * D, F), "wd": (E * F, D),
}
SCRATCH = {"xn": (N, D), "eo": (SLOTS, D), "eo2": (SLOTS, D), "x2": (N, D)}


def build(nc, book, parts=None):
    const, _, level = constants()
    dram = {n: nc.dram_tensor(f"in_{n}", s, F32, kind="ExternalInput").ap() for n, s in DRAM_IN.items()}
    dram["const"] = nc.dram_tensor("in_const", const.shape, F32, kind="ExternalInput").ap()
    dram["level"] = nc.dram_tensor("in_level", level.shape, I32, kind="ExternalInput").ap()
    for n, s in SCRATCH.items():
        dram[n] = nc.dram_tensor(f"tmp_{n}", s, F32, kind="Internal").ap()
    dram["out"] = nc.dram_tensor("out", (N, D), F32, kind="ExternalOutput").ap()
    with ExitStack() as ctx:
        p = Program(nc, book, ctx, dram)
        (parts or Program.build)(p)
    return nc


def layout(inputs):
    a = {n: np.ascontiguousarray(inputs["L0_attn_" + n]) for n in DRAM_IN if "L0_attn_" + n in inputs}
    a["x"] = a["x"].reshape(N, D)
    a["router_t"] = np.ascontiguousarray(np.transpose(inputs["L0_ffn_router_w"]))
    for n in ("wg", "wu", "wd"):
        w = np.ascontiguousarray(inputs["L0_ffn_" + n])
        a[n] = w.reshape(w.shape[0] * w.shape[1], w.shape[2])
    const, _, level = constants()
    a["const"], a["level"] = const, level
    return {f"in_{n}": x for n, x in a.items()}


def kernel(**inputs):
    import concourse.bacc as bacc
    from concourse.bass_utils import run_bass_kernel_spmd

    book = {}
    build(bacc.Bacc("TRN2", target_bir_lowering=False, num_devices=1), book)
    nc = build(bacc.Bacc("TRN2", target_bir_lowering=False, num_devices=1), book)
    r = run_bass_kernel_spmd(nc, [layout(inputs)], core_ids=[0])
    return r.results[0]["out"].reshape(B, T, D)
```
